# Optimizing a Trainium2 kernel written in Bass

```python
import numpy as np
import jax
import jax.numpy as jnp

def _softmax(x, axis=-1):
    return jax.nn.softmax(x, axis=axis)

def _gelu(x):
    return jax.nn.gelu(x, approximate=True)

def _silu(x):
    return jax.nn.silu(x)

def _sigmoid(x):
    return jax.nn.sigmoid(x)

def _layernorm(x, axis=-1, eps=1e-05):
    m = jnp.mean(x, axis=axis, keepdims=True)
    v = jnp.var(x, axis=axis, keepdims=True)
    return (x - m) / jnp.sqrt(v + eps)

def _scatter_add(tgt, idx, src, axis=0):
    return tgt.at[idx].add(src)

def _segment_sum(src, seg, n):
    return jax.ops.segment_sum(src, seg, n)
kernel_name = 'mk_gnn_resnorm_d2_gnn_r8_152b1c'

def setup_inputs(seed: int=0):
    np.random.seed(seed)
    _w = jnp.asarray

    def _rec_inputs():
        import jax
        import jax.numpy as jnp
        _gk = jax.random.key(seed)
        x = -0.000202 + 1 * jax.random.normal(jax.random.fold_in(_gk, 1), (6250, 128), jnp.float32)
        src = jax.random.randint(jax.random.fold_in(_gk, 2), (100000,), 0, 6250, jnp.int32)
        dst = jax.random.randint(jax.random.fold_in(_gk, 3), (100000,), 0, 6250, jnp.int32)
        _o = jnp.argsort(dst, stable=True)
        src = src[_o]
        dst = dst[_o]
        edge_attr_64 = 2.43349e-05 + 1.00019 * jax.random.normal(jax.random.fold_in(_gk, 11), (100000, 64), jnp.float32)
        edge_attr_64_n2 = 2.43349e-05 + 1.00019 * jax.random.normal(jax.random.fold_in(_gk, 12), (100000, 64), jnp.float32)
        edge_attr_64_n3 = 2.43349e-05 + 1.00019 * jax.random.normal(jax.random.fold_in(_gk, 13), (100000, 64), jnp.float32)
        return (x, src, dst, edge_attr_64, edge_attr_64_n2, edge_attr_64_n3)
    x, src, dst, edge_attr_64, edge_attr_64_n2, edge_attr_64_n3 = _rec_inputs()

    def _L0_gnn_setup():
        import jax, jax.numpy as jnp
        import numpy as np
        BN_EPS = 1e-05

        def _batchnorm(h, gamma, beta):
            mean = jnp.mean(h, axis=0)
            var = jnp.var(h, axis=0)
            return (h - mean) * jax.lax.rsqrt(var + BN_EPS) * gamma + beta
        N, E, D_IN, D_OUT = (6250, 100000, 128, 128)
        key = jax.random.key(seed)
        ks = jax.random.split(key, 6)
        x = jax.random.normal(ks[0], (N, D_IN), dtype=jnp.float32)
        edge_index = jax.random.randint(ks[1], (2, E), 0, N, dtype=jnp.int32)
        lim1 = 1.0 / np.sqrt(2 * D_IN)
        lim2 = 1.0 / np.sqrt(D_OUT)
        W1 = jax.random.uniform(ks[2], (D_OUT, 2 * D_IN), jnp.float32, -lim1, lim1)
        b1 = jax.random.uniform(ks[3], (D_OUT,), jnp.float32, -lim1, lim1)
        W2 = jax.random.uniform(ks[4], (D_OUT, D_OUT), jnp.float32, -lim2, lim2)
        b2 = jax.random.uniform(ks[5], (D_OUT,), jnp.float32, -lim2, lim2)
        g1 = jnp.ones((D_OUT,), jnp.float32)
        be1 = jnp.zeros((D_OUT,), jnp.float32)
        g2 = jnp.ones((D_OUT,), jnp.float32)
        be2 = jnp.zeros((D_OUT,), jnp.float32)
        return {'x': x, 'edge_index': edge_index, 'W1': W1, 'b1': b1, 'g1': g1, 'be1': be1, 'W2': W2, 'b2': b2, 'g2': g2, 'be2': be2}
    _L0_gnn_all = _L0_gnn_setup()
    _L0_gnn_in = {k: v for k, v in _L0_gnn_all.items() if k in ('W1', 'b1', 'g1', 'be1', 'W2', 'b2', 'g2', 'be2')}
    del _L0_gnn_all

    def _L1_gnn_setup():
        import jax, jax.numpy as jnp
        import numpy as np
        N_NODES = 6250
        N_EDGES = 31250
        N_HEAD = 2
        OUT_DIM = 128
        D_K = OUT_DIM // N_HEAD
        SCALE = D_K ** (-0.5)
        key = jax.random.key(seed)
        ks = jax.random.split(key, 12)

        def lin(k, fan_in, fan_out):
            return jax.random.normal(k, (fan_in, fan_out), jnp.float32) / np.sqrt(fan_in)
        return {'node_feature': jax.random.normal(ks[0], (N_NODES, 128), jnp.float32), 'edge_feature': jax.random.normal(ks[1], (N_EDGES, 64), jnp.float32), 'src_time_features': jax.random.normal(ks[2], (N_EDGES, 64), jnp.float32), 'edge_time': jax.random.normal(ks[3], (N_EDGES, 64), jnp.float32), 'Wq': lin(ks[4], 192, OUT_DIM), 'bq': jnp.zeros((OUT_DIM,), jnp.float32), 'Wk': lin(ks[5], 256, OUT_DIM), 'bk': jnp.zeros((OUT_DIM,), jnp.float32), 'Wv': lin(ks[6], 256, OUT_DIM), 'bv': jnp.zeros((OUT_DIM,), jnp.float32), 'W1': lin(ks[7], 256, 128), 'b1': jnp.zeros((128,), jnp.float32), 'W2': lin(ks[8], 128, OUT_DIM), 'b2': jnp.zeros((OUT_DIM,), jnp.float32), 'edge_index': jax.random.randint(ks[9], (N_EDGES, 2), 0, N_NODES, jnp.int64)}
    _L1_gnn_all = _L1_gnn_setup()
    _L1_gnn_in = {k: v for k, v in _L1_gnn_all.items() if k in ('Wq', 'bq', 'Wk', 'bk', 'Wv', 'bv', 'W1', 'b1', 'W2', 'b2')}
    del _L1_gnn_all
    return {'x': x, 'src': src, 'dst': dst, 'edge_attr_64': edge_attr_64, 'edge_attr_64_n2': edge_attr_64_n2, 'edge_attr_64_n3': edge_attr_64_n3, 'L0_gnn_W1': _L0_gnn_in['W1'], 'L0_gnn_b1': _L0_gnn_in['b1'], 'L0_gnn_g1': _L0_gnn_in['g1'], 'L0_gnn_be1': _L0_gnn_in['be1'], 'L0_gnn_W2': _L0_gnn_in['W2'], 'L0_gnn_b2': _L0_gnn_in['b2'], 'L0_gnn_g2': _L0_gnn_in['g2'], 'L0_gnn_be2': _L0_gnn_in['be2'], 'L1_gnn_Wq': _L1_gnn_in['Wq'], 'L1_gnn_bq': _L1_gnn_in['bq'], 'L1_gnn_Wk': _L1_gnn_in['Wk'], 'L1_gnn_bk': _L1_gnn_in['bk'], 'L1_gnn_Wv': _L1_gnn_in['Wv'], 'L1_gnn_bv': _L1_gnn_in['bv'], 'L1_gnn_W1': _L1_gnn_in['W1'], 'L1_gnn_b1': _L1_gnn_in['b1'], 'L1_gnn_W2': _L1_gnn_in['W2'], 'L1_gnn_b2': _L1_gnn_in['b2']}

def reference(x, src, dst, edge_attr_64, edge_attr_64_n2, edge_attr_64_n3, L0_gnn_W1, L0_gnn_b1, L0_gnn_g1, L0_gnn_be1, L0_gnn_W2, L0_gnn_b2, L0_gnn_g2, L0_gnn_be2, L1_gnn_Wq, L1_gnn_bq, L1_gnn_Wk, L1_gnn_bk, L1_gnn_Wv, L1_gnn_bv, L1_gnn_W1, L1_gnn_b1, L1_gnn_W2, L1_gnn_b2):
    import jax
    import jax.numpy as jnp

    def _L0_gnn_ref(x, edge_index, W1, b1, g1, be1, W2, b2, g2, be2):
        import jax, jax.numpy as jnp
        import numpy as np
        BN_EPS = 1e-05

        def _batchnorm(h, gamma, beta):
            mean = jnp.mean(h, axis=0)
            var = jnp.var(h, axis=0)
            return (h - mean) * jax.lax.rsqrt(var + BN_EPS) * gamma + beta
        src, dst = (edge_index[0], edge_index[1])
        edge_features = jnp.concatenate([x[src], x[dst]], axis=1)
        h = edge_features @ W1.T + b1
        h = jax.nn.relu(_batchnorm(h, g1, be1))
        h = h @ W2.T + b2
        edge_updates = jax.nn.relu(_batchnorm(h, g2, be2))
        x_out = jax.ops.segment_sum(edge_updates, dst, num_segments=x.shape[0])
        return x_out

    def _L1_gnn_ref(node_feature, edge_feature, src_time_features, edge_time, Wq, bq, Wk, bk, Wv, bv, W1, b1, W2, b2, edge_index):
        import jax, jax.numpy as jnp
        import numpy as np
        N_NODES = 6250
        N_EDGES = 31250
        N_HEAD = 2
        OUT_DIM = 128
        D_K = OUT_DIM // N_HEAD
        SCALE = D_K ** (-0.5)
        N = node_feature.shape[0]
        ei = jnp.concatenate([edge_index, edge_index[:, ::-1]], axis=0)
        ef = jnp.concatenate([edge_feature, edge_feature], axis=0)
        stf = jnp.concatenate([src_time_features, src_time_features], axis=0)
        et = jnp.concatenate([edge_time, edge_time], axis=0)
        time_unit = stf[0:1]
        node_id = jnp.arange(N, dtype=ei.dtype)
        ei = jnp.concatenate([ei, jnp.stack([node_id, node_id], axis=1)], axis=0)
        ef = jnp.concatenate([ef, jnp.zeros((N, ef.shape[1]), ef.dtype)], axis=0)
        stf = jnp.concatenate([stf, jnp.tile(time_unit, (N, 1))], axis=0)
        et = jnp.concatenate([et, jnp.tile(time_unit, (N, 1))], axis=0)
        node_i = ei[:, 0]
        node_j = ei[:, 1]
        src_vec = jnp.concatenate([node_feature[node_i], stf], axis=1)
        tgt_vec = jnp.concatenate([node_feature[node_j], ef, et], axis=1)
        q = jax.nn.relu(src_vec @ Wq + bq).reshape(-1, N_HEAD, D_K)
        k = jax.nn.relu(tgt_vec @ Wk + bk).reshape(-1, N_HEAD, D_K)
        v = (tgt_vec @ Wv + bv).reshape(-1, N_HEAD, D_K)
        att = jnp.sum(q * k, axis=-1) * SCALE
        m = jax.ops.segment_max(att, node_i, num_segments=N)
        e = jnp.exp(att - m[node_i])
        denom = jax.ops.segment_sum(e, node_i, num_segments=N)
        scores = e / denom[node_i]
        msg = (scores[:, :, None] * v).reshape(-1, OUT_DIM)
        out_emb = jax.ops.segment_sum(msg, node_i, num_segments=N)
        h = jax.nn.relu(jnp.concatenate([out_emb, node_feature], axis=1) @ W1 + b1)
        return h @ W2 + b2
    edge_index = jnp.stack([src, dst])
    edge_index_t = jnp.stack([src, dst], axis=1)
    x = _layernorm(x + _L0_gnn_ref(x, edge_index, L0_gnn_W1, L0_gnn_b1, L0_gnn_g1, L0_gnn_be1, L0_gnn_W2, L0_gnn_b2, L0_gnn_g2, L0_gnn_be2), axis=-1)
    x = _layernorm(x + _L1_gnn_ref(x, edge_attr_64, edge_attr_64_n2, edge_attr_64_n3, L1_gnn_Wq, L1_gnn_bq, L1_gnn_Wk, L1_gnn_bk, L1_gnn_Wv, L1_gnn_bv, L1_gnn_W1, L1_gnn_b1, L1_gnn_W2, L1_gnn_b2, edge_index_t), axis=-1)
    return x

_drawn_inputs = setup_inputs


def setup_inputs(seed=0):
    import zlib

    import numpy as np

    out = dict(_drawn_inputs(seed))
    spreads = {'L0_gnn_g1': (1.0, 0.2),
     'L0_gnn_be1': (0.0, 0.1),
     'L0_gnn_g2': (1.0, 0.2),
     'L0_gnn_be2': (0.0, 0.1),
     'L1_gnn_bq': (0.0, 0.8),
     'L1_gnn_bk': (0.0, 0.8),
     'L1_gnn_bv': (0.0, 0.1),
     'L1_gnn_b1': (0.0, 0.1),
     'L1_gnn_b2': (0.0, 0.1)}
    factors = {'L0_gnn_b1': 8.0, 'L0_gnn_b2': 8.0}
    for name, (base, spread) in spreads.items():
        noise = np.random.default_rng([zlib.crc32(name.encode()), seed]).standard_normal(out[name].shape)
        drawn = base * np.exp(spread * noise) if base else spread * noise
        out[name] = jnp.asarray(drawn.astype(out[name].dtype))
    for name, factor in factors.items():
        out[name] = (out[name] * factor).astype(out[name].dtype)
    return out
```

```python
import math
from contextlib import ExitStack

import concourse.bass as bass
from concourse import mybir

P = 128
N, E, D, DE = 6250, 100000, 128, 64
HEADS = 2
DK = D // HEADS
SCALE = DK ** -0.5
EPS = 1e-5
CG = 4
GE = CG * P
GROUPS = 2 * -(-E // (2 * GE))
EP = GROUPS * GE
LAST = E - (GROUPS - 1) * GE
NB = 2 * -(-(N + 1) // (2 * P))
NP_ = NB * P
SLOTS = 16
PAD = N
TB_W = D + 1
TN_W = 3 * D + 2
MSG_W = D + HEADS
NEG = -1.0e30
BANK = 512

f32, bf16, i32 = mybir.dt.float32, mybir.dt.bfloat16, mybir.dt.int32
ALU = mybir.AluOpType
ACT = mybir.ActivationFunctionType
X = mybir.AxisListType.X
ds = bass.ds


class Names:
    pass


def turns(eng, count, body):
    body(0)
    if count > 1:
        with eng.Fori(1, count) as i:
            body(i)


def first(i):
    return isinstance(i, int) and i == 0


def step(eng, ins, sem, count):
    ins.then_inc(sem, 1)
    eng.wait_ge(sem, count)


def hold(eng, sem, value, passed):
    eng.wait_ge(sem, value)
    eng.sem_inc(passed, 1)


def scope(nc, tag):
    ctx = ExitStack()

    def sb(name, shape, dt=f32):
        return ctx.enter_context(nc.sbuf_tensor(f"{tag}_{name}", shape, dt))

    def pb(name, shape):
        size = math.prod(shape[1:])
        whole = ctx.enter_context(nc.psum_tensor(f"{tag}_{name}", [shape[0], -(-size // BANK) * BANK], f32))
        if len(shape) == 2:
            return whole[:, 0:size]
        return whole[:, 0:size].rearrange("p (a b) -> p a b", b=shape[2])

    sems = []

    def sem(name):
        sems.append(nc.alloc_semaphore(f"{tag}_{name}"))
        return sems[-1]

    ctx.callback(nc.all_engine_barrier)
    ctx.callback(lambda: nc.clear_and_free_semaphores(sems))
    return ctx, sb, pb, sem


def setup(nc, d, m):
    ctx, sb, pb, sem = scope(nc, "setup")
    with ctx:
        keys, lows, highs = (sb(x, [P, 2, EP // P], i32) for x in ("keys", "lows", "highs"))
        rows, row_lows = (sb(x, [P, 2, EP // P], i32) for x in ("rows", "row_lows"))
        rowf = sb("rowf", [P, 2, 2, EP // P])
        w_in, k_in, zeroed, split, rowf_ok, rowf_out = (
            sem(x) for x in ("w_in", "k_in", "zeroed", "split", "rowf_ok", "rowf_out"))
        with nc.Block() as block:
            @block.sync
            def _(sp):
                sp.dma_start(keys[:, :, :], d.keys).then_inc(k_in, 16)
                sp.dma_start(rows[:, :, :], d.key_rows).then_inc(k_in, 16)
                sp.dma_start(m.cols[:, :], d.cols).then_inc(w_in, 16)
                sp.dma_start(m.w2t[:, :], d.w2t).then_inc(w_in, 16)
                sp.wait_ge(w_in, 32)

            @block.gpsimd
            def _(g):
                g.iota(m.iota_row[:, :], [[1, P]], base=0, channel_multiplier=0,
                       allow_small_or_imprecise_dtypes=True)
                g.iota(m.iota_p[:, :], [[0, 1]], base=0, channel_multiplier=1,
                       allow_small_or_imprecise_dtypes=True)
                g.memset(m.ones[:, :], 1.0)
                for t in (m.ident, m.before, m.after):
                    g.memset(t[:, :], 0.0).then_inc(zeroed, 1)
                g.memset(m.real[:, :], 1.0).then_inc(zeroed, 1)
                g.wait_ge(zeroed, 4)
                g.affine_select(out=m.ident[:, :], in_=m.ident[:, :], compare_op=ALU.not_equal, fill=1.0,
                                base=0, pattern=[[-1, P]], channel_multiplier=1)
                g.affine_select(out=m.before[:, :], in_=m.before[:, :], compare_op=ALU.is_ge, fill=1.0,
                                base=0, pattern=[[1, P]], channel_multiplier=-1)
                g.affine_select(out=m.after[:, :], in_=m.after[:, :], compare_op=ALU.is_ge, fill=1.0,
                                base=0, pattern=[[-1, P]], channel_multiplier=1)
                g.affine_select(out=m.real[:, :], in_=m.real[:, :], compare_op=ALU.is_ge, fill=0.0,
                                base=N - 1, pattern=[[-P, NB]], channel_multiplier=-1)

            @block.vector
            def _(v):
                v.wait_ge(k_in, 32)
                nc.vector.tensor_scalar(lows[:, :, :], keys[:, :, :], P - 1, None, ALU.bitwise_and).then_inc(split, 1)
                nc.vector.tensor_scalar(highs[:, :, :], keys[:, :, :], P.bit_length() - 1, None,
                                        ALU.arith_shift_right).then_inc(split, 1)
                nc.vector.tensor_scalar(row_lows[:, :, :], rows[:, :, :], P - 1, None,
                                        ALU.bitwise_and).then_inc(split, 1)
                nc.vector.tensor_copy(m.key[:, :, :], keys[:, :, :])
                nc.vector.tensor_copy(rowf[:, :, 0, :], rows[:, :, :]).then_inc(rowf_ok, 1)
                v.wait_ge(split, 3)
                nc.vector.tensor_copy(m.lo[:, :, :], lows[:, :, :])
                nc.vector.tensor_copy(m.hi[:, :, :], highs[:, :, :])
                nc.vector.tensor_copy(rowf[:, :, 1, :], row_lows[:, :, :]).then_inc(rowf_ok, 1)

            @block.scalar
            def _(act):
                act.wait_ge(rowf_ok, 2)
                act.dma_start(d.rowf.rearrange("w t (p j) -> p w t j", p=P), rowf[:, :, :, :]).then_inc(rowf_out, 16)
                act.wait_ge(rowf_out, 16)


def l0_tables(nc, d, m):
    ctx, sb, pb, sem = scope(nc, "tab0")
    R = 5
    with ctx:
        w = sb("w", [P, 2 * D])
        b1 = sb("b1", [P, D])
        xt = [sb(f"xt{k}", [P, P]) for k in range(R)]
        tab = [sb(f"tab{k}", [P, D + TB_W]) for k in range(R)]
        ps = [pb(f"ps{k}", [P, 2 * D]) for k in range(R)]
        w_in, mm, tab_ok = (sem(x) for x in ("w_in", "mm", "tab_ok"))
        xt_in = [sem(f"xt_in{k}") for k in range(R)]
        tab_out = [sem(f"tab_out{k}") for k in range(R)]
        with nc.Block() as block:
            @block.sync
            def _(sp):
                sp.dma_start(w[:, :], d.w1).then_inc(w_in, 16)
                sp.dma_start(b1[:, :], d.b1.partition_broadcast(P)).then_inc(w_in, 16)

                def body(i):
                    for k in range(R):
                        if not first(i):
                            sp.wait_ge(mm, i * R - R + k + 1)
                        sp.dma_start(xt[k][:, :], d.xT[:, ds(i * (R * P) + k * P, P)]).then_inc(xt_in[k], 16)
                turns(sp, NB // R, body)

            @block.tensor
            def _(pe):
                pe.wait_ge(w_in, 32)

                def body(i):
                    for k in range(R):
                        pe.wait_ge(xt_in[k], i * 16 + 16)
                        if not first(i):
                            pe.wait_ge(tab_ok, i * (3 * R) - 3 * R + 3 * k + 3)
                        nc.tensor.matmul(ps[k][:, :], xt[k][:, :], w[:, :], start=True, stop=True).then_inc(mm, 1)
                turns(pe, NB // R, body)

            @block.vector
            def _(v):
                v.wait_ge(w_in, 32)

                def body(i):
                    for k in range(R):
                        v.wait_ge(mm, i * R + k + 1)
                        if not first(i):
                            v.wait_ge(tab_out[k], i * 32)
                        nc.vector.tensor_tensor(tab[k][:, 0:D], ps[k][:, 0:D], b1[:, :], ALU.add).then_inc(tab_ok, 1)
                        nc.vector.tensor_scalar(tab[k][:, D:2 * D], ps[k][:, D:2 * D], 0.0, None,
                                                ALU.add).then_inc(tab_ok, 1)
                        nc.vector.tensor_scalar(tab[k][:, 2 * D:2 * D + 1], m.place[:, ds(i * R + k, 1), 1], 0.0, None,
                                                ALU.add).then_inc(tab_ok, 1)
                turns(v, NB // R, body)

            @block.scalar
            def _(act):
                def body(i):
                    for k in range(R):
                        act.wait_ge(tab_ok, i * (3 * R) + 3 * k + 3)
                        row = ds(i * (R * P) + k * P, P)
                        act.dma_start(d.ta[row, :], tab[k][:, 0:D]).then_inc(tab_out[k], 16)
                        act.dma_start(d.tb[row, :], tab[k][:, D:D + TB_W]).then_inc(tab_out[k], 16)
                turns(act, NB // R, body)
                for k in range(R):
                    act.wait_ge(tab_out[k], 32 * (NB // R))


def rank(nc, d, m, which, tag):
    ctx, sb, pb, sem = scope(nc, tag)
    with ctx:
        keyrow = [sb(f"keyrow{p}", [P, 2, GE]) for p in range(2)]
        ohl = [sb(f"ohl{p}", [P, CG, P], bf16) for p in range(2)]
        ohh = [sb(f"ohh{p}", [P, CG, NB], bf16) for p in range(2)]
        ohT = [sb(f"ohT{p}", [P, GE]) for p in range(2)]
        same = [sb(f"same{c}", [P, P], bf16) for c in range(CG)]
        inside = [sb(f"inside{p}", [P, CG]) for p in range(2)]
        table = [sb(f"table{p}", [P, CG, NB]) for p in range(2)]
        hit = [sb(f"hit{p}", [P, CG, NB]) for p in range(2)]
        found = [sb(f"found{p}", [P, CG]) for p in range(2)]
        ps_n = [pb(f"ps_n{p}", [P, CG, NB]) for p in range(2)]
        ps_t = [pb(f"ps_t{p}", [P, CG, NB]) for p in range(2)]
        row_in = [sem(f"row_in{p}") for p in range(2)]
        onehot, compared, counted, stepped, looked, hit_ok, found_ok, ranked, zeroed = (
            sem(x) for x in ("onehot", "compared", "counted", "stepped", "looked", "hit_ok", "found_ok",
                             "ranked", "zeroed"))
        with nc.Block() as block:
            @block.sync
            def _(sp):
                def body(i):
                    for p in range(2):
                        if not first(i):
                            sp.wait_ge(ranked, i * 2 + p - 1)
                        sp.dma_start(keyrow[p][:, :, :],
                                     d.rowf[which, :, ds(i * (2 * GE) + p * GE, GE)].partition_broadcast(P)
                                     ).then_inc(row_in[p], 16)
                turns(sp, GROUPS // 2, body)

            @block.vector
            def _(v):
                step(v, nc.vector.memset(table[0][:, 0, :], 0.0), zeroed, 1)

                def finish(n, p, col):
                    v.wait_ge(looked, n)
                    step(v, nc.vector.tensor_tensor(hit[p][:, :, :], ps_t[p][:, :, :], ohh[p][:, :, :],
                                                    ALU.mult), hit_ok, n)
                    step(v, nc.vector.tensor_reduce(found[p][:, :], hit[p][:, :, :], X, ALU.add), found_ok, n)
                    v.wait_ge(compared, n * CG)
                    nc.vector.tensor_tensor(m.rank[:, which, col], found[p][:, :], inside[p][:, :],
                                            ALU.add).then_inc(ranked, 1)

                def body(i):
                    for p in range(2):
                        g = i * 2 + p
                        at = i * (2 * CG) + p * CG
                        v.wait_ge(row_in[p], i * 16 + 16)
                        lo = m.lo[:, which, ds(at, CG)].unsqueeze(2).to_broadcast([P, CG, P])
                        hi = m.hi[:, which, ds(at, CG)].unsqueeze(2).to_broadcast([P, CG, NB])
                        nc.vector.tensor_tensor(ohl[p][:, :, :],
                                                m.iota_row[:, :].unsqueeze(1).to_broadcast([P, CG, P]),
                                                lo, ALU.is_equal)
                        nc.vector.tensor_tensor(ohh[p][:, :, :],
                                                m.iota_row[:, 0:NB].unsqueeze(1).to_broadcast([P, CG, NB]),
                                                hi, ALU.is_equal)
                        nc.vector.tensor_scalar(ohT[p][:, :], keyrow[p][:, 1, :], m.iota_p[:, 0:1], None,
                                                ALU.is_equal).then_inc(onehot, 1)
                        for c in range(CG):
                            nc.vector.scalar_tensor_tensor(same[c][:, :], keyrow[p][:, 0, c * P:(c + 1) * P],
                                                           m.key[:, which, ds(at + c, 1)],
                                                           m.before[:, :], ALU.is_equal, ALU.mult,
                                                           accum_out=inside[p][:, c:c + 1]).then_inc(compared, 1)
                        if not (first(i) and p == 0):
                            finish(g, 1 - p, ds(at - CG, CG))
                        v.wait_ge(counted, g + 1)
                        for c in range(CG):
                            to = table[p][:, c + 1, :] if c + 1 < CG else table[1 - p][:, 0, :]
                            step(v, nc.vector.tensor_tensor(to, table[p][:, c, :], ps_n[p][:, c, :], ALU.add),
                                 stepped, g * CG + c + 1)
                turns(v, GROUPS // 2, body)
                finish(GROUPS, 1, ds((GROUPS - 1) * CG, CG))
                nc.vector.tensor_tensor(m.deg[:, which, 0:NB], table[0][:, 0, :], m.real[:, :], ALU.mult)
                nc.vector.tensor_copy(m.count[:, which, :], table[0][:, 0, :])

            @block.tensor
            def _(pe):
                def body(i):
                    for p in range(2):
                        g = i * 2 + p
                        pe.wait_ge(onehot, g + 1)
                        for c in range(CG):
                            last = nc.tensor.matmul(ps_n[p][:, c, :], ohl[p][:, c, :], ohh[p][:, c, :],
                                                    start=True, stop=True)
                        last.then_inc(counted, 1)
                        pe.wait_ge(stepped, g * CG + CG)
                        for c in range(CG):
                            last = nc.tensor.matmul(ps_t[p][:, c, :], ohT[p][:, c * P:(c + 1) * P],
                                                    table[p][:, c, :], start=True, stop=True)
                        last.then_inc(looked, 1)
                turns(pe, GROUPS // 2, body)


def places(nc, d, m):
    ctx, sb, pb, sem = scope(nc, "places")
    with ctx:
        total = [sb(f"total{w}", [NB, P]) for w in range(2)]
        most = sb("most", [P, 2])
        most_all = sb("most_all", [P, 2])
        visits_f = sb("visits_f", [P, 2])
        half = sb("half", [P, 2])
        ps_t = [pb(f"ps_t{w}", [NB, P]) for w in range(2)]
        ps_o = [pb(f"ps_o{w}", [P, NB]) for w in range(2)]
        summed, total_ok, placed, first_ok, most_ok, most_all_ok, chain, trips_ok = (
            sem(x) for x in ("summed", "total_ok", "placed", "first_ok", "most_ok", "most_all_ok",
                             "chain", "trips_ok"))
        with nc.Block() as block:
            @block.tensor
            def _(pe):
                for w in range(2):
                    nc.tensor.matmul(ps_t[w][:, :], m.count[:, w, :], m.ones[:, :], start=True,
                                     stop=True).then_inc(summed, 1)
                for w in range(2):
                    pe.wait_ge(total_ok, w + 1)
                    nc.tensor.matmul(ps_o[w][:, :], m.after[:, :], m.count[:, w, :], start=True, stop=False)
                    nc.tensor.matmul(ps_o[w][:, :], total[w][:, :], m.after[0:NB, 0:NB], start=False,
                                     stop=True).then_inc(placed, 1)

            @block.vector
            def _(v):
                for w in range(2):
                    v.wait_ge(summed, w + 1)
                    nc.vector.tensor_copy(total[w][:, :], ps_t[w][:, :]).then_inc(total_ok, 1)
                nc.vector.tensor_reduce(most[:, :], m.deg[:, :, 0:NB], X, ALU.max).then_inc(most_ok, 1)
                for w in range(2):
                    v.wait_ge(placed, w + 1)
                    step(v, nc.vector.tensor_copy(m.place[:, 0:NB, w], ps_o[w][:, :]), first_ok, w + 1)
                step(v, nc.vector.tensor_scalar(m.place[:, NB, :], m.place[:, 0, :], float(SLOTS), None, ALU.add),
                     chain, 1)
                v.wait_ge(most_all_ok, 2)
                step(v, nc.vector.tensor_scalar(half[:, :], most_all[:, :], float(SLOTS - 1), float(SLOTS),
                                                ALU.add, ALU.max), chain, 2)
                step(v, nc.vector.tensor_copy(m.visits[:, 0:2], half[:, :]), chain, 3)
                step(v, nc.vector.tensor_tensor(m.visits[:, 2:3], m.visits[:, 0:1], m.visits[:, 1:2], ALU.max), chain, 4)
                nc.vector.tensor_scalar(m.trips[:, :], m.visits[:, :], SLOTS.bit_length() - 1, None,
                                        ALU.arith_shift_right).then_inc(trips_ok, 1)

            @block.gpsimd
            def _(g):
                g.wait_ge(most_ok, 1)
                for w in range(2):
                    g.partition_all_reduce(most_all[:, w:w + 1], most[:, w:w + 1], P, bass.bass_isa.ReduceOp.max
                                           ).then_inc(most_all_ok, 1)


def l0_first(nc, d, m):
    ctx, sb, pb, sem = scope(nc, "first")
    with ctx:
        idx = [sb(f"idx{p}", [P, 2 * CG], i32) for p in range(2)]
        gs = [sb(f"gs{p}", [P, CG, D]) for p in range(2)]
        gt = [sb(f"gt{p}", [P, CG, TB_W]) for p in range(2)]
        hsum = [sb(f"hsum{p}", [P, CG, D]) for p in range(2)]
        h1 = [sb(f"h1{p}", [P, GE]) for p in range(2)]
        stats = sb("stats", [P, GROUPS, 6])
        ps = [pb(f"ps{p}", [P, GE]) for p in range(2)]
        idx_in = [sem(f"idx_in{p}") for p in range(2)]
        got = [sem(f"got{p}") for p in range(2)]
        stored = [sem(f"stored{p}") for p in range(2)]
        added, turned, copied, measured, passed, passed_act, stats_ok = (
            sem(x) for x in ("added", "turned", "copied", "measured", "passed", "passed_act", "stats_ok"))
        with nc.Block() as block:
            @block.sync
            def _(sp):
                def body(i):
                    for p in range(2):
                        if not first(i):
                            sp.wait_ge(got[p], i * (2 * CG * 16))
                        sp.dma_start(idx[p][:, :], d.idx[ds(i * 2 + p, 1), :, :].rearrange("a p c -> (a p) c")
                                     ).then_inc(idx_in[p], 16)
                turns(sp, GROUPS // 2, body)

            @block.gpsimd
            def _(g):
                def body(i):
                    for p in range(2):
                        hold(g, idx_in[p], i * 16 + 16, passed)
                        if not first(i):
                            hold(g, added, i * 2 + p - 1, passed)
                        for c in range(CG):
                            g.indirect_dma_start(gs[p][:, c, :], None, d.ta,
                                                 bass.IndirectOffsetOnAxis(ap=idx[p][:, c:c + 1], axis=0)
                                                 ).then_inc(got[p], 16)
                            g.indirect_dma_start(gt[p][:, c, :], None, d.tb,
                                                 bass.IndirectOffsetOnAxis(ap=idx[p][:, CG + c:CG + c + 1], axis=0)
                                                 ).then_inc(got[p], 16)
                turns(g, GROUPS // 2, body)

            @block.vector
            def _(v):
                def body(i):
                    for p in range(2):
                        v.wait_ge(got[p], (i + 1) * (2 * CG * 16))
                        if not first(i):
                            v.wait_ge(turned, i * 2 + p - 1)
                        at = ds(i * (2 * CG) + p * CG, CG)
                        nc.vector.tensor_tensor(m.where_t[:, at], m.rank[:, 1, at], gt[p][:, :, D], ALU.add)
                        nc.vector.tensor_tensor(hsum[p][:, :, :], gs[p][:, :, :], gt[p][:, :, 0:D],
                                                ALU.add).then_inc(added, 1)
                        hold(v, copied, i * 2 + p + 1, passed)
                        nc.vector.bn_stats(stats[:, ds(i * 2 + p, 1), :].rearrange("p a s -> p (a s)"),
                                           h1[p][:, :]).then_inc(measured, 1)
                turns(v, GROUPS // 2, body)
                v.wait_ge(measured, GROUPS)
                nc.vector.bn_stats(stats[:, GROUPS - 1, :], h1[1][:, 0:LAST]).then_inc(stats_ok, 1)
                v.wait_ge(stats_ok, 1)
                nc.vector.bn_aggr(m.mv1[:, :], stats[:, :, :].rearrange("p g s -> p (g s)"))

            @block.tensor
            def _(pe):
                def body(i):
                    for p in range(2):
                        pe.wait_ge(added, i * 2 + p + 1)
                        if not first(i):
                            pe.wait_ge(copied, i * 2 + p - 1)
                        for c in range(CG):
                            last = nc.tensor.transpose(ps[p][:, c * P:(c + 1) * P], hsum[p][:, c, :], m.ident[:, :])
                        last.then_inc(turned, 1)
                turns(pe, GROUPS // 2, body)

            @block.scalar
            def _(act):
                def body(i):
                    for p in range(2):
                        hold(act, turned, i * 2 + p + 1, passed_act)
                        if not first(i):
                            act.wait_ge(stored[p], i * 16)
                            hold(act, measured, i * 2 + p - 1, passed_act)
                        nc.scalar.activation(h1[p][:, :], ps[p][:, :], ACT.Copy).then_inc(copied, 1)
                        act.wait_ge(copied, i * 2 + p + 1)
                        act.dma_start(d.h1[:, ds(i * (2 * GE) + p * GE, GE)], h1[p][:, :]).then_inc(stored[p], 16)
                turns(act, GROUPS // 2, body)
                for p in range(2):
                    act.wait_ge(stored[p], 16 * (GROUPS // 2))


def norm_terms(nc, m, mv, gamma, beta, scale, shift, tag, mean_extra=None):
    ctx, sb, pb, sem = scope(nc, tag)
    with ctx:
        vpe, root, inv, t = (sb(x, [P, 1]) for x in ("vpe", "root", "inv", "t"))
        eps_ok, root_ok, chain = (sem(x) for x in ("eps_ok", "root_ok", "chain"))
        with nc.Block() as block:
            @block.vector
            def _(v):
                nc.vector.tensor_scalar(vpe[:, :], mv[:, 1:2], EPS, None, ALU.add).then_inc(eps_ok, 1)
                v.wait_ge(root_ok, 1)
                step(v, nc.vector.reciprocal(inv[:, :], root[:, :]), chain, 1)
                step(v, nc.vector.tensor_tensor(scale[:, :], inv[:, :], gamma, ALU.mult), chain, 2)
                step(v, nc.vector.tensor_tensor(t[:, :], mv[:, 0:1], scale[:, :], ALU.mult), chain, 3)
                step(v, nc.vector.tensor_tensor(shift[:, :], beta, t[:, :], ALU.subtract), chain, 4)

            @block.scalar
            def _(act):
                act.wait_ge(eps_ok, 1)
                nc.scalar.activation(root[:, :], vpe[:, :], ACT.Sqrt).then_inc(root_ok, 1)


def l0_second(nc, d, m):
    ctx, sb, pb, sem = scope(nc, "second")
    R = 4
    with ctx:
        h1 = [sb(f"h1{k}", [P, GE]) for k in range(R)]
        hr = [sb(f"hr{k}", [P, GE]) for k in range(R)]
        stats = sb("stats", [P, GROUPS, 6])
        raw = sb("raw", [P, 2])
        ps = [pb(f"ps{k}", [P, GE]) for k in range(R)]
        h1_in = [sem(f"h1_in{k}") for k in range(R)]
        relued, mm, measured, passed, stats_ok, raw_ok = (
            sem(x) for x in ("relued", "mm", "measured", "passed", "stats_ok", "raw_ok"))
        with nc.Block() as block:
            @block.sync
            def _(sp):
                def body(i):
                    for k in range(R):
                        if not first(i):
                            sp.wait_ge(relued, i * R - R + k + 1)
                        sp.dma_start(h1[k][:, :], d.h1[:, ds(i * (R * GE) + k * GE, GE)]).then_inc(h1_in[k], 16)
                turns(sp, GROUPS // R, body)

            @block.scalar
            def _(act):
                def body(i):
                    for k in range(R):
                        act.wait_ge(h1_in[k], i * 16 + 16)
                        if not first(i):
                            act.wait_ge(mm, i * R - R + k + 1)
                        nc.scalar.activation(hr[k][:, :], h1[k][:, :], ACT.Relu, bias=m.shift1[:, 0:1],
                                             scale=m.scale1[:, 0:1]).then_inc(relued, 1)
                turns(act, GROUPS // R, body)

            @block.tensor
            def _(pe):
                def body(i):
                    for k in range(R):
                        pe.wait_ge(relued, i * R + k + 1)
                        if not first(i):
                            pe.wait_ge(measured, i * R - R + k + 1)
                        nc.tensor.matmul(ps[k][:, :], m.w2t[:, :], hr[k][:, :], start=True, stop=True).then_inc(mm, 1)
                turns(pe, GROUPS // R, body)

            @block.vector
            def _(v):
                def body(i):
                    for k in range(R):
                        hold(v, mm, i * R + k + 1, passed)
                        nc.vector.bn_stats(stats[:, ds(i * R + k, 1), :].rearrange("p a s -> p (a s)"),
                                           ps[k][:, :]).then_inc(measured, 1)
                turns(v, GROUPS // R, body)
                v.wait_ge(measured, GROUPS)
                nc.vector.bn_stats(stats[:, GROUPS - 1, :], ps[R - 1][:, 0:LAST]).then_inc(stats_ok, 1)
                v.wait_ge(stats_ok, 1)
                step(v, nc.vector.bn_aggr(raw[:, :], stats[:, :, :].rearrange("p g s -> p (g s)")), raw_ok, 1)
                nc.vector.tensor_tensor(m.mv2[:, 0:1], raw[:, 0:1], m.cols[:, 4:5], ALU.add)
                nc.vector.tensor_copy(m.mv2[:, 1:2], raw[:, 1:2])


def fold_second(nc, d, m):
    ctx, sb, pb, sem = scope(nc, "fold")
    with ctx:
        w2 = sb("w2", [P, D])
        w2s = sb("w2s", [P, D])
        t, col = sb("t", [P, 1]), sb("col", [P, 1])
        ps_w, ps_r = pb("ps_w", [P, D]), pb("ps_r", [1, D])
        w_in, scaled, t_ok, col_ok, turned = (sem(x) for x in ("w_in", "scaled", "t_ok", "col_ok", "turned"))
        with nc.Block() as block:
            @block.sync
            def _(sp):
                sp.dma_start(w2[:, :], d.w2).then_inc(w_in, 16)

            @block.vector
            def _(v):
                v.wait_ge(w_in, 16)
                nc.vector.tensor_scalar(w2s[:, :], w2[:, :], m.scale2[:, 0:1], None, ALU.mult).then_inc(scaled, 1)
                step(v, nc.vector.tensor_tensor(t[:, :], m.cols[:, 4:5], m.scale2[:, :], ALU.mult), t_ok, 1)
                nc.vector.tensor_tensor(col[:, :], t[:, :], m.shift2[:, :], ALU.add).then_inc(col_ok, 1)
                v.wait_ge(turned, 2)
                nc.vector.tensor_copy(m.w2ts[:, :], ps_w[:, :])
                nc.vector.tensor_copy(m.row2[:, :], ps_r[:, :])

            @block.tensor
            def _(pe):
                pe.wait_ge(scaled, 1)
                nc.tensor.transpose(ps_w[:, :], w2s[:, :], m.ident[:, :]).then_inc(turned, 1)
                pe.wait_ge(col_ok, 1)
                nc.tensor.matmul(ps_r[:, :], col[:, :], m.ident[:, :], start=True, stop=True).then_inc(turned, 1)


def l0_third(nc, d, m):
    ctx, sb, pb, sem = scope(nc, "third")
    with ctx:
        h1 = [sb(f"h1{p}", [P, GE]) for p in range(2)]
        hr = [sb(f"hr{p}", [P, GE]) for p in range(2)]
        up = [sb(f"up{p}", [P, CG, D]) for p in range(2)]
        to = [sb(f"to{p}", [P, CG], i32) for p in range(2)]
        zero = sb("zero", [SLOTS, D])
        ps = [pb(f"ps{p}", [P, CG, D]) for p in range(2)]
        h1_in = [sem(f"h1_in{p}") for p in range(2)]
        put = [sem(f"put{p}") for p in range(2)]
        relued, mm, up_ok, to_ok, passed, zero_ok, zero_out = (
            sem(x) for x in ("relued", "mm", "up_ok", "to_ok", "passed", "zero_ok", "zero_out"))
        with nc.Block() as block:
            @block.sync
            def _(sp):
                sp.wait_ge(zero_ok, 1)
                sp.dma_start(d.up[EP:EP + SLOTS, :], zero[:, :]).then_inc(zero_out, 16)

                def body(i):
                    for p in range(2):
                        if not first(i):
                            sp.wait_ge(relued, i * 2 + p - 1)
                        sp.dma_start(h1[p][:, :], d.h1[:, ds(i * (2 * GE) + p * GE, GE)]).then_inc(h1_in[p], 16)
                turns(sp, GROUPS // 2, body)
                sp.wait_ge(zero_out, 16)

            @block.vector
            def _(v):
                nc.vector.memset(zero[:, :], 0.0).then_inc(zero_ok, 1)

                def body(i):
                    for p in range(2):
                        if not first(i):
                            v.wait_ge(put[p], i * (16 * CG))
                        nc.vector.tensor_scalar(to[p][:, :], m.where_t[:, ds(i * (2 * CG) + p * CG, CG)], 0.0, None,
                                                ALU.add).then_inc(to_ok, 1)
                turns(v, GROUPS // 2, body)

            @block.scalar
            def _(act):
                def body(i):
                    for p in range(2):
                        act.wait_ge(h1_in[p], i * 16 + 16)
                        if not first(i):
                            act.wait_ge(mm, i * 2 + p - 1)
                        nc.scalar.activation(hr[p][:, :], h1[p][:, :], ACT.Relu, bias=m.shift1[:, 0:1],
                                             scale=m.scale1[:, 0:1]).then_inc(relued, 1)
                        act.wait_ge(mm, i * 2 + p + 1)
                        if not first(i):
                            act.wait_ge(put[p], i * (16 * CG))
                        nc.scalar.activation(up[p][:, :, :], ps[p][:, :, :], ACT.Relu).then_inc(up_ok, 1)
                turns(act, GROUPS // 2, body)

            @block.tensor
            def _(pe):
                def body(i):
                    for p in range(2):
                        pe.wait_ge(relued, i * 2 + p + 1)
                        if not first(i):
                            pe.wait_ge(up_ok, i * 2 + p - 1)
                        for c in range(CG):
                            nc.tensor.matmul(ps[p][:, c, :], hr[p][:, c * P:(c + 1) * P], m.w2ts[:, :],
                                             start=True, stop=False)
                            last = nc.tensor.matmul(ps[p][:, c, :], m.ones[0:1, :], m.row2[:, :],
                                                    start=False, stop=True)
                        last.then_inc(mm, 1)
                turns(pe, GROUPS // 2, body)

            @block.gpsimd
            def _(g):
                def body(i):
                    for p in range(2):
                        hold(g, to_ok, i * 2 + p + 1, passed)
                        hold(g, up_ok, i * 2 + p + 1, passed)
                        for c in range(CG):
                            g.indirect_dma_start(d.up, bass.IndirectOffsetOnAxis(ap=to[p][:, c:c + 1], axis=0),
                                                 up[p][:, c, :], None).then_inc(put[p], 16)
                turns(g, GROUPS // 2, body)
                for p in range(2):
                    g.wait_ge(put[p], 16 * CG * (GROUPS // 2))


def l0_gather(nc, d, m):
    ctx, sb, pb, sem = scope(nc, "sum")
    with ctx:
        run = [sb(f"run{p}", [P, SLOTS, D]) for p in range(2)]
        at_f = [sb(f"at_f{p}", [P, 1]) for p in range(2)]
        at_c = [sb(f"at_c{p}", [P, 1]) for p in range(2)]
        at = [sb(f"at{p}", [P, 1], i32) for p in range(2)]
        left = [sb(f"left{p}", [P, 1]) for p in range(2)]
        live = [sb(f"live{p}", [P, SLOTS]) for p in range(2)]
        masked = [sb(f"masked{p}", [P, SLOTS, D]) for p in range(2)]
        part = [sb(f"part{p}", [P, D]) for p in range(2)]
        passed_slots = sb("passed_slots", [P, 1])
        got = [sem(f"got{p}") for p in range(2)]
        at_f_ok, at_c_ok, at_ok, left_ok, live_ok, masked_ok, part_ok, passed, summed, slots_ok, zeroed = (
            sem(x) for x in ("at_f_ok", "at_c_ok", "at_ok", "left_ok", "live_ok", "masked_ok", "part_ok",
                             "passed", "summed", "slots_ok", "zeroed"))
        with nc.Block() as block:
            @block.vector
            def _(v):
                rounds = v.value_load(m.trips[0:1, 1:2], min_val=1, max_val=EP // SLOTS + 1)
                nc.vector.memset(m.agg[:, :, :], 0.0).then_inc(zeroed, 1)
                step(v, nc.vector.memset(passed_slots[:, :], 0.0), zeroed, 2)

                def aim(n, b, p):
                    step(v, nc.vector.tensor_tensor(at_f[p][:, :], m.place[:, ds(b, 1), 1], passed_slots[:, :],
                                                    ALU.add), at_f_ok, n)
                    step(v, nc.vector.tensor_scalar(at_c[p][:, :], at_f[p][:, :], float(EP), float(D), ALU.min,
                                                    ALU.mult), at_c_ok, n)
                    nc.vector.tensor_copy(at[p][:, :], at_c[p][:, :]).then_inc(at_ok, 1)

                aim(1, 0, 0)
                with v.Fori(0, rounds) as r:
                    with v.Fori(0, NB // 2) as j:
                        for p in range(2):
                            n = r * NB + j * 2 + p + 1
                            b = j * 2 + p
                            aim(n + 1, b + 1, 1 - p)
                            step(v, nc.vector.tensor_tensor(left[p][:, :], m.deg[:, 1, ds(b, 1)], passed_slots[:, :],
                                                            ALU.subtract), left_ok, n)
                            step(v, nc.vector.tensor_scalar(live[p][:, :], m.iota_row[:, 0:SLOTS], left[p][:, 0:1],
                                                            None, ALU.is_lt), live_ok, n)
                            v.wait_ge(got[p], r * (NB // 2 * 16) + j * 16 + 16)
                            step(v, nc.vector.tensor_tensor(
                                masked[p][:, :, :], run[p][:, :, :],
                                live[p][:, :].unsqueeze(2).to_broadcast([P, SLOTS, D]), ALU.mult), masked_ok, n)
                            step(v, nc.vector.tensor_reduce(part[p][:, :],
                                                            masked[p][:, :, :].rearrange("p s f -> p f s"), X,
                                                            ALU.add), part_ok, n)
                            step(v, nc.vector.tensor_tensor(m.agg[:, ds(b, 1), :].rearrange("p a f -> p (a f)"),
                                                            m.agg[:, ds(b, 1), :].rearrange("p a f -> p (a f)"),
                                                            part[p][:, :], ALU.add), summed, n)
                    step(v, nc.vector.tensor_scalar(passed_slots[:, :], passed_slots[:, :], float(SLOTS), None,
                                                    ALU.add), slots_ok, r + 1)

            @block.gpsimd
            def _(g):
                rounds = g.value_load(m.trips[0:1, 1:2], min_val=1, max_val=EP // SLOTS + 1)
                flat = d.up.rearrange("n f -> (n f)").rearrange("(n o) -> n o", o=1)

                def fetch(n, p):
                    hold(g, at_ok, n, passed)
                    g.indirect_dma_start(run[p][:, :, :].rearrange("p s f -> p (s f)"), None, flat,
                                         bass.IndirectOffsetOnAxis(ap=at[p][:, 0:1], axis=0)).then_inc(got[p], 16)

                fetch(1, 0)
                with g.Fori(0, rounds) as r:
                    with g.Fori(0, NB // 2) as j:
                        for p in range(2):
                            n = r * NB + j * 2 + p + 1
                            fetch(n + 1, 1 - p)
                g.wait_ge(got[0], rounds * (NB // 2 * 16) + 16)


def layer_norm(nc, d, m):
    ctx, sb, pb, sem = scope(nc, "norm1")
    with ctx:
        x = sb("x", [P, NB, D])
        sq = sb("sq", [P, NB, D])
        tot, mean, var, root, inv = (sb(n, [P, NB]) for n in ("tot", "mean", "var", "root", "inv"))
        x_in, chain, sq_ok, var_ok, root_ok, out_ok, stored, cent_ok = (
            sem(n) for n in ("x_in", "chain", "sq_ok", "var_ok", "root_ok", "out_ok", "stored", "cent_ok"))
        wide = [P, NB, D]
        with nc.Block() as block:
            @block.sync
            def _(sp):
                sp.dma_start(x[:, :, :], d.x.rearrange("(b p) f -> p b f", p=P)).then_inc(x_in, 16)
                sp.wait_ge(out_ok, 1)
                sp.dma_start(d.x1.rearrange("(b p) f -> p b f", p=P), m.agg[:, :, :]).then_inc(stored, 16)
                sp.wait_ge(stored, 16)

            @block.vector
            def _(v):
                v.wait_ge(x_in, 16)
                step(v, nc.vector.tensor_tensor(x[:, :, :], x[:, :, :], m.agg[:, :, :], ALU.add), chain, 1)
                step(v, nc.vector.tensor_reduce(tot[:, :], x[:, :, :], X, ALU.add), chain, 2)
                step(v, nc.vector.tensor_scalar(mean[:, :], tot[:, :], 1.0 / D, None, ALU.mult), chain, 3)
                nc.vector.tensor_tensor(x[:, :, :], x[:, :, :], mean[:, :].unsqueeze(2).to_broadcast(wide),
                                        ALU.subtract).then_inc(cent_ok, 1)
                v.wait_ge(sq_ok, 1)
                step(v, nc.vector.tensor_reduce(tot[:, :], sq[:, :, :], X, ALU.add), chain, 4)
                nc.vector.tensor_scalar(var[:, :], tot[:, :], 1.0 / D, EPS, ALU.mult, ALU.add).then_inc(var_ok, 1)
                v.wait_ge(root_ok, 1)
                step(v, nc.vector.reciprocal(inv[:, :], root[:, :]), chain, 5)
                nc.vector.tensor_tensor(m.agg[:, :, :], x[:, :, :], inv[:, :].unsqueeze(2).to_broadcast(wide),
                                        ALU.mult).then_inc(out_ok, 1)

            @block.scalar
            def _(act):
                act.wait_ge(cent_ok, 1)
                nc.scalar.activation(sq[:, :, :], x[:, :, :], ACT.Square).then_inc(sq_ok, 1)
                act.wait_ge(var_ok, 1)
                nc.scalar.activation(root[:, :], var[:, :], ACT.Sqrt).then_inc(root_ok, 1)
def l1_self_terms(nc, d, m):
    ctx, sb, pb, sem = scope(nc, "selft")
    with ctx:
        col, cols, wt, we = sb("col", [DE, 1]), sb("cols", [DE, P]), sb("wt", [DE, D]), sb("we", [DE, 2 * D])
        ps = pb("ps", [P, 3 * D])
        w_in, cols_ok, mm = (sem(x) for x in ("w_in", "cols_ok", "mm"))
        with nc.Block() as block:
            @block.sync
            def _(sp):
                sp.dma_start(col[:, :], d.time0).then_inc(w_in, 16)
                sp.dma_start(wt[:, :], d.wt).then_inc(w_in, 16)
                sp.dma_start(we[:, :], d.we[DE:2 * DE, :]).then_inc(w_in, 16)

            @block.vector
            def _(v):
                v.wait_ge(w_in, 48)
                nc.vector.tensor_copy(cols[:, :], col[:, 0:1].to_broadcast([DE, P])).then_inc(cols_ok, 1)
                v.wait_ge(mm, 1)
                nc.vector.tensor_copy(m.selfadd[:, :], ps[:, :])

            @block.tensor
            def _(pe):
                pe.wait_ge(cols_ok, 1)
                nc.tensor.matmul(ps[:, 0:D], cols[:, :], wt[:, :], start=True, stop=True)
                nc.tensor.matmul(ps[:, D:3 * D], cols[:, :], we[:, :], start=True, stop=True).then_inc(mm, 1)


def l1_tables(nc, d, m):
    ctx, sb, pb, sem = scope(nc, "tables")
    R = 3
    NR = NB - NB % R
    with ctx:
        wx, bx = sb("wx", [P, 3 * D]), sb("bx", [P, 3 * D])
        xb = [sb(f"xb{k}", [P, D]) for k in range(R)]
        xbT = [sb(f"xbT{k}", [P, D]) for k in range(R)]
        tn = [sb(f"tn{k}", [P, TN_W]) for k in range(R)]
        me = [sb(f"me{k}", [P, 3 * D]) for k in range(R)]
        kr = [sb(f"kr{k}", [P, D]) for k in range(R)]
        qk = [sb(f"qk{k}", [P, D]) for k in range(R)]
        score = [sb(f"score{k}", [P, HEADS]) for k in range(R)]
        ps_t = [pb(f"ps_t{k}", [P, D]) for k in range(R)]
        ps = [pb(f"ps{k}", [P, 3 * D]) for k in range(R)]
        w_in, turned, xbT_ok, mm, tn_ok, me_ok, kr_ok, qk_ok, score_ok, kept = (
            sem(x) for x in ("w_in", "turned", "xbT_ok", "mm", "tn_ok", "me_ok", "kr_ok", "qk_ok", "score_ok", "kept"))
        xb_in = [sem(f"xb_in{k}") for k in range(R)]
        stored = [sem(f"stored{k}") for k in range(R)]

        def blocks(eng, one):
            def body(i):
                for k in range(R):
                    one(i, k, i * R + k + 1)
            turns(eng, NR // R, body)
            for k in range(NB - NR):
                one(NR // R, k, NR + k + 1)

        with nc.Block() as block:
            @block.sync
            def _(sp):
                sp.dma_start(wx[:, :], d.wx).then_inc(w_in, 16)
                sp.dma_start(bx[:, :], d.bx.partition_broadcast(P)).then_inc(w_in, 16)

                def one(i, k, n):
                    if not first(i):
                        sp.wait_ge(turned, n - R)
                    sp.dma_start(xb[k][:, :], d.x1[ds((n - 1) * P, P), :]).then_inc(xb_in[k], 16)
                blocks(sp, one)

            @block.tensor
            def _(pe):
                pe.wait_ge(w_in, 32)

                def one(i, k, n):
                    pe.wait_ge(xb_in[k], i * 16 + 16)
                    if not first(i):
                        pe.wait_ge(xbT_ok, n - R)
                    nc.tensor.transpose(ps_t[k][:, :], xb[k][:, :], m.ident[:, :]).then_inc(turned, 1)
                    pe.wait_ge(xbT_ok, n)
                    if not first(i):
                        pe.wait_ge(tn_ok, (n - R) * 2)
                    nc.tensor.matmul(ps[k][:, :], xbT[k][:, :], wx[:, :], start=True, stop=True).then_inc(mm, 1)
                blocks(pe, one)

            @block.scalar
            def _(act):
                def one(i, k, n):
                    act.wait_ge(turned, n)
                    if not first(i):
                        act.wait_ge(mm, n - R)
                    nc.scalar.activation(xbT[k][:, :], ps_t[k][:, :], ACT.Copy).then_inc(xbT_ok, 1)
                    act.wait_ge(tn_ok, n * 2)
                    act.dma_start(d.tn[ds((n - 1) * P, P), :], tn[k][:, :]).then_inc(stored[k], 16)
                blocks(act, one)
                for k in range(R):
                    act.wait_ge(stored[k], 16 * (NR // R + (k < NB - NR)))

            @block.vector
            def _(v):
                def one(i, k, n):
                    if not first(i):
                        v.wait_ge(stored[k], i * 16)
                    nc.vector.tensor_scalar(tn[k][:, 3 * D:TN_W], m.place[:, ds(n - 1, 1), :].rearrange("p a w -> p (a w)"),
                                            0.0, None, ALU.add).then_inc(tn_ok, 1)
                    v.wait_ge(mm, n)
                    nc.vector.tensor_tensor(tn[k][:, 0:3 * D], ps[k][:, :], bx[:, :], ALU.add).then_inc(tn_ok, 1)
                    v.wait_ge(tn_ok, n * 2)
                    step(v, nc.vector.tensor_tensor(me[k][:, :], tn[k][:, 0:3 * D], m.selfadd[:, :], ALU.add), me_ok, n)
                    step(v, nc.vector.tensor_scalar(kr[k][:, :], me[k][:, D:2 * D], 0.0, None, ALU.max), kr_ok, n)
                    step(v, nc.vector.scalar_tensor_tensor(qk[k][:, :], me[k][:, 0:D], 0.0, kr[k][:, :], ALU.max,
                                                           ALU.mult), qk_ok, n)
                    step(v, nc.vector.tensor_reduce(score[k][:, :], qk[k][:, :].rearrange("p (h f) -> p h f", h=HEADS),
                                                    X, ALU.add), score_ok, n)
                    nc.vector.tensor_scalar(m.top[:, ds(n - 1, 1), :].rearrange("p a h -> p (a h)"), score[k][:, :],
                                            0.0, None, ALU.add)
                    nc.vector.tensor_scalar(m.agg[:, ds(n - 1, 1), :].rearrange("p a f -> p (a f)"),
                                            me[k][:, 2 * D:3 * D], 0.0, None, ALU.add)
                nc.vector.memset(m.den[:, :, :], 1.0)
                blocks(v, one)


def l1_edges(nc, d, m):
    ctx, sb, pb, sem = scope(nc, "edges")
    with ctx:
        wt, we = sb("wt", [DE, D]), sb("we", [P, 2 * D])
        idx = [sb(f"idx{p}", [P, 2 * CG], i32) for p in range(2)]
        ft = [sb(f"ft{p}", [DE, GE]) for p in range(2)]
        fe = [sb(f"fe{p}", [P, GE]) for p in range(2)]
        rows = [[sb(f"rows{w}{p}", [P, CG, TN_W]) for p in range(2)] for w in range(2)]
        qk = [[sb(f"qk{w}{p}", [P, CG, 2 * D]) for p in range(2)] for w in range(2)]
        prod = [[sb(f"prod{w}{p}", [P, CG, D]) for p in range(2)] for w in range(2)]
        msg = [[sb(f"msg{w}{p}", [P, CG, MSG_W]) for p in range(2)] for w in range(2)]
        to_f = [sb(f"to_f{p}", [P, CG]) for p in range(2)]
        to = [[sb(f"to{w}{p}", [P, CG], i32) for p in range(2)] for w in range(2)]
        zero = sb("zero", [SLOTS, MSG_W])
        ps = [pb(f"ps{p}", [P, CG, BANK]) for p in range(2)]
        w_in, mm, added, v_ok, relued, prod_ok, msg_ok, to_ok, passed, zero_ok, zero_out = (
            sem(x) for x in ("w_in", "mm", "added", "v_ok", "relued", "prod_ok", "msg_ok", "to_ok", "passed", "zero_ok",
                             "zero_out"))
        idx_in, f_in, got, put = ([sem(f"{x}{p}") for p in range(2)] for x in ("idx_in", "f_in", "got", "put"))
        GOT = 2 * CG * 16
        with nc.Block() as block:
            @block.sync
            def _(sp):
                sp.dma_start(wt[:, :], d.wt).then_inc(w_in, 16)
                sp.dma_start(we[:, :], d.we).then_inc(w_in, 16)
                sp.wait_ge(zero_ok, 1)
                for w in range(2):
                    sp.dma_start(d.msg_of[w][EP:EP + SLOTS, :], zero[:, :]).then_inc(zero_out, 16)

                def body(i):
                    for p in range(2):
                        if not first(i):
                            sp.wait_ge(got[p], i * GOT)
                        sp.dma_start(idx[p][:, :], d.idx[ds(i * 2 + p, 1), :, :].rearrange("a p c -> (a p) c")
                                     ).then_inc(idx_in[p], 16)
                        if not first(i):
                            sp.wait_ge(mm, i * 2 + p - 1)
                        sp.dma_start(ft[p][:, :], d.ft[:, ds(i * (2 * GE) + p * GE, GE)]).then_inc(f_in[p], 16)
                        sp.dma_start(fe[p][:, :], d.fe[:, ds(i * (2 * GE) + p * GE, GE)]).then_inc(f_in[p], 16)
                turns(sp, GROUPS // 2, body)
                sp.wait_ge(zero_out, 32)

            @block.gpsimd
            def _(g):
                def gather(i, p, n):
                    hold(g, idx_in[p], i * 16 + 16, passed)
                    if not first(i):
                        hold(g, to_ok, (n - 2) * 2, passed)
                    for c in range(CG):
                        for w in range(2):
                            g.indirect_dma_start(rows[w][p][:, c, :], None, d.tn, bass.IndirectOffsetOnAxis(
                                ap=idx[p][:, w * CG + c:w * CG + c + 1], axis=0)).then_inc(got[p], 16)

                def scatter(p, n):
                    hold(g, msg_ok, n * 2, passed)
                    hold(g, to_ok, n * 2, passed)
                    for c in range(CG):
                        for w in range(2):
                            g.indirect_dma_start(d.msg_of[w], bass.IndirectOffsetOnAxis(
                                ap=to[w][p][:, c:c + 1], axis=0), msg[w][p][:, c, :], None).then_inc(put[p], 16)

                def body(i):
                    gather(i, 0, i * 2 + 1)
                    if not first(i):
                        scatter(1, i * 2)
                    gather(i, 1, i * 2 + 2)
                    scatter(0, i * 2 + 1)
                turns(g, GROUPS // 2, body)
                scatter(1, GROUPS)
                for p in range(2):
                    g.wait_ge(put[p], GOT * (GROUPS // 2))

            @block.tensor
            def _(pe):
                pe.wait_ge(w_in, 32)

                def body(i):
                    for p in range(2):
                        n = i * 2 + p + 1
                        pe.wait_ge(f_in[p], i * 32 + 32)
                        if not first(i):
                            pe.wait_ge(v_ok, (n - 2) * 2)
                        for c in range(CG):
                            nc.tensor.matmul(ps[p][:, c, D:3 * D], fe[p][:, c * P:(c + 1) * P], we[:, :],
                                             start=True, stop=True)
                            last = nc.tensor.matmul(ps[p][:, c, 0:D], ft[p][:, c * P:(c + 1) * P], wt[:, :],
                                                    start=True, stop=True)
                        last.then_inc(mm, 1)
                turns(pe, GROUPS // 2, body)

            @block.vector
            def _(v):
                nc.vector.memset(zero[:, :], 0.0).then_inc(zero_ok, 1)

                def finish(p, n):
                    for w in range(2):
                        v.wait_ge(relued, (n - 1) * 2 + w + 1)
                        step(v, nc.vector.tensor_tensor(prod[w][p][:, :, :], qk[w][p][:, :, 0:D],
                                                        qk[w][p][:, :, D:2 * D], ALU.mult), prod_ok, (n - 1) * 2 + w + 1)
                        nc.vector.tensor_reduce(msg[w][p][:, :, D:MSG_W],
                                                prod[w][p][:, :, :].rearrange("p c (h f) -> p c h f", h=HEADS),
                                                X, ALU.add).then_inc(msg_ok, 1)

                def body(i):
                    for p in range(2):
                        n = i * 2 + p + 1
                        v.wait_ge(mm, n)
                        v.wait_ge(got[p], (i + 1) * GOT)
                        if not first(i):
                            v.wait_ge(put[p], i * GOT)
                            v.wait_ge(msg_ok, (n - 2) * 2)
                        for w in range(2):
                            nc.vector.tensor_tensor(qk[w][p][:, :, 0:D], ps[p][:, :, 0:D], rows[w][p][:, :, 0:D],
                                                    ALU.add).then_inc(added, 1)
                            nc.vector.tensor_tensor(qk[w][p][:, :, D:2 * D], ps[p][:, :, D:2 * D],
                                                    rows[1 - w][p][:, :, D:2 * D], ALU.add).then_inc(added, 1)
                        for w in range(2):
                            nc.vector.tensor_tensor(msg[w][p][:, :, 0:D], ps[p][:, :, 2 * D:3 * D],
                                                    rows[1 - w][p][:, :, 2 * D:3 * D], ALU.add).then_inc(v_ok, 1)
                        for w in range(2):
                            at = ds(i * (2 * CG) + p * CG, CG)
                            nc.vector.tensor_tensor(to[w][p][:, :], m.rank[:, w, at], rows[w][p][:, :, 3 * D + w],
                                                    ALU.add).then_inc(to_ok, 1)
                        if not (first(i) and p == 0):
                            finish(1 - p, n - 1)
                turns(v, GROUPS // 2, body)
                finish(1, GROUPS)

            @block.scalar
            def _(act):
                def body(i):
                    for p in range(2):
                        n = i * 2 + p + 1
                        for w in range(2):
                            act.wait_ge(added, (n - 1) * 4 + 2 * w + 2)
                            nc.scalar.activation(qk[w][p][:, :, :], qk[w][p][:, :, :], ACT.Relu).then_inc(relued, 1)
                turns(act, GROUPS // 2, body)


def l1_softmax(nc, d, m):
    ctx, sb, pb, sem = scope(nc, "soft")
    with ctx:
        run = [sb(f"run{p}", [P, 2, SLOTS, MSG_W]) for p in range(2)]
        at_f, at_c, left = ([sb(f"{x}{p}", [P, 2]) for p in range(2)] for x in ("at_f", "at_c", "left"))
        at = [sb(f"at{p}", [P, 2], i32) for p in range(2)]
        off = [sb(f"off{p}", [P, 2, SLOTS]) for p in range(2)]
        score = [sb(f"score{p}", [P, 2 * SLOTS, HEADS]) for p in range(2)]
        under = [sb(f"under{p}", [P, 2 * SLOTS, HEADS]) for p in range(2)]
        w = [sb(f"w{p}", [P, 2 * SLOTS, HEADS]) for p in range(2)]
        most, top, fall, corr, wsum, den = ([sb(f"{x}{p}", [P, HEADS]) for p in range(2)]
                                            for x in ("most", "top", "fall", "corr", "wsum", "den"))
        prod = [sb(f"prod{p}", [P, 2 * SLOTS, D]) for p in range(2)]
        part = [sb(f"part{p}", [P, D]) for p in range(2)]
        old = [sb(f"old{p}", [P, D]) for p in range(2)]
        passed_slots = sb("passed_slots", [P, 2])
        got = [sem(f"got{p}") for p in range(2)]
        (at_f_ok, at_c_ok, at_ok, left_ok, off_ok, score_ok, most_ok, top_ok, under_ok, w_ok, wsum_ok, den_ok,
         prod_ok, part_ok, old_ok, summed, passed, slots_ok) = (
            sem(x) for x in ("at_f_ok", "at_c_ok", "at_ok", "left_ok", "off_ok", "score_ok", "most_ok", "top_ok",
                             "under_ok", "w_ok", "wsum_ok", "den_ok", "prod_ok", "part_ok", "old_ok", "summed",
                             "passed", "slots_ok"))
        with nc.Block() as block:
            @block.vector
            def _(v):
                rounds = v.value_load(m.trips[0:1, 2:3], min_val=1, max_val=EP // SLOTS + 1)
                step(v, nc.vector.memset(passed_slots[:, :], 0.0), slots_ok, 1)

                def aim(n, b, p):
                    step(v, nc.vector.tensor_tensor(at_f[p][:, :], m.place[:, ds(b, 1), :].rearrange("p a w -> p (a w)"),
                                                    passed_slots[:, :], ALU.add), at_f_ok, n)
                    step(v, nc.vector.tensor_scalar(at_c[p][:, :], at_f[p][:, :], float(EP), float(MSG_W), ALU.min,
                                                    ALU.mult), at_c_ok, n)
                    nc.vector.tensor_copy(at[p][:, :], at_c[p][:, :]).then_inc(at_ok, 1)

                aim(1, 0, 0)
                with v.Fori(0, rounds) as r:
                    with v.Fori(0, NB // 2) as j:
                        for p in range(2):
                            n = r * NB + j * 2 + p + 1
                            b = j * 2 + p
                            state_top = m.top[:, ds(b, 1), :].rearrange("p a h -> p (a h)")
                            state_den = m.den[:, ds(b, 1), :].rearrange("p a h -> p (a h)")
                            state_sum = m.agg[:, ds(b, 1), :].rearrange("p a f -> p (a f)")
                            aim(n + 1, b + 1, 1 - p)
                            step(v, nc.vector.tensor_tensor(left[p][:, :], m.deg[:, :, ds(b, 1)].rearrange("p w a -> p (w a)"),
                                                            passed_slots[:, :], ALU.subtract), left_ok, n)
                            for x in range(2):
                                nc.vector.tensor_scalar(off[p][:, x, :], m.iota_row[:, 0:SLOTS], left[p][:, x:x + 1],
                                                        NEG, ALU.is_ge, ALU.mult).then_inc(off_ok, 1)
                            v.wait_ge(off_ok, n * 2)
                            v.wait_ge(got[p], r * (NB // 2 * 32) + j * 32 + 32)
                            slots = run[p][:, :, :, :].rearrange("p x s f -> p (x s) f")
                            step(v, nc.vector.tensor_tensor(
                                score[p][:, :, :], slots[:, :, D:MSG_W],
                                off[p][:, :, :].rearrange("p x s -> p (x s)").unsqueeze(2)
                                .to_broadcast([P, 2 * SLOTS, HEADS]), ALU.add), score_ok, n)
                            step(v, nc.vector.tensor_reduce(most[p][:, :], score[p][:, :, :].rearrange("p s h -> p h s"),
                                                            X, ALU.max), most_ok, n)
                            step(v, nc.vector.tensor_tensor(top[p][:, :], most[p][:, :], state_top, ALU.max), top_ok, n)
                            nc.vector.tensor_tensor(fall[p][:, :], state_top, top[p][:, :], ALU.subtract
                                                    ).then_inc(under_ok, 1)
                            nc.vector.tensor_tensor(under[p][:, :, :], score[p][:, :, :],
                                                    top[p][:, :].unsqueeze(1).to_broadcast([P, 2 * SLOTS, HEADS]),
                                                    ALU.subtract).then_inc(under_ok, 1)
                            v.wait_ge(w_ok, n * 2)
                            nc.vector.tensor_scalar(state_top, top[p][:, :], 0.0, None, ALU.add)
                            nc.vector.tensor_reduce(wsum[p][:, :], w[p][:, :, :].rearrange("p s h -> p h s"),
                                                    X, ALU.add).then_inc(wsum_ok, 1)
                            step(v, nc.vector.tensor_tensor(den[p][:, :], state_den, corr[p][:, :], ALU.mult), den_ok, n * 2 - 1)
                            v.wait_ge(wsum_ok, n)
                            nc.vector.tensor_tensor(state_den, den[p][:, :], wsum[p][:, :], ALU.add).then_inc(den_ok, 1)
                            nc.vector.tensor_tensor(
                                prod[p][:, :, :].rearrange("p s (h f) -> p s h f", h=HEADS),
                                slots[:, :, 0:D].rearrange("p s (h f) -> p s h f", h=HEADS),
                                w[p][:, :, :].unsqueeze(3).to_broadcast([P, 2 * SLOTS, HEADS, DK]),
                                ALU.mult).then_inc(prod_ok, 1)
                            nc.vector.tensor_tensor(
                                old[p][:, :].rearrange("p (h f) -> p h f", h=HEADS),
                                state_sum.rearrange("p (h f) -> p h f", h=HEADS),
                                corr[p][:, :].unsqueeze(2).to_broadcast([P, HEADS, DK]), ALU.mult).then_inc(old_ok, 1)
                            v.wait_ge(prod_ok, n)
                            step(v, nc.vector.tensor_reduce(part[p][:, :], prod[p][:, :, :].rearrange("p s f -> p f s"),
                                                            X, ALU.add), part_ok, n)
                            v.wait_ge(old_ok, n)
                            step(v, nc.vector.tensor_tensor(state_sum, old[p][:, :], part[p][:, :], ALU.add), summed, n)
                    step(v, nc.vector.tensor_scalar(passed_slots[:, :], passed_slots[:, :], float(SLOTS), None,
                                                    ALU.add), slots_ok, r + 2)

            @block.scalar
            def _(act):
                rounds = act.value_load(m.trips[0:1, 2:3], min_val=1, max_val=EP // SLOTS + 1)
                with act.Fori(0, rounds) as r:
                    with act.Fori(0, NB // 2) as j:
                        for p in range(2):
                            n = r * NB + j * 2 + p + 1
                            act.wait_ge(under_ok, n * 2)
                            nc.scalar.activation(corr[p][:, :], fall[p][:, :], ACT.Exp, scale=SCALE).then_inc(w_ok, 1)
                            nc.scalar.activation(w[p][:, :, :], under[p][:, :, :], ACT.Exp, scale=SCALE
                                                 ).then_inc(w_ok, 1)

            @block.gpsimd
            def _(g):
                rounds = g.value_load(m.trips[0:1, 2:3], min_val=1, max_val=EP // SLOTS + 1)

                def fetch(n, p):
                    hold(g, at_ok, n, passed)
                    for x in range(2):
                        flat = d.msg_of[x].rearrange("n f -> (n f)").rearrange("(n o) -> n o", o=1)
                        g.indirect_dma_start(run[p][:, x, :, :].rearrange("p s f -> p (s f)"), None, flat,
                                             bass.IndirectOffsetOnAxis(ap=at[p][:, x:x + 1], axis=0)
                                             ).then_inc(got[p], 16)

                fetch(1, 0)
                with g.Fori(0, rounds) as r:
                    with g.Fori(0, NB // 2) as j:
                        for p in range(2):
                            fetch(r * NB + j * 2 + p + 2, 1 - p)
                g.wait_ge(got[0], rounds * (NB // 2 * 32) + 32)


def l1_out(nc, d, m):
    ctx, sb, pb, sem = scope(nc, "out")
    R = 2
    with ctx:
        wa, wb, w2, b2 = sb("wa", [P, D]), sb("wb", [P, D]), sb("w2", [P, D]), sb("b2", [P, D])
        inv = sb("inv", [P, NB, HEADS])
        x1 = [sb(f"x1{k}", [P, D]) for k in range(R)]
        emb, embT, x1T, hid, x1b, z, cent, out = ([sb(f"{x}{k}", [P, D]) for k in range(R)]
                                             for x in ("emb", "embT", "x1T", "hid", "x1b", "z", "cent", "out"))
        st = [sb(f"st{k}", [P, 6]) for k in range(R)]
        mv = [sb(f"mv{k}", [P, 2]) for k in range(R)]
        vpe, root, rinv = ([sb(f"{x}{k}", [P, 1]) for k in range(R)] for x in ("vpe", "root", "rinv"))
        ps_t = [pb(f"ps_t{k}", [P, 2, D]) for k in range(R)]
        ps_h = [pb(f"ps_h{k}", [P, D]) for k in range(R)]
        ps_y = [pb(f"ps_y{k}", [P, D]) for k in range(R)]
        (w_in, inv_ok, emb_ok, turned, copied, mm_h, hid_ok, mm_y, x1b_ok, z_ok, st_ok, mv_ok, vpe_ok, root_ok,
         rinv_ok, out_ok, passed) = (
            sem(x) for x in ("w_in", "inv_ok", "emb_ok", "turned", "copied", "mm_h", "hid_ok", "mm_y", "x1b_ok",
                             "z_ok", "st_ok", "mv_ok", "vpe_ok", "root_ok", "rinv_ok", "out_ok", "passed"))
        x1_in = [sem(f"x1_in{k}") for k in range(R)]
        stored = [sem(f"stored{k}") for k in range(R)]
        with nc.Block() as block:
            @block.sync
            def _(sp):
                sp.dma_start(wa[:, :], d.l1_w1[0:D, :]).then_inc(w_in, 16)
                sp.dma_start(wb[:, :], d.l1_w1[D:2 * D, :]).then_inc(w_in, 16)
                sp.dma_start(w2[:, :], d.l1_w2).then_inc(w_in, 16)
                sp.dma_start(b2[:, :], d.l1_b2.partition_broadcast(P)).then_inc(w_in, 16)

                def body(i):
                    for k in range(R):
                        if not first(i):
                            sp.wait_ge(x1b_ok, i * R - R + k + 1)
                            sp.wait_ge(turned, i * R - R + k + 1)
                        sp.dma_start(x1[k][:, :], d.x1[ds(i * (R * P) + k * P, P), :]).then_inc(x1_in[k], 16)
                turns(sp, NB // R, body)
                for k in range(R):
                    sp.wait_ge(stored[k], 16 * (NB // R))

            @block.tensor
            def _(pe):
                pe.wait_ge(w_in, 64)

                def body(i):
                    for k in range(R):
                        n = i * R + k + 1
                        pe.wait_ge(x1_in[k], i * 16 + 16)
                        if not first(i):
                            pe.wait_ge(copied, (n - R) * 2)
                        nc.tensor.transpose(ps_t[k][:, 1, :], x1[k][:, :], m.ident[:, :])
                        pe.wait_ge(emb_ok, n)
                        nc.tensor.transpose(ps_t[k][:, 0, :], emb[k][:, :], m.ident[:, :]).then_inc(turned, 1)
                        pe.wait_ge(copied, n * 2)
                        if not first(i):
                            pe.wait_ge(hid_ok, n - R)
                        nc.tensor.matmul(ps_h[k][:, :], wa[:, :], embT[k][:, :], start=True, stop=False)
                        nc.tensor.matmul(ps_h[k][:, :], wb[:, :], x1T[k][:, :], start=False, stop=True).then_inc(mm_h, 1)
                        pe.wait_ge(hid_ok, n)
                        if not first(i):
                            pe.wait_ge(z_ok, n - R)
                        nc.tensor.matmul(ps_y[k][:, :], hid[k][:, :], w2[:, :], start=True, stop=True).then_inc(mm_y, 1)
                turns(pe, NB // R, body)

            @block.scalar
            def _(act):
                def body(i):
                    for k in range(R):
                        n = i * R + k + 1
                        act.wait_ge(turned, n)
                        if not first(i):
                            act.wait_ge(mm_h, n - R)
                        nc.scalar.activation(embT[k][:, :], ps_t[k][:, 0, :], ACT.Copy).then_inc(copied, 1)
                        nc.scalar.activation(x1T[k][:, :], ps_t[k][:, 1, :], ACT.Copy).then_inc(copied, 1)
                        act.wait_ge(mm_h, n)
                        if not first(i):
                            act.wait_ge(mm_y, n - R)
                        nc.scalar.activation(hid[k][:, :], ps_h[k][:, :], ACT.Relu, bias=m.cols[:, 5:6]
                                             ).then_inc(hid_ok, 1)
                        act.wait_ge(vpe_ok, n)
                        nc.scalar.activation(root[k][:, :], vpe[k][:, :], ACT.Sqrt).then_inc(root_ok, 1)
                        act.wait_ge(out_ok, n)
                        act.dma_start(d.out[ds((n - 1) * P, P), :], out[k][:, :]).then_inc(stored[k], 16)
                turns(act, NB // R, body)

            @block.vector
            def _(v):
                v.wait_ge(w_in, 64)
                step(v, nc.vector.reciprocal(inv[:, :, :], m.den[:, :, :]), inv_ok, 1)

                def embed(i, k, n):
                    nc.vector.tensor_tensor(
                        emb[k][:, :].rearrange("p (h f) -> p h f", h=HEADS),
                        m.agg[:, ds(n - 1, 1), :].rearrange("p a (h f) -> p (a h) f", h=HEADS),
                        inv[:, ds(n - 1, 1), :].rearrange("p a h -> p (a h)").unsqueeze(2)
                        .to_broadcast([P, HEADS, DK]), ALU.mult).then_inc(emb_ok, 1)

                def body(i):
                    for k in range(R):
                        n = i * R + k + 1
                        if not first(i):
                            v.wait_ge(turned, n - R)
                        embed(i, k, n)
                        v.wait_ge(x1_in[k], i * 16 + 16)
                        step(v, nc.vector.tensor_tensor(x1b[k][:, :], x1[k][:, :], b2[:, :], ALU.add), x1b_ok, n)
                        v.wait_ge(mm_y, n)
                        step(v, nc.vector.tensor_tensor(z[k][:, :], x1b[k][:, :], ps_y[k][:, :], ALU.add), z_ok, n)
                        nc.vector.bn_stats(st[k][:, :], z[k][:, :]).then_inc(st_ok, 1)
                        hold(v, st_ok, n, passed)
                        step(v, nc.vector.bn_aggr(mv[k][:, :], st[k][:, :]), mv_ok, n)
                        nc.vector.tensor_scalar(vpe[k][:, :], mv[k][:, 1:2], EPS, None, ALU.add).then_inc(vpe_ok, 1)
                        v.wait_ge(root_ok, n)
                        if not first(i):
                            v.wait_ge(stored[k], i * 16)
                        step(v, nc.vector.reciprocal(rinv[k][:, :], root[k][:, :]), rinv_ok, n)
                        nc.vector.tensor_scalar(out[k][:, :], z[k][:, :], mv[k][:, 0:1], rinv[k][:, 0:1], ALU.subtract,
                                                ALU.mult).then_inc(out_ok, 1)
                turns(v, NB // R, body)


def build(nc, d):
    ctx = ExitStack()
    with ctx:
        def keep(name, shape, dt=f32):
            return ctx.enter_context(nc.sbuf_tensor(name, shape, dt))
        m = Names()
        m.iota_row, m.iota_p, m.ones = keep("iota_row", [P, P]), keep("iota_p", [P, 1]), keep("ones", [P, P])
        m.ident, m.before, m.after = keep("ident", [P, P]), keep("before", [P, P]), keep("after", [P, P])
        m.real, m.cols = keep("real", [P, NB]), keep("cols", [P, 6])
        m.w2t, m.w2ts, m.row2 = keep("w2t", [P, D]), keep("w2ts", [P, D]), keep("row2", [1, D])
        m.selfadd = keep("selfadd", [P, 3 * D])
        m.key, m.lo, m.hi = (keep(x, [P, 2, EP // P]) for x in ("key", "lo", "hi"))
        m.rank, m.where_t = keep("rank", [P, 2, EP // P]), keep("where_t", [P, EP // P])
        m.count, m.deg, m.place = keep("count", [P, 2, NB]), keep("deg", [P, 2, NB]), keep("place", [P, NB + 1, 2])
        m.visits, m.trips = keep("visits", [P, 3], i32), keep("trips", [P, 3], i32)
        m.mv1, m.mv2 = keep("mv1", [P, 2]), keep("mv2", [P, 2])
        m.scale1, m.shift1 = keep("scale1", [P, 1]), keep("shift1", [P, 1])
        m.scale2, m.shift2 = keep("scale2", [P, 1]), keep("shift2", [P, 1])
        m.agg, m.top, m.den = keep("agg", [P, NB, D]), keep("top", [P, NB, HEADS]), keep("den", [P, NB, HEADS])
        setup(nc, d, m)
        rank(nc, d, m, 0, "rank_s")
        rank(nc, d, m, 1, "rank_t")
        places(nc, d, m)
        l0_tables(nc, d, m)
        l0_first(nc, d, m)
        norm_terms(nc, m, m.mv1, m.cols[:, 0:1], m.cols[:, 1:2], m.scale1, m.shift1, "norm_a")
        l0_second(nc, d, m)
        norm_terms(nc, m, m.mv2, m.cols[:, 2:3], m.cols[:, 3:4], m.scale2, m.shift2, "norm_b")
        fold_second(nc, d, m)
        l0_third(nc, d, m)
        l0_gather(nc, d, m)
        layer_norm(nc, d, m)
        l1_self_terms(nc, d, m)
        l1_tables(nc, d, m)
        l1_edges(nc, d, m)
        l1_softmax(nc, d, m)
        l1_out(nc, d, m)


def kernel(**inputs):
    import numpy as np
    import concourse.bacc as bacc
    from concourse.bass_utils import run_bass_kernel_spmd

    a = {k: np.asarray(v) for k, v in inputs.items()}

    def rows_to(x, n, fill=0):
        return np.concatenate([x, np.full((n - x.shape[0],) + x.shape[1:], fill, x.dtype)])

    x = rows_to(a["x"], NP_)
    src, dst = rows_to(a["src"], EP, PAD), rows_to(a["dst"], EP, PAD)
    by_chunk = [k.reshape(-1, P).T for k in (src, dst)]
    ef, tf, et = (rows_to(a[k], EP).T for k in ("edge_attr_64", "edge_attr_64_n2", "edge_attr_64_n3"))
    w1 = a["L0_gnn_W1"]
    wq, wk, wv = a["L1_gnn_Wq"], a["L1_gnn_Wk"], a["L1_gnn_Wv"]
    nc = bacc.Bacc("TRN2", target_bir_lowering=False, num_devices=1)
    arrays = {}

    def given(name, v):
        arrays[name] = np.ascontiguousarray(v)
        return nc.dram_tensor(name, v.shape, mybir.dt.from_np(v.dtype), kind="ExternalInput").ap()

    def scratch(name, *shape):
        return nc.dram_tensor(name, shape, f32, kind="Internal").ap()

    d = Names()
    d.x, d.xT = given("in_x", x), given("in_xT", x.T)
    d.idx = given("in_idx", np.concatenate([k.reshape(GROUPS, CG, P).transpose(0, 2, 1) for k in (src, dst)], axis=2))
    d.keys = given("in_keys", np.stack(by_chunk, axis=1))
    d.key_rows = given("in_key_rows", np.stack([k.reshape(P, -1) for k in (src, dst)], axis=1))
    d.ft, d.fe = given("in_ft", tf), given("in_fe", np.concatenate([ef, et]))
    d.time0 = given("in_time0", a["edge_attr_64_n2"][0:1].T)
    d.w1 = given("in_w1", np.concatenate([w1[:, :D].T, w1[:, D:].T], axis=1))
    d.b1 = given("in_b1", a["L0_gnn_b1"])
    d.w2, d.w2t = given("in_w2", a["L0_gnn_W2"]), given("in_w2t", a["L0_gnn_W2"].T)
    d.cols = given("in_cols", np.stack([a[k] for k in ("L0_gnn_g1", "L0_gnn_be1", "L0_gnn_g2", "L0_gnn_be2",
                                                       "L0_gnn_b2", "L1_gnn_b1")], axis=1))
    d.wx = given("in_wx", np.concatenate([w[:D] for w in (wq, wk, wv)], axis=1))
    d.bx = given("in_bx", np.concatenate([a[k] for k in ("L1_gnn_bq", "L1_gnn_bk", "L1_gnn_bv")]))
    d.wt, d.we = given("in_wt", wq[D:]), given("in_we", np.concatenate([wk[D:], wv[D:]], axis=1))
    d.l1_w1, d.l1_w2 = given("in_l1_w1", a["L1_gnn_W1"]), given("in_l1_w2", a["L1_gnn_W2"])
    d.l1_b2 = given("in_l1_b2", a["L1_gnn_b2"])
    d.ta, d.tb, d.tn = scratch("ta", NP_, D), scratch("tb", NP_, TB_W), scratch("tn", NP_, TN_W)
    d.rowf, d.h1, d.up, d.x1 = scratch("rowf", 2, 2, EP), scratch("h1", D, EP), scratch("up", EP + SLOTS, D), scratch("x1", NP_, D)
    d.msg_of = [scratch("msg_s", EP + SLOTS, MSG_W), scratch("msg_t", EP + SLOTS, MSG_W)]
    d.out = nc.dram_tensor("out", (NP_, D), f32, kind="ExternalOutput").ap()
    build(nc, d)
    r = run_bass_kernel_spmd(nc, [arrays], core_ids=[0])
    return r.results[0]["out"][:N]
```

```python
import math
from contextlib import ExitStack

import concourse.bass as bass
from concourse import mybir

P = 128
N, E, D, DE = 6250, 100000, 128, 64
HEADS = 2
DK = D // HEADS
SCALE = DK ** -0.5
EPS = 1e-5
CG = 4
GE = CG * P
GROUPS = 4 * -(-E // (4 * GE))
EP = GROUPS * GE
LAST = E - (GROUPS - 1) * GE
NB = 2 * -(-(N + 1) // (2 * P))
NP_ = NB * P
SLOTS = 16
SOFT_RING, AHEAD = 5, 3
PAD = N
TB_W = D + 1
TN_W = 3 * D + 2
MSG_W = D + HEADS
NEG = -1.0e30
BANK = 512

f32, bf16, i32, u16 = mybir.dt.float32, mybir.dt.bfloat16, mybir.dt.int32, mybir.dt.uint16
ALU = mybir.AluOpType
ACT = mybir.ActivationFunctionType
X = mybir.AxisListType.X
ds = bass.ds


class Names:
    pass


def turns(eng, count, body):
    body(0)
    if count > 1:
        with eng.Fori(1, count) as i:
            body(i)


def first(i):
    return isinstance(i, int) and i == 0


def step(eng, ins, sem, count):
    ins.then_inc(sem, 1)
    eng.wait_ge(sem, count)


def real_part(columns):
    return columns.rearrange("f (c p) -> f c p", c=CG)[:, :, 0:LAST // CG]


def hold(eng, sem, value, passed):
    eng.wait_ge(sem, value)
    eng.sem_inc(passed, 1)


def scope(nc, tag):
    ctx = ExitStack()

    def sb(name, shape, dt=f32):
        return ctx.enter_context(nc.sbuf_tensor(f"{tag}_{name}", shape, dt))

    def pb(name, shape):
        size = math.prod(shape[1:])
        whole = ctx.enter_context(nc.psum_tensor(f"{tag}_{name}", [shape[0], -(-size // BANK) * BANK], f32))
        if len(shape) == 2:
            return whole[:, 0:size]
        return whole[:, 0:size].rearrange("p (a b) -> p a b", b=shape[2])

    sems = []

    def sem(name):
        sems.append(nc.alloc_semaphore(f"{tag}_{name}"))
        return sems[-1]

    ctx.callback(nc.all_engine_barrier)
    ctx.callback(lambda: nc.clear_and_free_semaphores(sems))
    return ctx, sb, pb, sem


def setup(nc, d, m):
    ctx, sb, pb, sem = scope(nc, "setup")
    with ctx:
        keys, lows, highs = (sb(x, [P, 2, EP // P], i32) for x in ("keys", "lows", "highs"))
        rows, row_lows = (sb(x, [P, 2, EP // P], i32) for x in ("rows", "row_lows"))
        rowf = sb("rowf", [P, 2, 2, EP // P], u16)
        now, then = sb("now", [P, EP // P], i32), sb("then", [P, EP // P], i32)
        ends = sb("ends", [P, 2, GROUPS], i32)
        falls, span, wide = sb("falls", [P, EP // P]), sb("span", [P, GROUPS]), sb("wide", [P, GROUPS])
        bad, bad2, bad_all = (sb(x, [P, 1]) for x in ("bad", "bad2", "bad_all"))
        w_in, k_in, o_in, zeroed, split, rowf_ok, rowf_out, made, chain, bad_ok, bad_all_ok = (
            sem(x) for x in ("w_in", "k_in", "o_in", "zeroed", "split", "rowf_ok", "rowf_out", "made", "chain",
                             "bad_ok", "bad_all_ok"))
        with nc.Block() as block:
            @block.sync
            def _(sp):
                sp.dma_start(keys[:, :, :], d.keys).then_inc(k_in, 16)
                sp.dma_start(rows[:, :, :], d.key_rows).then_inc(k_in, 16)
                sp.dma_start(now[:, :], d.now).then_inc(o_in, 16)
                sp.dma_start(then[:, :], d.then).then_inc(o_in, 16)
                sp.dma_start(ends[:, :, :], d.ends.partition_broadcast(P)).then_inc(o_in, 16)
                sp.dma_start(m.bases[:, :], d.ends[0:1, :]).then_inc(w_in, 16)
                sp.dma_start(m.cols[:, :], d.cols).then_inc(w_in, 16)
                sp.dma_start(m.w2t[:, :], d.w2t).then_inc(w_in, 16)
                sp.wait_ge(w_in, 48)

            @block.gpsimd
            def _(g):
                g.iota(m.iota_row[:, :], [[1, P]], base=0, channel_multiplier=0,
                       allow_small_or_imprecise_dtypes=True)
                g.iota(m.iota_p[:, :], [[0, 1]], base=0, channel_multiplier=1,
                       allow_small_or_imprecise_dtypes=True).then_inc(made, 1)
                g.memset(m.ones[:, :], 1.0)
                for t in (m.ident, m.before, m.after):
                    g.memset(t[:, :], 0.0).then_inc(zeroed, 1)
                g.memset(m.real[:, :], 1.0).then_inc(zeroed, 1)
                g.wait_ge(zeroed, 4)
                g.affine_select(out=m.ident[:, :], in_=m.ident[:, :], compare_op=ALU.not_equal, fill=1.0,
                                base=0, pattern=[[-1, P]], channel_multiplier=1)
                g.affine_select(out=m.before[:, :], in_=m.before[:, :], compare_op=ALU.is_ge, fill=1.0,
                                base=0, pattern=[[1, P]], channel_multiplier=-1)
                g.affine_select(out=m.after[:, :], in_=m.after[:, :], compare_op=ALU.is_ge, fill=1.0,
                                base=0, pattern=[[-1, P]], channel_multiplier=1)
                g.affine_select(out=m.real[:, :], in_=m.real[:, :], compare_op=ALU.is_ge, fill=0.0,
                                base=N - 1, pattern=[[-P, NB]], channel_multiplier=-1)
                g.wait_ge(bad_ok, 1)
                g.partition_all_reduce(bad_all[:, :], bad[:, :], P, bass.bass_isa.ReduceOp.add
                                       ).then_inc(bad_all_ok, 1)

            @block.vector
            def _(v):
                v.wait_ge(k_in, 32)
                nc.vector.tensor_scalar(lows[:, :, :], keys[:, :, :], P - 1, None, ALU.bitwise_and).then_inc(split, 1)
                nc.vector.tensor_scalar(highs[:, :, :], keys[:, :, :], P.bit_length() - 1, None,
                                        ALU.arith_shift_right).then_inc(split, 1)
                nc.vector.tensor_scalar(row_lows[:, :, :], rows[:, :, :], P - 1, None,
                                        ALU.bitwise_and).then_inc(split, 1)
                nc.vector.tensor_copy(m.key[:, :, :], keys[:, :, :])
                nc.vector.tensor_copy(rowf[:, :, 0, :], rows[:, :, :]).then_inc(rowf_ok, 1)
                v.wait_ge(split, 3)
                nc.vector.tensor_copy(m.lo[:, :, :], lows[:, :, :])
                nc.vector.tensor_copy(m.hi[:, :, :], highs[:, :, :])
                nc.vector.tensor_copy(rowf[:, :, 1, :], row_lows[:, :, :]).then_inc(rowf_ok, 1)
                nc.vector.memset(m.visits[:, :], SLOTS)
                v.wait_ge(o_in, 48)
                step(v, nc.vector.tensor_tensor(falls[:, :], now[:, :], then[:, :], ALU.is_gt), chain, 1)
                step(v, nc.vector.tensor_reduce(bad[:, :], falls[:, :], X, ALU.add), chain, 2)
                step(v, nc.vector.tensor_tensor(span[:, :], ends[:, 1, :], ends[:, 0, :], ALU.subtract), chain, 3)
                step(v, nc.vector.tensor_scalar(wide[:, :], span[:, :], float(P), None, ALU.is_ge), chain, 4)
                step(v, nc.vector.tensor_reduce(bad2[:, :], wide[:, :], X, ALU.add), chain, 5)
                nc.vector.tensor_tensor(bad[:, :], bad[:, :], bad2[:, :], ALU.add).then_inc(bad_ok, 1)
                v.wait_ge(made, 1)
                step(v, nc.vector.tensor_copy(m.window[:, :], ends[:, 0, :]), chain, 6)
                nc.vector.tensor_tensor(m.inside[:, :].rearrange("p (g c) -> p g c", c=CG),
                                        m.key[:, 1, :].rearrange("p (g c) -> p g c", c=CG),
                                        m.window[:, :].unsqueeze(2).to_broadcast([P, GROUPS, CG]),
                                        ALU.subtract).then_inc(chain, 1)
                v.wait_ge(chain, 7)
                nc.vector.tensor_scalar(m.window[:, :], m.window[:, :], m.iota_p[:, 0:1], None, ALU.add)
                v.wait_ge(bad_all_ok, 1)
                nc.vector.tensor_scalar(m.ordered[:, :], bad_all[:, :], 0.0, None, ALU.is_equal)

            @block.scalar
            def _(act):
                act.wait_ge(rowf_ok, 2)
                act.dma_start(d.rowf.rearrange("w t (p j) -> p w t j", p=P), rowf[:, :, :, :]).then_inc(rowf_out, 16)
                act.wait_ge(rowf_out, 16)


def l0_tables(nc, d, m, placed, tag):
    ctx, sb, pb, sem = scope(nc, tag)
    W = TB_W if placed else D
    S = 3 if placed else 2
    R = 5
    with ctx:
        w = sb("w", [P, 2 * D])
        b1 = sb("b1", [P, D])
        xt = [sb(f"xt{k}", [P, P]) for k in range(R)]
        tab = [sb(f"tab{k}", [P, D + TB_W]) for k in range(R)]
        ps = [pb(f"ps{k}", [P, 2 * D]) for k in range(R)]
        w_in, mm, tab_ok = (sem(x) for x in ("w_in", "mm", "tab_ok"))
        xt_in = [sem(f"xt_in{k}") for k in range(R)]
        tab_out = [sem(f"tab_out{k}") for k in range(R)]
        with nc.Block() as block:
            @block.sync
            def _(sp):
                sp.dma_start(w[:, :], d.w1).then_inc(w_in, 16)
                sp.dma_start(b1[:, :], d.b1.partition_broadcast(P)).then_inc(w_in, 16)

                def body(i):
                    for k in range(R):
                        if not first(i):
                            sp.wait_ge(mm, i * R - R + k + 1)
                        sp.dma_start(xt[k][:, :], d.xT[:, ds(i * (R * P) + k * P, P)]).then_inc(xt_in[k], 16)
                turns(sp, NB // R, body)

            @block.tensor
            def _(pe):
                pe.wait_ge(w_in, 32)

                def body(i):
                    for k in range(R):
                        pe.wait_ge(xt_in[k], i * 16 + 16)
                        if not first(i):
                            pe.wait_ge(tab_ok, i * (S * R) - S * R + S * k + S)
                        nc.tensor.matmul(ps[k][:, :], xt[k][:, :], w[:, :], start=True, stop=True).then_inc(mm, 1)
                turns(pe, NB // R, body)

            @block.vector
            def _(v):
                v.wait_ge(w_in, 32)

                def body(i):
                    for k in range(R):
                        v.wait_ge(mm, i * R + k + 1)
                        if not first(i):
                            v.wait_ge(tab_out[k], i * 32)
                        nc.vector.tensor_tensor(tab[k][:, 0:D], ps[k][:, 0:D], b1[:, :], ALU.add).then_inc(tab_ok, 1)
                        nc.vector.tensor_scalar(tab[k][:, D:2 * D], ps[k][:, D:2 * D], 0.0, None,
                                                ALU.add).then_inc(tab_ok, 1)
                        if placed:
                            nc.vector.tensor_scalar(tab[k][:, 2 * D:2 * D + 1], m.place[:, ds(i * R + k, 1), 1], 0.0,
                                                    None, ALU.add).then_inc(tab_ok, 1)
                turns(v, NB // R, body)

            @block.gpsimd
            def _(g):
                g.nop()

            @block.scalar
            def _(act):
                def body(i):
                    for k in range(R):
                        act.wait_ge(tab_ok, i * (S * R) + S * k + S)
                        row = ds(i * (R * P) + k * P, P)
                        act.dma_start(d.ta[row, :], tab[k][:, 0:D]).then_inc(tab_out[k], 16)
                        act.dma_start(d.tb[row, 0:W], tab[k][:, D:D + W]).then_inc(tab_out[k], 16)
                turns(act, NB // R, body)
                for k in range(R):
                    act.wait_ge(tab_out[k], 32 * (NB // R))


class Ranks:
    pass


def ranks(nc, d, m, which, sb, pb, sem):
    keyrow = [sb(f"keyrow{p}", [P, 2, GE], u16) for p in range(2)]
    ohl = [sb(f"ohl{p}", [P, CG, P], bf16) for p in range(2)]
    ohh = [sb(f"ohh{p}", [P, CG, NB], bf16) for p in range(2)]
    ohT = [sb(f"ohT{p}", [P, GE]) for p in range(2)]
    same = [sb(f"same{c}", [P, P], bf16) for c in range(CG)]
    inside = [sb(f"inside{p}", [P, CG]) for p in range(2)]
    table = [sb(f"table{p}", [P, CG, NB]) for p in range(2)]
    hit = [sb(f"hit{p}", [P, CG, NB]) for p in range(2)]
    found = [sb(f"found{p}", [P, CG]) for p in range(2)]
    ps_n = [pb(f"ps_n{p}", [P, CG, NB]) for p in range(2)]
    ps_t = [pb(f"ps_t{p}", [P, CG, NB]) for p in range(2)]
    row_in = [sem(f"row_in{p}") for p in range(2)]
    onehot, compared, counted, stepped, looked, hit_ok, found_ok, ranked, zeroed, passed_sp = (
        sem(x) for x in ("onehot", "compared", "counted", "stepped", "looked", "hit_ok", "found_ok",
                         "ranked", "zeroed", "ranks_passed_sp"))

    def load(sp, i, p):
        if not first(i):
            hold(sp, ranked, i * 2 + p - 1, passed_sp)
        sp.dma_start(keyrow[p][:, :, :],
                     d.rowf[which, :, ds(i * (2 * GE) + p * GE, GE)].partition_broadcast(P)).then_inc(row_in[p], 16)

    def start(v):
        step(v, nc.vector.memset(table[0][:, 0, :], 0.0), zeroed, 1)

    def finish(v, n, p, col):
        v.wait_ge(looked, n)
        step(v, nc.vector.tensor_tensor(hit[p][:, :, :], ps_t[p][:, :, :], ohh[p][:, :, :], ALU.mult), hit_ok, n)
        step(v, nc.vector.tensor_reduce(found[p][:, :], hit[p][:, :, :], X, ALU.add), found_ok, n)
        v.wait_ge(compared, n * CG)
        nc.vector.tensor_tensor(m.rank[:, which, col], found[p][:, :], inside[p][:, :], ALU.add).then_inc(ranked, 1)

    def compare(v, i, p):
        g = i * 2 + p
        at = i * (2 * CG) + p * CG
        v.wait_ge(row_in[p], i * 16 + 16)
        lo = m.lo[:, which, ds(at, CG)].unsqueeze(2).to_broadcast([P, CG, P])
        hi = m.hi[:, which, ds(at, CG)].unsqueeze(2).to_broadcast([P, CG, NB])
        nc.vector.tensor_tensor(ohl[p][:, :, :], m.iota_row[:, :].unsqueeze(1).to_broadcast([P, CG, P]),
                                lo, ALU.is_equal)
        nc.vector.tensor_tensor(ohh[p][:, :, :], m.iota_row[:, 0:NB].unsqueeze(1).to_broadcast([P, CG, NB]),
                                hi, ALU.is_equal)
        nc.vector.tensor_scalar(ohT[p][:, :], keyrow[p][:, 1, :], m.iota_p[:, 0:1], None,
                                ALU.is_equal).then_inc(onehot, 1)
        for c in range(CG):
            nc.vector.scalar_tensor_tensor(same[c][:, :], keyrow[p][:, 0, c * P:(c + 1) * P],
                                           m.key[:, which, ds(at + c, 1)], m.before[:, :], ALU.is_equal, ALU.mult,
                                           accum_out=inside[p][:, c:c + 1]).then_inc(compared, 1)
        if not (first(i) and p == 0):
            finish(v, g, 1 - p, ds(at - CG, CG))
        v.wait_ge(counted, g + 1)
        for c in range(CG):
            to = table[p][:, c + 1, :] if c + 1 < CG else table[1 - p][:, 0, :]
            step(v, nc.vector.tensor_tensor(to, table[p][:, c, :], ps_n[p][:, c, :], ALU.add),
                 stepped, g * CG + c + 1)

    def end(v):
        finish(v, GROUPS, 1, ds((GROUPS - 1) * CG, CG))
        nc.vector.tensor_tensor(m.deg[:, which, 0:NB], table[0][:, 0, :], m.real[:, :], ALU.mult)
        nc.vector.tensor_copy(m.count[:, which, :], table[0][:, 0, :])

    def count(pe, i, p):
        g = i * 2 + p
        pe.wait_ge(onehot, g + 1)
        for c in range(CG):
            last = nc.tensor.matmul(ps_n[p][:, c, :], ohl[p][:, c, :], ohh[p][:, c, :], start=True, stop=True)
        last.then_inc(counted, 1)
        pe.wait_ge(stepped, g * CG + CG)
        for c in range(CG):
            last = nc.tensor.matmul(ps_t[p][:, c, :], ohT[p][:, c * P:(c + 1) * P], table[p][:, c, :],
                                    start=True, stop=True)
        last.then_inc(looked, 1)

    r = Ranks()
    r.load, r.start, r.compare, r.end, r.count = load, start, compare, end, count
    return r


def rank_targets(nc, d, m):
    ctx, sb, pb, sem = scope(nc, "rank_t")
    with ctx:
        r = ranks(nc, d, m, 1, sb, pb, sem)
        with nc.Block() as block:
            @block.sync
            def _(sp):
                def body(i):
                    for p in range(2):
                        r.load(sp, i, p)
                turns(sp, GROUPS // 2, body)

            @block.gpsimd
            def _(g):
                g.nop()

            @block.scalar
            def _(act):
                act.nop()

            @block.vector
            def _(v):
                r.start(v)

                def body(i):
                    for p in range(2):
                        r.compare(v, i, p)
                turns(v, GROUPS // 2, body)
                r.end(v)

            @block.tensor
            def _(pe):
                def body(i):
                    for p in range(2):
                        r.count(pe, i, p)
                turns(pe, GROUPS // 2, body)


def places(nc, d, m, w, tag):
    ctx, sb, pb, sem = scope(nc, tag)
    with ctx:
        total = sb("total", [NB, P])
        most, most_all, room = (sb(x, [P, 1]) for x in ("most", "most_all", "room"))
        ps_t, ps_o = pb("ps_t", [NB, P]), pb("ps_o", [P, NB])
        summed, total_ok, placed, most_ok, most_all_ok, chain = (
            sem(x) for x in ("summed", "total_ok", "placed", "most_ok", "most_all_ok", "chain"))
        with nc.Block() as block:
            @block.sync
            def _(sp):
                sp.nop()

            @block.scalar
            def _(act):
                act.nop()

            @block.tensor
            def _(pe):
                nc.tensor.matmul(ps_t[:, :], m.count[:, w, :], m.ones[:, :], start=True, stop=True).then_inc(summed, 1)
                pe.wait_ge(total_ok, 1)
                nc.tensor.matmul(ps_o[:, :], m.after[:, :], m.count[:, w, :], start=True, stop=False)
                nc.tensor.matmul(ps_o[:, :], total[:, :], m.after[0:NB, 0:NB], start=False,
                                 stop=True).then_inc(placed, 1)

            @block.vector
            def _(v):
                v.wait_ge(summed, 1)
                nc.vector.tensor_copy(total[:, :], ps_t[:, :]).then_inc(total_ok, 1)
                nc.vector.tensor_reduce(most[:, :], m.deg[:, w, 0:NB], X, ALU.max).then_inc(most_ok, 1)
                v.wait_ge(placed, 1)
                step(v, nc.vector.tensor_copy(m.place[:, 0:NB, w], ps_o[:, :]), chain, 1)
                step(v, nc.vector.tensor_scalar(m.place[:, NB:NB + AHEAD, w], m.place[:, 0:AHEAD, w], float(SLOTS),
                                                None, ALU.add), chain, 2)
                v.wait_ge(most_all_ok, 1)
                step(v, nc.vector.tensor_scalar(room[:, :], most_all[:, :], float(SLOTS - 1), float(SLOTS),
                                                ALU.add, ALU.max), chain, 3)
                step(v, nc.vector.tensor_copy(m.visits[:, w:w + 1], room[:, :]), chain, 4)
                step(v, nc.vector.tensor_tensor(m.visits[:, 2:3], m.visits[:, 0:1], m.visits[:, 1:2],
                                                ALU.max), chain, 5)
                nc.vector.tensor_scalar(m.trips[:, :], m.visits[:, :], SLOTS.bit_length() - 1, None,
                                        ALU.arith_shift_right)

            @block.gpsimd
            def _(g):
                g.wait_ge(most_ok, 1)
                g.partition_all_reduce(most_all[:, :], most[:, :], P, bass.bass_isa.ReduceOp.max
                                       ).then_inc(most_all_ok, 1)


def l0_first(nc, d, m):
    ctx, sb, pb, sem = scope(nc, "first")
    with ctx:
        r = ranks(nc, d, m, 0, sb, pb, sem)
        idx = [sb(f"idx{p}", [P, 2 * CG], i32) for p in range(2)]
        gs = [sb(f"gs{p}", [P, CG, D]) for p in range(2)]
        gt = [sb(f"gt{p}", [P, CG, TB_W]) for p in range(2)]
        hsum = [sb(f"hsum{p}", [P, CG, D]) for p in range(2)]
        h1 = [sb(f"h1{p}", [P, GE]) for p in range(2)]
        stats = sb("stats", [P, GROUPS, 6])
        ps = [pb(f"ps{p}", [P, GE]) for p in range(2)]
        idx_in = [sem(f"idx_in{p}") for p in range(2)]
        got = [sem(f"got{p}") for p in range(2)]
        stored = [sem(f"stored{p}") for p in range(2)]
        added, turned, copied, measured, passed, passed_act, stats_ok = (
            sem(x) for x in ("added", "turned", "copied", "measured", "passed", "passed_act", "stats_ok"))
        with nc.Block() as block:
            @block.sync
            def _(sp):
                def body(i):
                    for p in range(2):
                        if not first(i):
                            sp.wait_ge(got[p], i * (2 * CG * 16))
                        sp.dma_start(idx[p][:, :], d.idx[ds(i * 2 + p, 1), :, :].rearrange("a p c -> (a p) c")
                                     ).then_inc(idx_in[p], 16)
                        r.load(sp, i, p)
                turns(sp, GROUPS // 2, body)

            @block.gpsimd
            def _(g):
                def body(i):
                    for p in range(2):
                        hold(g, idx_in[p], i * 16 + 16, passed)
                        if not first(i):
                            hold(g, added, i * 2 + p - 1, passed)
                        for c in range(CG):
                            g.indirect_dma_start(gs[p][:, c, :], None, d.ta,
                                                 bass.IndirectOffsetOnAxis(ap=idx[p][:, c:c + 1], axis=0)
                                                 ).then_inc(got[p], 16)
                            g.indirect_dma_start(gt[p][:, c, :], None, d.tb,
                                                 bass.IndirectOffsetOnAxis(ap=idx[p][:, CG + c:CG + c + 1], axis=0)
                                                 ).then_inc(got[p], 16)
                turns(g, GROUPS // 2, body)

            @block.vector
            def _(v):
                r.start(v)

                def body(i):
                    for p in range(2):
                        v.wait_ge(got[p], (i + 1) * (2 * CG * 16))
                        if not first(i):
                            v.wait_ge(turned, i * 2 + p - 1)
                        at = ds(i * (2 * CG) + p * CG, CG)
                        nc.vector.tensor_tensor(m.where_t[:, at], m.rank[:, 1, at], gt[p][:, :, D], ALU.add)
                        nc.vector.tensor_tensor(hsum[p][:, :, :], gs[p][:, :, :], gt[p][:, :, 0:D],
                                                ALU.add).then_inc(added, 1)
                        r.compare(v, i, p)
                        hold(v, copied, i * 2 + p + 1, passed)
                        nc.vector.bn_stats(stats[:, ds(i * 2 + p, 1), :].rearrange("p a s -> p (a s)"),
                                           h1[p][:, :]).then_inc(measured, 1)
                turns(v, GROUPS // 2, body)
                v.wait_ge(measured, GROUPS)
                nc.vector.bn_stats(stats[:, GROUPS - 1, :], real_part(h1[1][:, :])).then_inc(stats_ok, 1)
                v.wait_ge(stats_ok, 1)
                nc.vector.bn_aggr(m.mv1[:, :], stats[:, :, :].rearrange("p g s -> p (g s)"))
                r.end(v)

            @block.tensor
            def _(pe):
                def body(i):
                    for p in range(2):
                        pe.wait_ge(added, i * 2 + p + 1)
                        if not first(i):
                            pe.wait_ge(copied, i * 2 + p - 1)
                        for c in range(CG):
                            last = nc.tensor.transpose(ps[p][:, c * P:(c + 1) * P], hsum[p][:, c, :], m.ident[:, :])
                        last.then_inc(turned, 1)
                        r.count(pe, i, p)
                turns(pe, GROUPS // 2, body)

            @block.scalar
            def _(act):
                def body(i):
                    for p in range(2):
                        hold(act, turned, i * 2 + p + 1, passed_act)
                        if not first(i):
                            act.wait_ge(stored[p], i * 16)
                            hold(act, measured, i * 2 + p - 1, passed_act)
                        nc.scalar.activation(h1[p][:, :], ps[p][:, :], ACT.Copy).then_inc(copied, 1)
                        act.wait_ge(copied, i * 2 + p + 1)
                        act.dma_start(d.h1[:, ds(i * (2 * GE) + p * GE, GE)], h1[p][:, :]).then_inc(stored[p], 16)
                turns(act, GROUPS // 2, body)
                for p in range(2):
                    act.wait_ge(stored[p], 16 * (GROUPS // 2))


def l0_first_ordered(nc, d, m):
    ctx, sb, pb, sem = scope(nc, "firsto")
    with ctx:
        r = ranks(nc, d, m, 0, sb, pb, sem)
        idx = [sb(f"idx{p}", [P, CG], i32) for p in range(2)]
        gs = [sb(f"gs{p}", [P, CG, D]) for p in range(2)]
        win = [sb(f"win{p}", [P, D]) for p in range(2)]
        target = [sb(f"target{p}", [P, GE], u16) for p in range(2)]
        pick = [sb(f"pick{p}", [P, GE]) for p in range(2)]
        h1 = [sb(f"h1{p}", [P, GE]) for p in range(2)]
        stats = sb("stats", [P, GROUPS, 6])
        ps = [pb(f"ps{p}", [P, GE]) for p in range(2)]
        idx_in, got, stored, win_in, target_in = (
            [sem(f"{x}{p}") for p in range(2)] for x in ("idx_in", "got", "stored", "win_in", "target_in"))
        picked, summed, copied, measured, passed, passed_act, passed_sp, stats_ok = (
            sem(x) for x in ("picked", "summed", "copied", "measured", "passed", "passed_act", "passed_sp",
                             "stats_ok"))
        with nc.Block() as block:
            @block.sync
            def _(sp):
                def body(i):
                    for p in range(2):
                        if not first(i):
                            sp.wait_ge(got[p], i * (CG * 16))
                        sp.dma_start(idx[p][:, :], d.idx[ds(i * 2 + p, 1), :, 0:CG].rearrange("a p c -> (a p) c")
                                     ).then_inc(idx_in[p], 16)
                        if not first(i):
                            sp.wait_ge(picked, i * 2 + p - 1)
                        sp.dma_start(target[p][:, :],
                                     d.rowf[1, 0, ds(i * (2 * GE) + p * GE, GE)].partition_broadcast(P)
                                     ).then_inc(target_in[p], 16)
                        r.load(sp, i, p)
                        if not first(i):
                            hold(sp, summed, i * 2 + p - 1, passed_sp)
                        base = sp.value_load(m.bases[0:1, ds(i * 2 + p, 1)], min_val=0, max_val=N)
                        sp.dma_start(win[p][:, :], d.tb[ds(base, P), 0:D]).then_inc(win_in[p], 16)
                turns(sp, GROUPS // 2, body)

            @block.gpsimd
            def _(g):
                def body(i):
                    for p in range(2):
                        hold(g, idx_in[p], i * 16 + 16, passed)
                        if not first(i):
                            hold(g, summed, i * 2 + p - 1, passed)
                        for c in range(CG):
                            g.indirect_dma_start(gs[p][:, c, :], None, d.ta,
                                                 bass.IndirectOffsetOnAxis(ap=idx[p][:, c:c + 1], axis=0)
                                                 ).then_inc(got[p], 16)
                turns(g, GROUPS // 2, body)

            @block.vector
            def _(v):
                r.start(v)

                def body(i):
                    for p in range(2):
                        v.wait_ge(target_in[p], i * 16 + 16)
                        if not first(i):
                            v.wait_ge(summed, i * 2 + p - 1)
                        nc.vector.tensor_scalar(pick[p][:, :], target[p][:, :], m.window[:, ds(i * 2 + p, 1)], None,
                                                ALU.is_equal).then_inc(picked, 1)
                        r.compare(v, i, p)
                        hold(v, copied, i * 2 + p + 1, passed)
                        nc.vector.bn_stats(stats[:, ds(i * 2 + p, 1), :].rearrange("p a s -> p (a s)"),
                                           h1[p][:, :]).then_inc(measured, 1)
                turns(v, GROUPS // 2, body)
                v.wait_ge(measured, GROUPS)
                nc.vector.bn_stats(stats[:, GROUPS - 1, :], real_part(h1[1][:, :])).then_inc(stats_ok, 1)
                v.wait_ge(stats_ok, 1)
                nc.vector.bn_aggr(m.mv1[:, :], stats[:, :, :].rearrange("p g s -> p (g s)"))
                r.end(v)

            @block.tensor
            def _(pe):
                def body(i):
                    for p in range(2):
                        pe.wait_ge(picked, i * 2 + p + 1)
                        pe.wait_ge(win_in[p], i * 16 + 16)
                        if not first(i):
                            pe.wait_ge(copied, i * 2 + p - 1)
                        nc.tensor.matmul(ps[p][:, :], win[p][:, :], pick[p][:, :], start=True, stop=False,
                                         skip_group_check=True)
                        pe.wait_ge(got[p], i * (CG * 16) + CG * 16)
                        for c in range(CG):
                            last = nc.tensor.matmul(ps[p][:, c * P:(c + 1) * P], gs[p][:, c, :], m.ident[:, :],
                                                    start=False, stop=True, skip_group_check=True)
                        last.then_inc(summed, 1)
                        r.count(pe, i, p)
                turns(pe, GROUPS // 2, body)

            @block.scalar
            def _(act):
                def body(i):
                    for p in range(2):
                        hold(act, summed, i * 2 + p + 1, passed_act)
                        if not first(i):
                            act.wait_ge(stored[p], i * 16)
                            hold(act, measured, i * 2 + p - 1, passed_act)
                        nc.scalar.activation(h1[p][:, :], ps[p][:, :], ACT.Copy).then_inc(copied, 1)
                        act.wait_ge(copied, i * 2 + p + 1)
                        act.dma_start(d.h1[:, ds(i * (2 * GE) + p * GE, GE)], h1[p][:, :]).then_inc(stored[p], 16)
                turns(act, GROUPS // 2, body)
                for p in range(2):
                    act.wait_ge(stored[p], 16 * (GROUPS // 2))


def norm_terms(nc, m, mv, gamma, beta, scale, shift, tag, mean_extra=None):
    ctx, sb, pb, sem = scope(nc, tag)
    with ctx:
        vpe, root, inv, t = (sb(x, [P, 1]) for x in ("vpe", "root", "inv", "t"))
        eps_ok, root_ok, chain = (sem(x) for x in ("eps_ok", "root_ok", "chain"))
        with nc.Block() as block:
            @block.vector
            def _(v):
                nc.vector.tensor_scalar(vpe[:, :], mv[:, 1:2], EPS, None, ALU.add).then_inc(eps_ok, 1)
                v.wait_ge(root_ok, 1)
                step(v, nc.vector.reciprocal(inv[:, :], root[:, :]), chain, 1)
                step(v, nc.vector.tensor_tensor(scale[:, :], inv[:, :], gamma, ALU.mult), chain, 2)
                step(v, nc.vector.tensor_tensor(t[:, :], mv[:, 0:1], scale[:, :], ALU.mult), chain, 3)
                step(v, nc.vector.tensor_tensor(shift[:, :], beta, t[:, :], ALU.subtract), chain, 4)

            @block.scalar
            def _(act):
                act.wait_ge(eps_ok, 1)
                nc.scalar.activation(root[:, :], vpe[:, :], ACT.Sqrt).then_inc(root_ok, 1)


def l0_second(nc, d, m):
    ctx, sb, pb, sem = scope(nc, "second")
    R = 4
    with ctx:
        h1 = [sb(f"h1{k}", [P, GE]) for k in range(R)]
        hr = [sb(f"hr{k}", [P, GE]) for k in range(R)]
        stats = sb("stats", [P, GROUPS, 6])
        raw = sb("raw", [P, 2])
        ps = [pb(f"ps{k}", [P, GE]) for k in range(R)]
        h1_in = [sem(f"h1_in{k}") for k in range(R)]
        relued, mm, measured, passed, stats_ok, raw_ok = (
            sem(x) for x in ("relued", "mm", "measured", "passed", "stats_ok", "raw_ok"))
        with nc.Block() as block:
            @block.sync
            def _(sp):
                def body(i):
                    for k in range(R):
                        if not first(i):
                            sp.wait_ge(relued, i * R - R + k + 1)
                        sp.dma_start(h1[k][:, :], d.h1[:, ds(i * (R * GE) + k * GE, GE)]).then_inc(h1_in[k], 16)
                turns(sp, GROUPS // R, body)

            @block.scalar
            def _(act):
                def body(i):
                    for k in range(R):
                        act.wait_ge(h1_in[k], i * 16 + 16)
                        if not first(i):
                            act.wait_ge(mm, i * R - R + k + 1)
                        nc.scalar.activation(hr[k][:, :], h1[k][:, :], ACT.Relu, bias=m.shift1[:, 0:1],
                                             scale=m.scale1[:, 0:1]).then_inc(relued, 1)
                turns(act, GROUPS // R, body)

            @block.tensor
            def _(pe):
                def body(i):
                    for k in range(R):
                        pe.wait_ge(relued, i * R + k + 1)
                        if not first(i):
                            pe.wait_ge(measured, i * R - R + k + 1)
                        nc.tensor.matmul(ps[k][:, :], m.w2t[:, :], hr[k][:, :], start=True, stop=True).then_inc(mm, 1)
                turns(pe, GROUPS // R, body)

            @block.vector
            def _(v):
                def body(i):
                    for k in range(R):
                        hold(v, mm, i * R + k + 1, passed)
                        nc.vector.bn_stats(stats[:, ds(i * R + k, 1), :].rearrange("p a s -> p (a s)"),
                                           ps[k][:, :]).then_inc(measured, 1)
                turns(v, GROUPS // R, body)
                v.wait_ge(measured, GROUPS)
                nc.vector.bn_stats(stats[:, GROUPS - 1, :], real_part(ps[R - 1])).then_inc(stats_ok, 1)
                v.wait_ge(stats_ok, 1)
                step(v, nc.vector.bn_aggr(raw[:, :], stats[:, :, :].rearrange("p g s -> p (g s)")), raw_ok, 1)
                nc.vector.tensor_tensor(m.mv2[:, 0:1], raw[:, 0:1], m.cols[:, 4:5], ALU.add)
                nc.vector.tensor_copy(m.mv2[:, 1:2], raw[:, 1:2])


def fold_second(nc, d, m):
    ctx, sb, pb, sem = scope(nc, "fold")
    with ctx:
        w2 = sb("w2", [P, D])
        w2s = sb("w2s", [P, D])
        t, col, cols = sb("t", [P, 1]), sb("col", [P, 1]), sb("cols", [P, P])
        ps_w, ps_r = pb("ps_w", [P, D]), pb("ps_r", [P, D])
        w_in, scaled, t_ok, col_ok, turned = (sem(x) for x in ("w_in", "scaled", "t_ok", "col_ok", "turned"))
        with nc.Block() as block:
            @block.sync
            def _(sp):
                sp.dma_start(w2[:, :], d.w2).then_inc(w_in, 16)

            @block.vector
            def _(v):
                v.wait_ge(w_in, 16)
                nc.vector.tensor_scalar(w2s[:, :], w2[:, :], m.scale2[:, 0:1], None, ALU.mult).then_inc(scaled, 1)
                step(v, nc.vector.tensor_tensor(t[:, :], m.cols[:, 4:5], m.scale2[:, :], ALU.mult), t_ok, 1)
                step(v, nc.vector.tensor_tensor(col[:, :], t[:, :], m.shift2[:, :], ALU.add), col_ok, 1)
                nc.vector.tensor_scalar(cols[:, :], m.ones[:, :], col[:, 0:1], None, ALU.mult).then_inc(col_ok, 1)
                v.wait_ge(turned, 2)
                nc.vector.tensor_copy(m.w2ts[:, :], ps_w[:, :])
                nc.vector.tensor_copy(m.row2[:, :], ps_r[:, :])

            @block.tensor
            def _(pe):
                pe.wait_ge(scaled, 1)
                nc.tensor.transpose(ps_w[:, :], w2s[:, :], m.ident[:, :]).then_inc(turned, 1)
                pe.wait_ge(col_ok, 2)
                nc.tensor.matmul(ps_r[:, :], cols[:, :], m.ident[:, :], start=True, stop=True).then_inc(turned, 1)


def l0_third(nc, d, m):
    ctx, sb, pb, sem = scope(nc, "third")
    R = 4
    with ctx:
        h1 = [sb(f"h1{p}", [P, GE]) for p in range(R)]
        hr = [sb(f"hr{p}", [P, GE]) for p in range(R)]
        up = [sb(f"up{p}", [P, CG, D]) for p in range(R)]
        to = [sb(f"to{p}", [P, CG], i32) for p in range(R)]
        zero = sb("zero", [SLOTS, D])
        ps = [pb(f"ps{p}", [P, CG, D]) for p in range(R)]
        h1_in = [sem(f"h1_in{p}") for p in range(R)]
        put = [sem(f"put{p}") for p in range(R)]
        relued, mm, up_ok, to_ok, passed, zero_ok, zero_out = (
            sem(x) for x in ("relued", "mm", "up_ok", "to_ok", "passed", "zero_ok", "zero_out"))
        with nc.Block() as block:
            @block.sync
            def _(sp):
                sp.wait_ge(zero_ok, 1)
                sp.dma_start(d.up[EP:EP + SLOTS, :], zero[:, :]).then_inc(zero_out, 16)

                def body(i):
                    for p in range(R):
                        if not first(i):
                            sp.wait_ge(relued, i * R - R + p + 1)
                        sp.dma_start(h1[p][:, :], d.h1[:, ds(i * (R * GE) + p * GE, GE)]).then_inc(h1_in[p], 16)
                turns(sp, GROUPS // R, body)
                sp.wait_ge(zero_out, 16)

            @block.vector
            def _(v):
                nc.vector.memset(zero[:, :], 0.0).then_inc(zero_ok, 1)

                def body(i):
                    for p in range(R):
                        if not first(i):
                            v.wait_ge(put[p], i * (16 * CG))
                        nc.vector.tensor_scalar(to[p][:, :], m.where_t[:, ds(i * (R * CG) + p * CG, CG)], 0.0, None,
                                                ALU.add).then_inc(to_ok, 1)
                turns(v, GROUPS // R, body)

            @block.scalar
            def _(act):
                def body(i):
                    for p in range(R):
                        act.wait_ge(h1_in[p], i * 16 + 16)
                        if not first(i):
                            act.wait_ge(mm, i * R - R + p + 1)
                        nc.scalar.activation(hr[p][:, :], h1[p][:, :], ACT.Relu, bias=m.shift1[:, 0:1],
                                             scale=m.scale1[:, 0:1]).then_inc(relued, 1)
                    for p in range(R):
                        act.wait_ge(mm, i * R + p + 1)
                        if not first(i):
                            act.wait_ge(put[p], i * (16 * CG))
                        nc.scalar.activation(up[p][:, :, :], ps[p][:, :, :], ACT.Relu).then_inc(up_ok, 1)
                turns(act, GROUPS // R, body)

            @block.tensor
            def _(pe):
                def body(i):
                    for p in range(R):
                        pe.wait_ge(relued, i * R + p + 1)
                        if not first(i):
                            pe.wait_ge(up_ok, i * R - R + p + 1)
                        for c in range(CG):
                            nc.tensor.matmul(ps[p][:, c, :], hr[p][:, c * P:(c + 1) * P], m.w2ts[:, :],
                                             start=True, stop=False)
                            last = nc.tensor.matmul(ps[p][:, c, :], m.ones[0:1, :], m.row2[0:1, :],
                                                    start=False, stop=True)
                        last.then_inc(mm, 1)
                turns(pe, GROUPS // R, body)

            @block.gpsimd
            def _(g):
                def body(i):
                    for p in range(R):
                        hold(g, to_ok, i * R + p + 1, passed)
                        hold(g, up_ok, i * R + p + 1, passed)
                        for c in range(CG):
                            g.indirect_dma_start(d.up, bass.IndirectOffsetOnAxis(ap=to[p][:, c:c + 1], axis=0),
                                                 up[p][:, c, :], None).then_inc(put[p], 16)
                turns(g, GROUPS // R, body)
                for p in range(R):
                    g.wait_ge(put[p], 16 * CG * (GROUPS // R))


def l0_third_ordered(nc, d, m):
    ctx, sb, pb, sem = scope(nc, "thirdo")
    R = 4
    with ctx:
        h1 = [sb(f"h1{p}", [P, GE]) for p in range(R)]
        hr = [sb(f"hr{p}", [P, GE]) for p in range(R)]
        pre = [sb(f"pre{p}", [P, CG, D]) for p in range(R)]
        up = [sb(f"up{p}", [P, CG, D]) for p in range(R)]
        ohl = [sb(f"ohl{p}", [P, CG, P], bf16) for p in range(R)]
        ohh = [sb(f"ohh{p}", [P, CG, NB], bf16) for p in range(R)]
        ohw = [sb(f"ohw{p}", [P, CG, P]) for p in range(R)]
        part = [sb(f"part{q}", [P, P]) for q in range(2)]
        sums = sb("sums", [P, NP_])
        block_sums = [sb(f"block_sums{q}", [P, P]) for q in range(2)]
        ps = [pb(f"ps{p}", [P, CG, D]) for p in range(R)]
        ps_n = pb("ps_n", [P, NB])
        ps_s = [pb(f"ps_s{q}", [P, P]) for q in range(2)]
        h1_in = [sem(f"h1_in{p}") for p in range(R)]
        (relued, mm, pre_ok, up_ok, onehot, counted, summed, part_ok, taken, zeroed, cut, turned, kept, passed,
         passed_act) = (
            sem(x) for x in ("relued", "mm", "pre_ok", "up_ok", "onehot", "counted", "summed", "part_ok", "taken",
                             "zeroed", "cut", "turned", "kept", "passed", "passed_act"))
        with nc.Block() as block:
            @block.sync
            def _(sp):
                def body(i):
                    for p in range(R):
                        if not first(i):
                            sp.wait_ge(relued, i * R - R + p + 1)
                        sp.dma_start(h1[p][:, :], d.h1[:, ds(i * (R * GE) + p * GE, GE)]).then_inc(h1_in[p], 16)
                turns(sp, GROUPS // R, body)

            @block.gpsimd
            def _(g):
                g.memset(sums[:, :], 0.0).then_inc(zeroed, 1)
                g.wait_ge(zeroed, 1)

                def body(i):
                    for p in range(R):
                        n = i * R + p + 1
                        hold(g, part_ok, n, passed)
                        if not (first(i) and p == 0):
                            hold(g, taken, n - 1, passed)
                        base = g.value_load(m.bases[0:1, ds(n - 1, 1)], min_val=0, max_val=N)
                        g.tensor_tensor(sums[:, ds(base, P)], sums[:, ds(base, P)], part[p % 2][:, :], ALU.add
                                        ).then_inc(taken, 1)
                turns(g, GROUPS // R, body)

            @block.vector
            def _(v):
                def bring(i, p, n):
                    v.wait_ge(summed, n)
                    if not (first(i) and p < 2):
                        v.wait_ge(taken, n - 2)
                    nc.vector.tensor_copy(part[p % 2][:, :], ps_s[p % 2]).then_inc(part_ok, 1)

                def body(i):
                    for p in range(R):
                        n = i * R + p + 1
                        if not first(i):
                            v.wait_ge(counted, n - R)
                            v.wait_ge(summed, n - R)
                        at = ds(i * (R * CG) + p * CG, CG)
                        wide = m.iota_row[:, :].unsqueeze(1).to_broadcast([P, CG, P])
                        nc.vector.tensor_tensor(ohl[p][:, :, :], wide,
                                                m.lo[:, 1, at].unsqueeze(2).to_broadcast([P, CG, P]), ALU.is_equal)
                        nc.vector.tensor_tensor(ohw[p][:, :, :], wide,
                                                m.inside[:, at].unsqueeze(2).to_broadcast([P, CG, P]), ALU.is_equal)
                        nc.vector.tensor_tensor(ohh[p][:, :, :],
                                                m.iota_row[:, 0:NB].unsqueeze(1).to_broadcast([P, CG, NB]),
                                                m.hi[:, 1, at].unsqueeze(2).to_broadcast([P, CG, NB]),
                                                ALU.is_equal).then_inc(onehot, 1)
                        v.wait_ge(mm, n)
                        if not first(i):
                            v.wait_ge(up_ok, n - R)
                        nc.vector.tensor_tensor(pre[p][:, :, :], ps[p],
                                                m.row2[:, :].unsqueeze(1).to_broadcast([P, CG, D]), ALU.add
                                                ).then_inc(pre_ok, 1)
                        if not (first(i) and p == 0):
                            bring(i if p else 1, (p - 1) % R, n - 1)
                turns(v, GROUPS // R, body)
                bring(1, R - 1, GROUPS)
                nc.vector.tensor_tensor(m.deg[:, 1, 0:NB], ps_n[:, :], m.real[:, :], ALU.mult)
                nc.vector.tensor_copy(m.count[:, 1, :], ps_n[:, :])

                def keep(i):
                    for q in range(2):
                        v.wait_ge(turned, i * 2 + q + 1)
                        nc.vector.tensor_scalar(m.agg[:, ds(i * 2 + q, 1), :].rearrange("p a f -> p (a f)"), ps_s[q],
                                                0.0, None, ALU.add).then_inc(kept, 1)
                turns(v, NB // 2, keep)

            @block.scalar
            def _(act):
                def body(i):
                    for p in range(R):
                        act.wait_ge(h1_in[p], i * 16 + 16)
                        if not first(i):
                            act.wait_ge(mm, i * R - R + p + 1)
                        nc.scalar.activation(hr[p][:, :], h1[p][:, :], ACT.Relu, bias=m.shift1[:, 0:1],
                                             scale=m.scale1[:, 0:1]).then_inc(relued, 1)
                    for p in range(R):
                        act.wait_ge(pre_ok, i * R + p + 1)
                        if not first(i):
                            act.wait_ge(summed, i * R - R + p + 1)
                        nc.scalar.activation(up[p][:, :, :], pre[p][:, :, :], ACT.Relu).then_inc(up_ok, 1)
                turns(act, GROUPS // R, body)
                act.wait_ge(taken, GROUPS)

                def separate(i):
                    for q in range(2):
                        if not first(i):
                            hold(act, turned, i * 2 + q - 1, passed_act)
                        nc.scalar.activation(block_sums[q][:, :], sums[:, ds(i * (2 * P) + q * P, P)], ACT.Copy
                                             ).then_inc(cut, 1)
                turns(act, NB // 2, separate)

            @block.tensor
            def _(pe):
                def add_up(i, p, n):
                    pe.wait_ge(up_ok, n)
                    if not (first(i) and p < 2):
                        pe.wait_ge(part_ok, n - 2)
                    for c in range(CG):
                        last = nc.tensor.matmul(ps_s[p % 2], up[p][:, c, :], ohw[p][:, c, :], start=c == 0,
                                                stop=c == CG - 1)
                    last.then_inc(summed, 1)

                def body(i):
                    for p in range(R):
                        n = i * R + p + 1
                        pe.wait_ge(relued, n)
                        if not first(i):
                            pe.wait_ge(pre_ok, n - R)
                        for c in range(CG):
                            last = nc.tensor.matmul(ps[p][:, c, :], hr[p][:, c * P:(c + 1) * P], m.w2ts[:, :],
                                                    start=True, stop=True)
                        last.then_inc(mm, 1)
                        pe.wait_ge(onehot, n)
                        for c in range(CG):
                            last = nc.tensor.matmul(ps_n[:, :], ohl[p][:, c, :], ohh[p][:, c, :],
                                                    start=first(i) and p == 0 and c == 0, stop=False,
                                                    skip_group_check=True)
                        last.then_inc(counted, 1)
                        if not (first(i) and p == 0):
                            add_up(i if p else 1, (p - 1) % R, n - 1)
                turns(pe, GROUPS // R, body)
                add_up(1, R - 1, GROUPS)
                pe.wait_ge(part_ok, GROUPS)

                def turn(i):
                    for q in range(2):
                        pe.wait_ge(cut, i * 2 + q + 1)
                        if not first(i):
                            pe.wait_ge(kept, i * 2 + q - 1)
                        nc.tensor.transpose(ps_s[q], block_sums[q][:, :], m.ident[:, :]).then_inc(turned, 1)
                turns(pe, NB // 2, turn)


def l0_gather(nc, d, m):
    ctx, sb, pb, sem = scope(nc, "sum")
    with ctx:
        run = [sb(f"run{p}", [P, SLOTS, D]) for p in range(2)]
        at_f = [sb(f"at_f{p}", [P, 1]) for p in range(2)]
        at_c = [sb(f"at_c{p}", [P, 1]) for p in range(2)]
        at = [sb(f"at{p}", [P, 1], i32) for p in range(2)]
        left = [sb(f"left{p}", [P, 1]) for p in range(2)]
        live = [sb(f"live{p}", [P, SLOTS]) for p in range(2)]
        masked = [sb(f"masked{p}", [P, SLOTS, D]) for p in range(2)]
        part = [sb(f"part{p}", [P, D]) for p in range(2)]
        passed_slots = sb("passed_slots", [P, 1])
        got = [sem(f"got{p}") for p in range(2)]
        at_f_ok, at_c_ok, at_ok, left_ok, live_ok, masked_ok, part_ok, passed, summed, slots_ok, zeroed = (
            sem(x) for x in ("at_f_ok", "at_c_ok", "at_ok", "left_ok", "live_ok", "masked_ok", "part_ok",
                             "passed", "summed", "slots_ok", "zeroed"))
        with nc.Block() as block:
            @block.vector
            def _(v):
                rounds = v.value_load(m.trips[0:1, 1:2], min_val=1, max_val=EP // SLOTS + 1)
                nc.vector.memset(m.agg[:, :, :], 0.0).then_inc(zeroed, 1)
                step(v, nc.vector.memset(passed_slots[:, :], 0.0), zeroed, 2)

                def aim(n, b, p):
                    step(v, nc.vector.tensor_tensor(at_f[p][:, :], m.place[:, ds(b, 1), 1], passed_slots[:, :],
                                                    ALU.add), at_f_ok, n)
                    step(v, nc.vector.tensor_scalar(at_c[p][:, :], at_f[p][:, :], float(EP), float(D), ALU.min,
                                                    ALU.mult), at_c_ok, n)
                    nc.vector.tensor_copy(at[p][:, :], at_c[p][:, :]).then_inc(at_ok, 1)

                aim(1, 0, 0)
                with v.Fori(0, rounds) as r:
                    with v.Fori(0, NB // 2) as j:
                        for p in range(2):
                            n = r * NB + j * 2 + p + 1
                            b = j * 2 + p
                            aim(n + 1, b + 1, 1 - p)
                            step(v, nc.vector.tensor_tensor(left[p][:, :], m.deg[:, 1, ds(b, 1)], passed_slots[:, :],
                                                            ALU.subtract), left_ok, n)
                            step(v, nc.vector.tensor_scalar(live[p][:, :], m.iota_row[:, 0:SLOTS], left[p][:, 0:1],
                                                            None, ALU.is_lt), live_ok, n)
                            v.wait_ge(got[p], r * (NB // 2 * 16) + j * 16 + 16)
                            step(v, nc.vector.tensor_tensor(
                                masked[p][:, :, :], run[p][:, :, :],
                                live[p][:, :].unsqueeze(2).to_broadcast([P, SLOTS, D]), ALU.mult), masked_ok, n)
                            step(v, nc.vector.tensor_reduce(part[p][:, :],
                                                            masked[p][:, :, :].rearrange("p s f -> p f s"), X,
                                                            ALU.add), part_ok, n)
                            step(v, nc.vector.tensor_tensor(m.agg[:, ds(b, 1), :].rearrange("p a f -> p (a f)"),
                                                            m.agg[:, ds(b, 1), :].rearrange("p a f -> p (a f)"),
                                                            part[p][:, :], ALU.add), summed, n)
                    step(v, nc.vector.tensor_scalar(passed_slots[:, :], passed_slots[:, :], float(SLOTS), None,
                                                    ALU.add), slots_ok, r + 1)

            @block.sync
            def _(sp):
                sp.nop()

            @block.scalar
            def _(act):
                act.nop()

            @block.tensor
            def _(pe):
                pe.nop()

            @block.gpsimd
            def _(g):
                rounds = g.value_load(m.trips[0:1, 1:2], min_val=1, max_val=EP // SLOTS + 1)
                flat = d.up.rearrange("n f -> (n f)").rearrange("(n o) -> n o", o=1)

                def fetch(n, p):
                    hold(g, at_ok, n, passed)
                    g.indirect_dma_start(run[p][:, :, :].rearrange("p s f -> p (s f)"), None, flat,
                                         bass.IndirectOffsetOnAxis(ap=at[p][:, 0:1], axis=0)).then_inc(got[p], 16)

                fetch(1, 0)
                with g.Fori(0, rounds) as r:
                    with g.Fori(0, NB // 2) as j:
                        for p in range(2):
                            n = r * NB + j * 2 + p + 1
                            fetch(n + 1, 1 - p)
                g.wait_ge(got[0], rounds * (NB // 2 * 16) + 16)


def layer_norm(nc, d, m):
    ctx, sb, pb, sem = scope(nc, "norm1")
    with ctx:
        x = sb("x", [P, NB, D])
        sq = sb("sq", [P, NB, D])
        tot, mean, var, root, inv = (sb(n, [P, NB]) for n in ("tot", "mean", "var", "root", "inv"))
        x_in, chain, sq_ok, var_ok, root_ok, out_ok, stored, cent_ok = (
            sem(n) for n in ("x_in", "chain", "sq_ok", "var_ok", "root_ok", "out_ok", "stored", "cent_ok"))
        wide = [P, NB, D]
        with nc.Block() as block:
            @block.sync
            def _(sp):
                sp.dma_start(x[:, :, :], d.x.rearrange("(b p) f -> p b f", p=P)).then_inc(x_in, 16)
                sp.wait_ge(out_ok, 1)
                sp.dma_start(d.x1.rearrange("(b p) f -> p b f", p=P), m.agg[:, :, :]).then_inc(stored, 16)
                sp.wait_ge(stored, 16)

            @block.vector
            def _(v):
                v.wait_ge(x_in, 16)
                step(v, nc.vector.tensor_tensor(x[:, :, :], x[:, :, :], m.agg[:, :, :], ALU.add), chain, 1)
                step(v, nc.vector.tensor_reduce(tot[:, :], x[:, :, :], X, ALU.add), chain, 2)
                step(v, nc.vector.tensor_scalar(mean[:, :], tot[:, :], 1.0 / D, None, ALU.mult), chain, 3)
                nc.vector.tensor_tensor(x[:, :, :], x[:, :, :], mean[:, :].unsqueeze(2).to_broadcast(wide),
                                        ALU.subtract).then_inc(cent_ok, 1)
                v.wait_ge(sq_ok, 1)
                step(v, nc.vector.tensor_reduce(tot[:, :], sq[:, :, :], X, ALU.add), chain, 4)
                nc.vector.tensor_scalar(var[:, :], tot[:, :], 1.0 / D, EPS, ALU.mult, ALU.add).then_inc(var_ok, 1)
                v.wait_ge(root_ok, 1)
                step(v, nc.vector.reciprocal(inv[:, :], root[:, :]), chain, 5)
                nc.vector.tensor_tensor(m.agg[:, :, :], x[:, :, :], inv[:, :].unsqueeze(2).to_broadcast(wide),
                                        ALU.mult).then_inc(out_ok, 1)

            @block.scalar
            def _(act):
                act.wait_ge(cent_ok, 1)
                nc.scalar.activation(sq[:, :, :], x[:, :, :], ACT.Square).then_inc(sq_ok, 1)
                act.wait_ge(var_ok, 1)
                nc.scalar.activation(root[:, :], var[:, :], ACT.Sqrt).then_inc(root_ok, 1)
def l1_self_terms(nc, d, m):
    ctx, sb, pb, sem = scope(nc, "selft")
    with ctx:
        col, cols, wt, we = sb("col", [DE, 1]), sb("cols", [DE, P]), sb("wt", [DE, D]), sb("we", [DE, 2 * D])
        ps = pb("ps", [P, 3 * D])
        w_in, cols_ok, mm = (sem(x) for x in ("w_in", "cols_ok", "mm"))
        with nc.Block() as block:
            @block.sync
            def _(sp):
                sp.dma_start(col[:, :], d.time0).then_inc(w_in, 16)
                sp.dma_start(wt[:, :], d.wt).then_inc(w_in, 16)
                sp.dma_start(we[:, :], d.we[DE:2 * DE, :]).then_inc(w_in, 16)

            @block.vector
            def _(v):
                v.wait_ge(w_in, 48)
                nc.vector.tensor_copy(cols[:, :], col[:, 0:1].to_broadcast([DE, P])).then_inc(cols_ok, 1)
                v.wait_ge(mm, 1)
                nc.vector.tensor_copy(m.selfadd[:, :], ps[:, :])

            @block.tensor
            def _(pe):
                pe.wait_ge(cols_ok, 1)
                nc.tensor.matmul(ps[:, 0:D], cols[:, :], wt[:, :], start=True, stop=True)
                nc.tensor.matmul(ps[:, D:3 * D], cols[:, :], we[:, :], start=True, stop=True).then_inc(mm, 1)


def l1_tables(nc, d, m):
    ctx, sb, pb, sem = scope(nc, "tables")
    R = 3
    NR = NB - NB % R
    with ctx:
        wx, bx = sb("wx", [P, 3 * D]), sb("bx", [P, 3 * D])
        xb = [sb(f"xb{k}", [P, D]) for k in range(R)]
        xbT = [sb(f"xbT{k}", [P, D]) for k in range(R)]
        tn = [sb(f"tn{k}", [P, TN_W]) for k in range(R)]
        me = [sb(f"me{k}", [P, 3 * D]) for k in range(R)]
        kr = [sb(f"kr{k}", [P, D]) for k in range(R)]
        qk = [sb(f"qk{k}", [P, D]) for k in range(R)]
        score = [sb(f"score{k}", [P, HEADS]) for k in range(R)]
        ps_t = [pb(f"ps_t{k}", [P, D]) for k in range(R)]
        ps = [pb(f"ps{k}", [P, 3 * D]) for k in range(R)]
        w_in, turned, xbT_ok, mm, tn_ok, me_ok, kr_ok, qk_ok, score_ok, kept = (
            sem(x) for x in ("w_in", "turned", "xbT_ok", "mm", "tn_ok", "me_ok", "kr_ok", "qk_ok", "score_ok", "kept"))
        xb_in = [sem(f"xb_in{k}") for k in range(R)]
        stored = [sem(f"stored{k}") for k in range(R)]

        def blocks(eng, one):
            def body(i):
                for k in range(R):
                    one(i, k, i * R + k + 1)
            turns(eng, NR // R, body)
            for k in range(NB - NR):
                one(NR // R, k, NR + k + 1)

        with nc.Block() as block:
            @block.sync
            def _(sp):
                sp.dma_start(wx[:, :], d.wx).then_inc(w_in, 16)
                sp.dma_start(bx[:, :], d.bx.partition_broadcast(P)).then_inc(w_in, 16)

                def one(i, k, n):
                    if not first(i):
                        sp.wait_ge(turned, n - R)
                    sp.dma_start(xb[k][:, :], d.x1[ds((n - 1) * P, P), :]).then_inc(xb_in[k], 16)
                blocks(sp, one)

            @block.tensor
            def _(pe):
                pe.wait_ge(w_in, 32)

                def one(i, k, n):
                    pe.wait_ge(xb_in[k], i * 16 + 16)
                    if not first(i):
                        pe.wait_ge(xbT_ok, n - R)
                    nc.tensor.transpose(ps_t[k][:, :], xb[k][:, :], m.ident[:, :]).then_inc(turned, 1)
                    pe.wait_ge(xbT_ok, n)
                    if not first(i):
                        pe.wait_ge(tn_ok, (n - R) * 2)
                    nc.tensor.matmul(ps[k][:, :], xbT[k][:, :], wx[:, :], start=True, stop=True).then_inc(mm, 1)
                blocks(pe, one)

            @block.scalar
            def _(act):
                def one(i, k, n):
                    act.wait_ge(turned, n)
                    if not first(i):
                        act.wait_ge(mm, n - R)
                    nc.scalar.activation(xbT[k][:, :], ps_t[k][:, :], ACT.Copy).then_inc(xbT_ok, 1)
                    act.wait_ge(tn_ok, n * 2)
                    act.dma_start(d.tn[ds((n - 1) * P, P), :], tn[k][:, :]).then_inc(stored[k], 16)
                blocks(act, one)
                for k in range(R):
                    act.wait_ge(stored[k], 16 * (NR // R + (k < NB - NR)))

            @block.vector
            def _(v):
                def one(i, k, n):
                    if not first(i):
                        v.wait_ge(stored[k], i * 16)
                    nc.vector.tensor_scalar(tn[k][:, 3 * D:TN_W], m.place[:, ds(n - 1, 1), :].rearrange("p a w -> p (a w)"),
                                            0.0, None, ALU.add).then_inc(tn_ok, 1)
                    v.wait_ge(mm, n)
                    nc.vector.tensor_tensor(tn[k][:, 0:3 * D], ps[k][:, :], bx[:, :], ALU.add).then_inc(tn_ok, 1)
                    v.wait_ge(tn_ok, n * 2)
                    step(v, nc.vector.tensor_tensor(me[k][:, :], tn[k][:, 0:3 * D], m.selfadd[:, :], ALU.add), me_ok, n)
                    step(v, nc.vector.tensor_scalar(kr[k][:, :], me[k][:, D:2 * D], 0.0, None, ALU.max), kr_ok, n)
                    step(v, nc.vector.scalar_tensor_tensor(qk[k][:, :], me[k][:, 0:D], 0.0, kr[k][:, :], ALU.max,
                                                           ALU.mult), qk_ok, n)
                    step(v, nc.vector.tensor_reduce(score[k][:, :], qk[k][:, :].rearrange("p (h f) -> p h f", h=HEADS),
                                                    X, ALU.add), score_ok, n)
                    nc.vector.tensor_scalar(m.top[:, ds(n - 1, 1), :].rearrange("p a h -> p (a h)"), score[k][:, :],
                                            0.0, None, ALU.add)
                    nc.vector.tensor_scalar(m.agg[:, ds(n - 1, 1), :].rearrange("p a f -> p (a f)"),
                                            me[k][:, 2 * D:3 * D], 0.0, None, ALU.add)
                nc.vector.memset(m.den[:, :, :], 1.0)
                blocks(v, one)


def l1_edges(nc, d, m):
    ctx, sb, pb, sem = scope(nc, "edges")
    with ctx:
        wt, we = sb("wt", [DE, D]), sb("we", [P, 2 * D])
        idx = [sb(f"idx{p}", [P, 2 * CG], i32) for p in range(2)]
        ft = [sb(f"ft{p}", [DE, GE]) for p in range(2)]
        fe = [sb(f"fe{p}", [P, GE]) for p in range(2)]
        rows = [[sb(f"rows{w}{p}", [P, CG, TN_W]) for p in range(2)] for w in range(2)]
        qk = [[sb(f"qk{w}{p}", [P, CG, 2 * D]) for p in range(2)] for w in range(2)]
        prod = [[sb(f"prod{w}{p}", [P, CG, D]) for p in range(2)] for w in range(2)]
        msg = [[sb(f"msg{w}{p}", [P, CG, MSG_W]) for p in range(2)] for w in range(2)]
        to_f = [sb(f"to_f{p}", [P, CG]) for p in range(2)]
        to = [[sb(f"to{w}{p}", [P, CG], i32) for p in range(2)] for w in range(2)]
        zero = sb("zero", [SLOTS, MSG_W])
        ps = [pb(f"ps{p}", [P, CG, BANK]) for p in range(2)]
        w_in, mm, added, v_ok, relued, prod_ok, msg_ok, to_ok, passed, zero_ok, zero_out = (
            sem(x) for x in ("w_in", "mm", "added", "v_ok", "relued", "prod_ok", "msg_ok", "to_ok", "passed", "zero_ok",
                             "zero_out"))
        idx_in, f_in, got, put = ([sem(f"{x}{p}") for p in range(2)] for x in ("idx_in", "f_in", "got", "put"))
        GOT = 2 * CG * 16
        with nc.Block() as block:
            @block.sync
            def _(sp):
                sp.dma_start(wt[:, :], d.wt).then_inc(w_in, 16)
                sp.dma_start(we[:, :], d.we).then_inc(w_in, 16)
                sp.wait_ge(zero_ok, 1)
                for w in range(2):
                    sp.dma_start(d.msg_of[w][EP:EP + SLOTS, :], zero[:, :]).then_inc(zero_out, 16)

                def body(i):
                    for p in range(2):
                        if not first(i):
                            sp.wait_ge(got[p], i * GOT)
                        sp.dma_start(idx[p][:, :], d.idx[ds(i * 2 + p, 1), :, :].rearrange("a p c -> (a p) c")
                                     ).then_inc(idx_in[p], 16)
                        if not first(i):
                            sp.wait_ge(mm, i * 2 + p - 1)
                        sp.dma_start(ft[p][:, :], d.ft[:, ds(i * (2 * GE) + p * GE, GE)]).then_inc(f_in[p], 16)
                        sp.dma_start(fe[p][:, :], d.fe[:, ds(i * (2 * GE) + p * GE, GE)]).then_inc(f_in[p], 16)
                turns(sp, GROUPS // 2, body)
                sp.wait_ge(zero_out, 32)

            @block.gpsimd
            def _(g):
                def gather(i, p, n):
                    hold(g, idx_in[p], i * 16 + 16, passed)
                    if not first(i):
                        hold(g, to_ok, (n - 2) * 2, passed)
                    for c in range(CG):
                        for w in range(2):
                            g.indirect_dma_start(rows[w][p][:, c, :], None, d.tn, bass.IndirectOffsetOnAxis(
                                ap=idx[p][:, w * CG + c:w * CG + c + 1], axis=0)).then_inc(got[p], 16)

                def scatter(p, n):
                    hold(g, msg_ok, n * 2, passed)
                    hold(g, to_ok, n * 2, passed)
                    for c in range(CG):
                        for w in range(2):
                            g.indirect_dma_start(d.msg_of[w], bass.IndirectOffsetOnAxis(
                                ap=to[w][p][:, c:c + 1], axis=0), msg[w][p][:, c, :], None).then_inc(put[p], 16)

                def body(i):
                    gather(i, 0, i * 2 + 1)
                    if not first(i):
                        scatter(1, i * 2)
                    gather(i, 1, i * 2 + 2)
                    scatter(0, i * 2 + 1)
                turns(g, GROUPS // 2, body)
                scatter(1, GROUPS)
                for p in range(2):
                    g.wait_ge(put[p], GOT * (GROUPS // 2))

            @block.tensor
            def _(pe):
                pe.wait_ge(w_in, 32)

                def body(i):
                    for p in range(2):
                        n = i * 2 + p + 1
                        pe.wait_ge(f_in[p], i * 32 + 32)
                        if not first(i):
                            pe.wait_ge(v_ok, (n - 2) * 2)
                        for c in range(CG):
                            nc.tensor.matmul(ps[p][:, c, D:3 * D], fe[p][:, c * P:(c + 1) * P], we[:, :],
                                             start=True, stop=True)
                            last = nc.tensor.matmul(ps[p][:, c, 0:D], ft[p][:, c * P:(c + 1) * P], wt[:, :],
                                                    start=True, stop=True)
                        last.then_inc(mm, 1)
                turns(pe, GROUPS // 2, body)

            @block.vector
            def _(v):
                nc.vector.memset(zero[:, :], 0.0).then_inc(zero_ok, 1)

                def finish(p, n):
                    for w in range(2):
                        v.wait_ge(relued, (n - 1) * 2 + w + 1)
                        step(v, nc.vector.tensor_tensor(prod[w][p][:, :, :], qk[w][p][:, :, 0:D],
                                                        qk[w][p][:, :, D:2 * D], ALU.mult), prod_ok, (n - 1) * 2 + w + 1)
                        nc.vector.tensor_reduce(msg[w][p][:, :, D:MSG_W],
                                                prod[w][p][:, :, :].rearrange("p c (h f) -> p c h f", h=HEADS),
                                                X, ALU.add).then_inc(msg_ok, 1)

                def body(i):
                    for p in range(2):
                        n = i * 2 + p + 1
                        v.wait_ge(mm, n)
                        v.wait_ge(got[p], (i + 1) * GOT)
                        if not first(i):
                            v.wait_ge(put[p], i * GOT)
                            v.wait_ge(msg_ok, (n - 2) * 2)
                        for w in range(2):
                            nc.vector.tensor_tensor(qk[w][p][:, :, 0:D], ps[p][:, :, 0:D], rows[w][p][:, :, 0:D],
                                                    ALU.add).then_inc(added, 1)
                            nc.vector.tensor_tensor(qk[w][p][:, :, D:2 * D], ps[p][:, :, D:2 * D],
                                                    rows[1 - w][p][:, :, D:2 * D], ALU.add).then_inc(added, 1)
                        for w in range(2):
                            nc.vector.tensor_tensor(msg[w][p][:, :, 0:D], ps[p][:, :, 2 * D:3 * D],
                                                    rows[1 - w][p][:, :, 2 * D:3 * D], ALU.add).then_inc(v_ok, 1)
                        for w in range(2):
                            at = ds(i * (2 * CG) + p * CG, CG)
                            nc.vector.tensor_tensor(to[w][p][:, :], m.rank[:, w, at], rows[w][p][:, :, 3 * D + w],
                                                    ALU.add).then_inc(to_ok, 1)
                        finish(p, n)
                turns(v, GROUPS // 2, body)

            @block.scalar
            def _(act):
                def body(i):
                    for p in range(2):
                        n = i * 2 + p + 1
                        for w in range(2):
                            act.wait_ge(added, (n - 1) * 4 + 2 * w + 2)
                            nc.scalar.activation(qk[w][p][:, :, :], qk[w][p][:, :, :], ACT.Relu).then_inc(relued, 1)
                turns(act, GROUPS // 2, body)


def l1_edges_ordered(nc, d, m):
    ctx, sb, pb, sem = scope(nc, "edgeso")
    R, AH = 4, 2
    with ctx:
        wt, we = sb("wt", [DE, D]), sb("we", [P, 2 * D])
        idx = [sb(f"idx{p}", [P, CG], i32) for p in range(R)]
        ft = [sb(f"ft{p}", [DE, GE]) for p in range(R)]
        fe = [sb(f"fe{p}", [P, GE]) for p in range(R)]
        target = [sb(f"target{p}", [P, GE], u16) for p in range(R)]
        win = [sb(f"win{p}", [P, 3 * D]) for p in range(R)]
        pick = [sb(f"pick{p}", [P, GE]) for p in range(R)]
        rows = [sb(f"rows{p}", [P, CG, TN_W]) for p in range(R)]
        fs = [sb(f"fs{p}", [P, CG, 2 * D]) for p in range(2)]
        ftr = [sb(f"ftr{p}", [P, CG, 2 * D]) for p in range(2)]
        prod = sb("prod", [P, CG, 2 * D])
        msg = [[sb(f"msg{w}{p}", [P, CG, MSG_W]) for p in range(R)] for w in range(2)]
        to = [sb(f"to{p}", [P, CG], i32) for p in range(R)]
        zero = sb("zero", [SLOTS, MSG_W])
        ps = [pb(f"ps{p}", [P, CG, BANK]) for p in range(2)]
        (w_in, picked, mm, added, sv_ok, to_ok, joined, cut, tv_ok, prod_ok, msg_ok, passed, passed_sp, zero_ok,
         zero_out) = (
            sem(x) for x in ("w_in", "picked", "mm", "added", "sv_ok", "to_ok", "joined", "cut", "tv_ok", "prod_ok",
                             "msg_ok", "passed", "passed_sp", "zero_ok", "zero_out"))
        idx_in, f_in, t_in, got, put, stored = (
            [sem(f"{x}{p}") for p in range(R)] for x in ("idx_in", "f_in", "t_in", "got", "put", "stored"))
        GOT = CG * 16
        T = GROUPS // R
        with nc.Block() as block:
            @block.sync
            def _(sp):
                sp.dma_start(wt[:, :], d.wt).then_inc(w_in, 16)
                sp.dma_start(we[:, :], d.we).then_inc(w_in, 16)
                sp.wait_ge(zero_ok, 1)
                for w in range(2):
                    sp.dma_start(d.msg_of[w][EP:EP + SLOTS, :], zero[:, :]).then_inc(zero_out, 16)

                def body(i):
                    for p in range(R):
                        n = i * R + p + 1
                        if not first(i):
                            sp.wait_ge(got[p], i * GOT)
                        sp.dma_start(idx[p][:, :], d.idx[ds(n - 1, 1), :, 0:CG].rearrange("a p c -> (a p) c")
                                     ).then_inc(idx_in[p], 16)
                        if not first(i):
                            sp.wait_ge(picked, n - R)
                        sp.dma_start(target[p][:, :],
                                     d.rowf[1, 0, ds(i * (R * GE) + p * GE, GE)].partition_broadcast(P)
                                     ).then_inc(t_in[p], 16)
                        if not first(i):
                            hold(sp, mm, n - R, passed_sp)
                        sp.dma_start(ft[p][:, :], d.ft[:, ds(i * (R * GE) + p * GE, GE)]).then_inc(f_in[p], 16)
                        sp.dma_start(fe[p][:, :], d.fe[:, ds(i * (R * GE) + p * GE, GE)]).then_inc(f_in[p], 16)
                        if not first(i):
                            hold(sp, joined, n - R, passed_sp)
                        base = sp.value_load(m.bases[0:1, ds(n - 1, 1)], min_val=0, max_val=N)
                        sp.dma_start(win[p][:, :], d.tn[ds(base, P), 0:3 * D]).then_inc(f_in[p], 16)
                turns(sp, T, body)
                sp.wait_ge(zero_out, 32)

            @block.gpsimd
            def _(g):
                def gather(i, p, n):
                    hold(g, idx_in[p], i * 16 + 16, passed)
                    if not first(i):
                        hold(g, to_ok, n - R, passed)
                    for c in range(CG):
                        g.indirect_dma_start(rows[p][:, c, :], None, d.tn, bass.IndirectOffsetOnAxis(
                            ap=idx[p][:, c:c + 1], axis=0)).then_inc(got[p], 16)

                def scatter(p, n):
                    hold(g, msg_ok, n * 2, passed)
                    hold(g, tv_ok, n, passed)
                    for c in range(CG):
                        g.indirect_dma_start(d.msg_of[0], bass.IndirectOffsetOnAxis(
                            ap=to[p][:, c:c + 1], axis=0), msg[0][p][:, c, :], None).then_inc(put[p], 16)

                def body(i):
                    for p in range(R):
                        n = i * R + p + 1
                        gather(i, p, n)
                        if not (first(i) and p < AH):
                            scatter((p - AH) % R, n - AH)
                turns(g, T, body)
                for n in range(GROUPS - AH, GROUPS):
                    scatter(n % R, n + 1)
                for p in range(R):
                    g.wait_ge(put[p], GOT * T)

            @block.tensor
            def _(pe):
                pe.wait_ge(w_in, 32)

                def join(p, n):
                    pe.wait_ge(picked, n)
                    pe.wait_ge(sv_ok, n)
                    for c in range(CG):
                        last = nc.tensor.matmul(ps[p % 2][:, c, 0:3 * D], pick[p][:, c * P:(c + 1) * P], win[p][:, :],
                                                start=False, stop=True, skip_group_check=True)
                    last.then_inc(joined, 1)

                def body(i):
                    for p in range(R):
                        n = i * R + p + 1
                        pe.wait_ge(f_in[p], i * 48 + 48)
                        if not (first(i) and p < 2):
                            pe.wait_ge(tv_ok, n - 2)
                        for c in range(CG):
                            nc.tensor.matmul(ps[p % 2][:, c, 0:D], ft[p][:, c * P:(c + 1) * P], wt[:, :],
                                             start=True, stop=False, skip_group_check=True)
                            last = nc.tensor.matmul(ps[p % 2][:, c, D:3 * D], fe[p][:, c * P:(c + 1) * P], we[:, :],
                                                    start=False, stop=False, skip_group_check=True)
                        last.then_inc(mm, 1)
                        if not (first(i) and p == 0):
                            join((p - 1) % R, n - 1)
                turns(pe, T, body)
                join(R - 1, GROUPS)

            @block.vector
            def _(v):
                nc.vector.memset(zero[:, :], 0.0).then_inc(zero_ok, 1)

                def finish(p, n):
                    v.wait_ge(cut, n * 2)
                    step(v, nc.vector.scalar_tensor_tensor(prod[:, :, :], fs[p % 2][:, :, :], 0.0, ftr[p % 2][:, :, :],
                                                           ALU.max, ALU.mult), prod_ok, n)
                    for w in range(2):
                        nc.vector.tensor_reduce(msg[w][p][:, :, D:MSG_W],
                                                prod[:, :, w * D:(w + 1) * D].rearrange("p c (h f) -> p c h f", h=HEADS),
                                                X, ALU.add).then_inc(msg_ok, 1)
                    v.wait_ge(msg_ok, n * 2)

                def body(i):
                    for p in range(R):
                        n = i * R + p + 1
                        v.wait_ge(t_in[p], i * 16 + 16)
                        if not first(i):
                            v.wait_ge(joined, n - R)
                        nc.vector.tensor_scalar(pick[p][:, :], target[p][:, :], m.window[:, ds(n - 1, 1)], None,
                                                ALU.is_equal).then_inc(picked, 1)
                        if not (first(i) and p == 0):
                            finish((p - 1) % R, n - 1)
                        v.wait_ge(mm, n)
                        v.wait_ge(got[p], i * GOT + GOT)
                        if not first(i):
                            v.wait_ge(put[p], i * GOT)
                            v.wait_ge(stored[p], i * 16)
                        nc.vector.tensor_tensor(fs[p % 2][:, :, :], ps[p % 2][:, :, 0:2 * D], rows[p][:, :, 0:2 * D],
                                                ALU.add).then_inc(added, 1)
                        nc.vector.tensor_tensor(msg[1][p][:, :, 0:D], ps[p % 2][:, :, 2 * D:3 * D],
                                                rows[p][:, :, 2 * D:3 * D], ALU.add).then_inc(sv_ok, 1)
                        nc.vector.tensor_tensor(to[p][:, :], m.rank[:, 0, ds(i * (R * CG) + p * CG, CG)],
                                                rows[p][:, :, 3 * D], ALU.add).then_inc(to_ok, 1)
                        v.wait_ge(added, n)
                turns(v, T, body)
                finish(R - 1, GROUPS)

            @block.scalar
            def _(act):
                def store(i, p, n):
                    act.wait_ge(msg_ok, n * 2)
                    act.dma_start(d.msg_of[1][ds((n - 1) * GE, GE), :].rearrange("(p c) f -> p c f", c=CG),
                                  msg[1][p][:, :, :]).then_inc(stored[p], 16)

                def body(i):
                    for p in range(R):
                        n = i * R + p + 1
                        act.wait_ge(joined, n)
                        if not (first(i) and p < 2):
                            act.wait_ge(prod_ok, n - 2)
                        for half in range(2):
                            nc.scalar.activation(ftr[p % 2][:, :, half * D:(half + 1) * D],
                                                 ps[p % 2][:, :, (1 - half) * D:(2 - half) * D],
                                                 ACT.Relu).then_inc(cut, 1)
                        if not first(i):
                            act.wait_ge(put[p], i * GOT)
                        nc.scalar.activation(msg[0][p][:, :, 0:D], ps[p % 2][:, :, 2 * D:3 * D], ACT.Copy
                                             ).then_inc(tv_ok, 1)
                        if not (first(i) and p == 0):
                            store(i, (p - 1) % R, n - 1)
                turns(act, T, body)
                store(T, R - 1, GROUPS)
                for p in range(R):
                    act.wait_ge(stored[p], 16 * T)


def l1_softmax(nc, d, m):
    ctx, sb, pb, sem = scope(nc, "soft")
    with ctx:
        R = SOFT_RING
        run = [sb(f"run{p}", [P, 2, SLOTS, MSG_W]) for p in range(R)]
        at_f, at_c, left = ([sb(f"{x}{p}", [P, 2]) for p in range(R)] for x in ("at_f", "at_c", "left"))
        at = [sb(f"at{p}", [P, 2], i32) for p in range(R)]
        off = [sb(f"off{p}", [P, 2, SLOTS]) for p in range(R)]
        score = [sb(f"score{p}", [P, 2 * SLOTS, HEADS]) for p in range(R)]
        under = [sb(f"under{p}", [P, 2 * SLOTS, HEADS]) for p in range(R)]
        w = [sb(f"w{p}", [P, 2 * SLOTS, HEADS]) for p in range(R)]
        most, top, fall, corr, wsum, den = ([sb(f"{x}{p}", [P, HEADS]) for p in range(R)]
                                            for x in ("most", "top", "fall", "corr", "wsum", "den"))
        prod = sb("prod", [P, 2 * SLOTS, D])
        part = [sb(f"part{p}", [P, D]) for p in range(R)]
        old = [sb(f"old{p}", [P, D]) for p in range(R)]
        passed_slots = sb("passed_slots", [P, 2])
        got = [sem(f"got{p}") for p in range(R)]
        (at_f_ok, at_c_ok, at_ok, left_ok, off_ok, score_ok, most_ok, top_ok, under_ok, w_ok, wsum_ok, den_ok,
         prod_ok, part_ok, old_ok, summed, passed, slots_ok) = (
            sem(x) for x in ("at_f_ok", "at_c_ok", "at_ok", "left_ok", "off_ok", "score_ok", "most_ok", "top_ok",
                             "under_ok", "w_ok", "wsum_ok", "den_ok", "prod_ok", "part_ok", "old_ok", "summed",
                             "passed", "slots_ok"))
        with nc.Block() as block:
            @block.vector
            def _(v):
                rounds = v.value_load(m.trips[0:1, 2:3], min_val=1, max_val=EP // SLOTS + 1)
                step(v, nc.vector.memset(passed_slots[:, :], 0.0), slots_ok, 1)

                def aim(n, b, p):
                    step(v, nc.vector.tensor_tensor(at_f[p][:, :], m.place[:, ds(b, 1), :].rearrange("p a w -> p (a w)"),
                                                    passed_slots[:, :], ALU.add), at_f_ok, n)
                    step(v, nc.vector.tensor_scalar(at_c[p][:, :], at_f[p][:, :], float(EP), float(MSG_W), ALU.min,
                                                    ALU.mult), at_c_ok, n)
                    nc.vector.tensor_copy(at[p][:, :], at_c[p][:, :]).then_inc(at_ok, 1)

                for b in range(AHEAD):
                    aim(b + 1, b, b)
                with v.Fori(0, rounds) as r:
                    with v.Fori(0, NB // R) as j:
                        for p in range(R):
                            n = r * NB + j * R + p + 1
                            b = j * R + p
                            state_top = m.top[:, ds(b, 1), :].rearrange("p a h -> p (a h)")
                            state_den = m.den[:, ds(b, 1), :].rearrange("p a h -> p (a h)")
                            state_sum = m.agg[:, ds(b, 1), :].rearrange("p a f -> p (a f)")
                            aim(n + AHEAD, b + AHEAD, (p + AHEAD) % R)
                            step(v, nc.vector.tensor_tensor(left[p][:, :], m.deg[:, :, ds(b, 1)].rearrange("p w a -> p (w a)"),
                                                            passed_slots[:, :], ALU.subtract), left_ok, n)
                            for x in range(2):
                                nc.vector.tensor_scalar(off[p][:, x, :], m.iota_row[:, 0:SLOTS], left[p][:, x:x + 1],
                                                        NEG, ALU.is_ge, ALU.mult).then_inc(off_ok, 1)
                            v.wait_ge(off_ok, n * 2)
                            v.wait_ge(got[p], r * (NB // R * 32) + j * 32 + 32)
                            slots = run[p][:, :, :, :].rearrange("p x s f -> p (x s) f")
                            step(v, nc.vector.tensor_tensor(
                                score[p][:, :, :], slots[:, :, D:MSG_W],
                                off[p][:, :, :].rearrange("p x s -> p (x s)").unsqueeze(2)
                                .to_broadcast([P, 2 * SLOTS, HEADS]), ALU.add), score_ok, n)
                            step(v, nc.vector.tensor_reduce(most[p][:, :], score[p][:, :, :].rearrange("p s h -> p h s"),
                                                            X, ALU.max), most_ok, n)
                            step(v, nc.vector.tensor_tensor(top[p][:, :], most[p][:, :], state_top, ALU.max), top_ok, n)
                            nc.vector.tensor_tensor(fall[p][:, :], state_top, top[p][:, :], ALU.subtract
                                                    ).then_inc(under_ok, 1)
                            nc.vector.tensor_tensor(under[p][:, :, :], score[p][:, :, :],
                                                    top[p][:, :].unsqueeze(1).to_broadcast([P, 2 * SLOTS, HEADS]),
                                                    ALU.subtract).then_inc(under_ok, 1)
                            v.wait_ge(w_ok, n * 2)
                            nc.vector.tensor_scalar(state_top, top[p][:, :], 0.0, None, ALU.add)
                            nc.vector.tensor_reduce(wsum[p][:, :], w[p][:, :, :].rearrange("p s h -> p h s"),
                                                    X, ALU.add).then_inc(wsum_ok, 1)
                            step(v, nc.vector.tensor_tensor(den[p][:, :], state_den, corr[p][:, :], ALU.mult), den_ok, n * 2 - 1)
                            v.wait_ge(wsum_ok, n)
                            nc.vector.tensor_tensor(state_den, den[p][:, :], wsum[p][:, :], ALU.add).then_inc(den_ok, 1)
                            nc.vector.tensor_tensor(
                                prod[:, :, :].rearrange("p s (h f) -> p s h f", h=HEADS),
                                slots[:, :, 0:D].rearrange("p s (h f) -> p s h f", h=HEADS),
                                w[p][:, :, :].unsqueeze(3).to_broadcast([P, 2 * SLOTS, HEADS, DK]),
                                ALU.mult).then_inc(prod_ok, 1)
                            nc.vector.tensor_tensor(
                                old[p][:, :].rearrange("p (h f) -> p h f", h=HEADS),
                                state_sum.rearrange("p (h f) -> p h f", h=HEADS),
                                corr[p][:, :].unsqueeze(2).to_broadcast([P, HEADS, DK]), ALU.mult).then_inc(old_ok, 1)
                            v.wait_ge(prod_ok, n)
                            step(v, nc.vector.tensor_reduce(part[p][:, :], prod[:, :, :].rearrange("p s f -> p f s"),
                                                            X, ALU.add), part_ok, n)
                            v.wait_ge(old_ok, n)
                            step(v, nc.vector.tensor_tensor(state_sum, old[p][:, :], part[p][:, :], ALU.add), summed, n)
                    step(v, nc.vector.tensor_scalar(passed_slots[:, :], passed_slots[:, :], float(SLOTS), None,
                                                    ALU.add), slots_ok, r + 2)

            @block.scalar
            def _(act):
                rounds = act.value_load(m.trips[0:1, 2:3], min_val=1, max_val=EP // SLOTS + 1)
                with act.Fori(0, rounds) as r:
                    with act.Fori(0, NB // R) as j:
                        for p in range(R):
                            n = r * NB + j * R + p + 1
                            act.wait_ge(under_ok, n * 2)
                            nc.scalar.activation(corr[p][:, :], fall[p][:, :], ACT.Exp, scale=SCALE).then_inc(w_ok, 1)
                            nc.scalar.activation(w[p][:, :, :], under[p][:, :, :], ACT.Exp, scale=SCALE
                                                 ).then_inc(w_ok, 1)

            @block.gpsimd
            def _(g):
                rounds = g.value_load(m.trips[0:1, 2:3], min_val=1, max_val=EP // SLOTS + 1)

                def fetch(n, p):
                    hold(g, at_ok, n, passed)
                    for x in range(2):
                        flat = d.msg_of[x].rearrange("n f -> (n f)").rearrange("(n o) -> n o", o=1)
                        g.indirect_dma_start(run[p][:, x, :, :].rearrange("p s f -> p (s f)"), None, flat,
                                             bass.IndirectOffsetOnAxis(ap=at[p][:, x:x + 1], axis=0)
                                             ).then_inc(got[p], 16)

                for b in range(AHEAD):
                    fetch(b + 1, b)
                with g.Fori(0, rounds) as r:
                    with g.Fori(0, NB // R) as j:
                        for p in range(R):
                            fetch(r * NB + j * R + p + 1 + AHEAD, (p + AHEAD) % R)
                for p in range(AHEAD):
                    g.wait_ge(got[p], rounds * (NB // R * 32) + 32)


def l1_out(nc, d, m):
    ctx, sb, pb, sem = scope(nc, "out")
    R = 2
    with ctx:
        wa, wb, w2, b2 = sb("wa", [P, D]), sb("wb", [P, D]), sb("w2", [P, D]), sb("b2", [P, D])
        inv = sb("inv", [P, NB, HEADS])
        x1 = [sb(f"x1{k}", [P, D]) for k in range(R)]
        emb, embT, x1T, hid, x1b, z, cent, out = ([sb(f"{x}{k}", [P, D]) for k in range(R)]
                                             for x in ("emb", "embT", "x1T", "hid", "x1b", "z", "cent", "out"))
        st = [sb(f"st{k}", [P, 6]) for k in range(R)]
        mv = [sb(f"mv{k}", [P, 2]) for k in range(R)]
        vpe, root, rinv = ([sb(f"{x}{k}", [P, 1]) for k in range(R)] for x in ("vpe", "root", "rinv"))
        ps_t = [pb(f"ps_t{k}", [P, 2, D]) for k in range(R)]
        ps_h = [pb(f"ps_h{k}", [P, D]) for k in range(R)]
        ps_y = [pb(f"ps_y{k}", [P, D]) for k in range(R)]
        (w_in, inv_ok, emb_ok, turned, copied, mm_h, hid_ok, mm_y, x1b_ok, z_ok, st_ok, mv_ok, vpe_ok, root_ok,
         rinv_ok, out_ok, passed) = (
            sem(x) for x in ("w_in", "inv_ok", "emb_ok", "turned", "copied", "mm_h", "hid_ok", "mm_y", "x1b_ok",
                             "z_ok", "st_ok", "mv_ok", "vpe_ok", "root_ok", "rinv_ok", "out_ok", "passed"))
        x1_in = [sem(f"x1_in{k}") for k in range(R)]
        stored = [sem(f"stored{k}") for k in range(R)]
        with nc.Block() as block:
            @block.sync
            def _(sp):
                sp.dma_start(wa[:, :], d.l1_w1[0:D, :]).then_inc(w_in, 16)
                sp.dma_start(wb[:, :], d.l1_w1[D:2 * D, :]).then_inc(w_in, 16)
                sp.dma_start(w2[:, :], d.l1_w2).then_inc(w_in, 16)
                sp.dma_start(b2[:, :], d.l1_b2.partition_broadcast(P)).then_inc(w_in, 16)

                def body(i):
                    for k in range(R):
                        if not first(i):
                            sp.wait_ge(x1b_ok, i * R - R + k + 1)
                            sp.wait_ge(turned, i * R - R + k + 1)
                        sp.dma_start(x1[k][:, :], d.x1[ds(i * (R * P) + k * P, P), :]).then_inc(x1_in[k], 16)
                turns(sp, NB // R, body)
                for k in range(R):
                    sp.wait_ge(stored[k], 16 * (NB // R))

            @block.tensor
            def _(pe):
                pe.wait_ge(w_in, 64)

                def body(i):
                    for k in range(R):
                        n = i * R + k + 1
                        pe.wait_ge(x1_in[k], i * 16 + 16)
                        if not first(i):
                            pe.wait_ge(copied, (n - R) * 2)
                        nc.tensor.transpose(ps_t[k][:, 1, :], x1[k][:, :], m.ident[:, :])
                        pe.wait_ge(emb_ok, n)
                        nc.tensor.transpose(ps_t[k][:, 0, :], emb[k][:, :], m.ident[:, :]).then_inc(turned, 1)
                        pe.wait_ge(copied, n * 2)
                        if not first(i):
                            pe.wait_ge(hid_ok, n - R)
                        nc.tensor.matmul(ps_h[k][:, :], wa[:, :], embT[k][:, :], start=True, stop=False)
                        nc.tensor.matmul(ps_h[k][:, :], wb[:, :], x1T[k][:, :], start=False, stop=True).then_inc(mm_h, 1)
                        pe.wait_ge(hid_ok, n)
                        if not first(i):
                            pe.wait_ge(z_ok, n - R)
                        nc.tensor.matmul(ps_y[k][:, :], hid[k][:, :], w2[:, :], start=True, stop=True).then_inc(mm_y, 1)
                turns(pe, NB // R, body)

            @block.scalar
            def _(act):
                def body(i):
                    for k in range(R):
                        n = i * R + k + 1
                        act.wait_ge(turned, n)
                        if not first(i):
                            act.wait_ge(mm_h, n - R)
                        nc.scalar.activation(embT[k][:, :], ps_t[k][:, 0, :], ACT.Copy).then_inc(copied, 1)
                        nc.scalar.activation(x1T[k][:, :], ps_t[k][:, 1, :], ACT.Copy).then_inc(copied, 1)
                        act.wait_ge(mm_h, n)
                        if not first(i):
                            act.wait_ge(mm_y, n - R)
                        nc.scalar.activation(hid[k][:, :], ps_h[k][:, :], ACT.Relu, bias=m.cols[:, 5:6]
                                             ).then_inc(hid_ok, 1)
                        act.wait_ge(vpe_ok, n)
                        nc.scalar.activation(root[k][:, :], vpe[k][:, :], ACT.Sqrt).then_inc(root_ok, 1)
                        act.wait_ge(out_ok, n)
                        act.dma_start(d.out[ds((n - 1) * P, P), :], out[k][:, :]).then_inc(stored[k], 16)
                turns(act, NB // R, body)

            @block.vector
            def _(v):
                v.wait_ge(w_in, 64)
                step(v, nc.vector.reciprocal(inv[:, :, :], m.den[:, :, :]), inv_ok, 1)

                def embed(i, k, n):
                    nc.vector.tensor_tensor(
                        emb[k][:, :].rearrange("p (h f) -> p h f", h=HEADS),
                        m.agg[:, ds(n - 1, 1), :].rearrange("p a (h f) -> p (a h) f", h=HEADS),
                        inv[:, ds(n - 1, 1), :].rearrange("p a h -> p (a h)").unsqueeze(2)
                        .to_broadcast([P, HEADS, DK]), ALU.mult).then_inc(emb_ok, 1)

                def body(i):
                    for k in range(R):
                        n = i * R + k + 1
                        if not first(i):
                            v.wait_ge(turned, n - R)
                        embed(i, k, n)
                        v.wait_ge(x1_in[k], i * 16 + 16)
                        step(v, nc.vector.tensor_tensor(x1b[k][:, :], x1[k][:, :], b2[:, :], ALU.add), x1b_ok, n)
                        v.wait_ge(mm_y, n)
                        step(v, nc.vector.tensor_tensor(z[k][:, :], x1b[k][:, :], ps_y[k][:, :], ALU.add), z_ok, n)
                        nc.vector.bn_stats(st[k][:, :], z[k][:, :]).then_inc(st_ok, 1)
                        hold(v, st_ok, n, passed)
                        step(v, nc.vector.bn_aggr(mv[k][:, :], st[k][:, :]), mv_ok, n)
                        nc.vector.tensor_scalar(vpe[k][:, :], mv[k][:, 1:2], EPS, None, ALU.add).then_inc(vpe_ok, 1)
                        v.wait_ge(root_ok, n)
                        if not first(i):
                            v.wait_ge(stored[k], i * 16)
                        step(v, nc.vector.reciprocal(rinv[k][:, :], root[k][:, :]), rinv_ok, n)
                        nc.vector.tensor_scalar(out[k][:, :], z[k][:, :], mv[k][:, 0:1], rinv[k][:, 0:1], ALU.subtract,
                                                ALU.mult).then_inc(out_ok, 1)
                turns(v, NB // R, body)


def build(nc, d):
    ctx = ExitStack()
    with ctx:
        def keep(name, shape, dt=f32):
            return ctx.enter_context(nc.sbuf_tensor(name, shape, dt))
        m = Names()
        m.iota_row, m.iota_p, m.ones = keep("iota_row", [P, P]), keep("iota_p", [P, 1]), keep("ones", [P, P])
        m.ident, m.before, m.after = keep("ident", [P, P]), keep("before", [P, P]), keep("after", [P, P])
        m.real, m.cols = keep("real", [P, NB]), keep("cols", [P, 6])
        m.w2t, m.w2ts, m.row2 = keep("w2t", [P, D]), keep("w2ts", [P, D]), keep("row2", [P, D])
        m.selfadd = keep("selfadd", [P, 3 * D])
        m.key, m.lo, m.hi = (keep(x, [P, 2, EP // P]) for x in ("key", "lo", "hi"))
        m.rank, m.where_t = keep("rank", [P, 2, EP // P]), keep("where_t", [P, EP // P])
        m.count, m.deg, m.place = keep("count", [P, 2, NB]), keep("deg", [P, 2, NB]), keep("place", [P, NB + AHEAD, 2])
        m.visits, m.trips = keep("visits", [P, 3], i32), keep("trips", [P, 3], i32)
        m.mv1, m.mv2 = keep("mv1", [P, 2]), keep("mv2", [P, 2])
        m.scale1, m.shift1 = keep("scale1", [P, 1]), keep("shift1", [P, 1])
        m.scale2, m.shift2 = keep("scale2", [P, 1]), keep("shift2", [P, 1])
        m.agg, m.top, m.den = keep("agg", [P, NB, D]), keep("top", [P, NB, HEADS]), keep("den", [P, NB, HEADS])
        m.bases, m.ordered = keep("bases", [1, GROUPS], i32), keep("ordered", [P, 1], i32)
        m.window = keep("window", [P, GROUPS])
        m.inside = keep("inside", [P, EP // P])
        setup(nc, d, m)

        def ordered():
            return nc.values_load(m.ordered[0:1, 0:1], min_val=0, max_val=1) > 0

        with nc.If(ordered()):
            l0_tables(nc, d, m, False, "tab0o")
            l0_first_ordered(nc, d, m)
        with nc.Else():
            rank_targets(nc, d, m)
            places(nc, d, m, 1, "places_t")
            l0_tables(nc, d, m, True, "tab0")
            l0_first(nc, d, m)
        places(nc, d, m, 0, "places_s")
        norm_terms(nc, m, m.mv1, m.cols[:, 0:1], m.cols[:, 1:2], m.scale1, m.shift1, "norm_a")
        l0_second(nc, d, m)
        norm_terms(nc, m, m.mv2, m.cols[:, 2:3], m.cols[:, 3:4], m.scale2, m.shift2, "norm_b")
        fold_second(nc, d, m)
        with nc.If(ordered()):
            l0_third_ordered(nc, d, m)
            places(nc, d, m, 1, "places_o")
        with nc.Else():
            l0_third(nc, d, m)
            l0_gather(nc, d, m)
        layer_norm(nc, d, m)
        l1_self_terms(nc, d, m)
        l1_tables(nc, d, m)
        with nc.If(ordered()):
            l1_edges_ordered(nc, d, m)
        with nc.Else():
            l1_edges(nc, d, m)
        l1_softmax(nc, d, m)
        l1_out(nc, d, m)


def kernel(**inputs):
    import numpy as np
    import concourse.bacc as bacc
    from concourse.bass_utils import run_bass_kernel_spmd

    a = {k: np.asarray(v) for k, v in inputs.items()}

    def rows_to(x, n, fill=0):
        return np.concatenate([x, np.full((n - x.shape[0],) + x.shape[1:], fill, x.dtype)])

    x = rows_to(a["x"], NP_)
    src, dst = rows_to(a["src"], EP, PAD), rows_to(a["dst"], EP, PAD)
    by_chunk = [k.reshape(GROUPS, P, CG).transpose(1, 0, 2).reshape(P, -1) for k in (src, dst)]

    def chunked(x):
        return x.reshape(-1, GROUPS, P, CG).transpose(0, 1, 3, 2).reshape(x.shape)

    ef, tf, et = (chunked(rows_to(a[k], EP).T) for k in ("edge_attr_64", "edge_attr_64_n2", "edge_attr_64_n3"))
    w1 = a["L0_gnn_W1"]
    wq, wk, wv = a["L1_gnn_Wq"], a["L1_gnn_Wk"], a["L1_gnn_Wv"]
    nc = bacc.Bacc("TRN2", target_bir_lowering=False, num_devices=1)
    arrays = {}

    def given(name, v):
        arrays[name] = np.ascontiguousarray(v)
        return nc.dram_tensor(name, v.shape, mybir.dt.from_np(v.dtype), kind="ExternalInput").ap()

    def scratch(name, *shape):
        return nc.dram_tensor(name, shape, f32, kind="Internal").ap()

    d = Names()
    d.x, d.xT = given("in_x", x), given("in_xT", x.T)
    d.idx = given("in_idx", np.concatenate([k.reshape(GROUPS, P, CG) for k in (src, dst)], axis=2))
    d.keys = given("in_keys", np.stack(by_chunk, axis=1))
    d.key_rows = given("in_key_rows", np.stack([chunked(k).reshape(P, -1) for k in (src, dst)], axis=1))
    d.now = given("in_now", dst.reshape(P, -1))
    d.then = given("in_then", rows_to(dst[1:], EP, PAD).reshape(P, -1))
    d.ends = given("in_ends", np.stack([dst[::GE], dst[GE - 1::GE]]))
    d.ft, d.fe = given("in_ft", tf), given("in_fe", np.concatenate([ef, et]))
    d.time0 = given("in_time0", a["edge_attr_64_n2"][0:1].T)
    d.w1 = given("in_w1", np.concatenate([w1[:, :D].T, w1[:, D:].T], axis=1))
    d.b1 = given("in_b1", a["L0_gnn_b1"])
    d.w2, d.w2t = given("in_w2", a["L0_gnn_W2"]), given("in_w2t", a["L0_gnn_W2"].T)
    d.cols = given("in_cols", np.stack([a[k] for k in ("L0_gnn_g1", "L0_gnn_be1", "L0_gnn_g2", "L0_gnn_be2",
                                                       "L0_gnn_b2", "L1_gnn_b1")], axis=1))
    d.wx = given("in_wx", np.concatenate([w[:D] for w in (wq, wk, wv)], axis=1))
    d.bx = given("in_bx", np.concatenate([a[k] for k in ("L1_gnn_bq", "L1_gnn_bk", "L1_gnn_bv")]))
    d.wt, d.we = given("in_wt", wq[D:]), given("in_we", np.concatenate([wk[D:], wv[D:]], axis=1))
    d.l1_w1, d.l1_w2 = given("in_l1_w1", a["L1_gnn_W1"]), given("in_l1_w2", a["L1_gnn_W2"])
    d.l1_b2 = given("in_l1_b2", a["L1_gnn_b2"])
    d.ta, d.tb, d.tn = scratch("ta", NP_, D), scratch("tb", NP_, TB_W), scratch("tn", NP_, TN_W)
    d.rowf = nc.dram_tensor("rowf", (2, 2, EP), u16, kind="Internal").ap()
    d.h1, d.up, d.x1 = scratch("h1", D, EP), scratch("up", EP + SLOTS, D), scratch("x1", NP_, D)
    d.msg_of = [scratch("msg_s", EP + SLOTS, MSG_W), scratch("msg_t", EP + SLOTS, MSG_W)]
    d.out = nc.dram_tensor("out", (NP_, D), f32, kind="ExternalOutput").ap()
    build(nc, d)
    r = run_bass_kernel_spmd(nc, [arrays], core_ids=[0])
    return r.results[0]["out"][:N]
```

```python
import math
from contextlib import ExitStack

import concourse.bass as bass
from concourse import mybir

P = 128
N, E, D, DE = 6250, 100000, 128, 64
HEADS = 2
DK = D // HEADS
SCALE = DK ** -0.5
EPS = 1e-5
CG = 4
GE = CG * P
GROUPS = 4 * -(-E // (4 * GE))
EP = GROUPS * GE
LAST = E - (GROUPS - 1) * GE
NB = 2 * -(-(N + 1) // (2 * P))
NP_ = NB * P
SLOTS = 16
SOFT_RING, AHEAD = 5, 3
PAD = N
TB_W = D + 1
TN_W = 3 * D + 2
MSG_W = D + HEADS
NEG = -1.0e30
BANK = 512

f32, bf16, i32, u16 = mybir.dt.float32, mybir.dt.bfloat16, mybir.dt.int32, mybir.dt.uint16
ALU = mybir.AluOpType
ACT = mybir.ActivationFunctionType
X = mybir.AxisListType.X
ds = bass.ds


class Names:
    pass


def turns(eng, count, body):
    body(0)
    if count > 1:
        with eng.Fori(1, count) as i:
            body(i)


def first(i):
    return isinstance(i, int) and i == 0


def step(eng, ins, sem, count):
    ins.then_inc(sem, 1)
    eng.wait_ge(sem, count)


def real_part(columns):
    return columns.rearrange("f (c p) -> f c p", c=CG)[:, :, 0:LAST // CG]


def hold(eng, sem, value, passed):
    eng.wait_ge(sem, value)
    eng.sem_inc(passed, 1)


def scope(nc, tag):
    ctx = ExitStack()

    def sb(name, shape, dt=f32):
        return ctx.enter_context(nc.sbuf_tensor(f"{tag}_{name}", shape, dt))

    def pb(name, shape):
        size = math.prod(shape[1:])
        whole = ctx.enter_context(nc.psum_tensor(f"{tag}_{name}", [shape[0], -(-size // BANK) * BANK], f32))
        if len(shape) == 2:
            return whole[:, 0:size]
        return whole[:, 0:size].rearrange("p (a b) -> p a b", b=shape[2])

    sems = []

    def sem(name):
        sems.append(nc.alloc_semaphore(f"{tag}_{name}"))
        return sems[-1]

    ctx.callback(nc.all_engine_barrier)
    ctx.callback(lambda: nc.clear_and_free_semaphores(sems))
    return ctx, sb, pb, sem


def setup(nc, d, m):
    ctx, sb, pb, sem = scope(nc, "setup")
    with ctx:
        keys, lows, highs = (sb(x, [P, 2, EP // P], i32) for x in ("keys", "lows", "highs"))
        rows, row_lows = (sb(x, [P, 2, EP // P], i32) for x in ("rows", "row_lows"))
        rowf = sb("rowf", [P, 2, 2, EP // P], u16)
        now, then = sb("now", [P, EP // P], i32), sb("then", [P, EP // P], i32)
        ends = sb("ends", [P, 2, GROUPS], i32)
        falls, span, wide = sb("falls", [P, EP // P]), sb("span", [P, GROUPS]), sb("wide", [P, GROUPS])
        bad, bad2, bad_all = (sb(x, [P, 1]) for x in ("bad", "bad2", "bad_all"))
        w_in, k_in, o_in, zeroed, split, rowf_ok, rowf_out, made, chain, bad_ok, bad_all_ok = (
            sem(x) for x in ("w_in", "k_in", "o_in", "zeroed", "split", "rowf_ok", "rowf_out", "made", "chain",
                             "bad_ok", "bad_all_ok"))
        with nc.Block() as block:
            @block.sync
            def _(sp):
                sp.dma_start(keys[:, :, :], d.keys).then_inc(k_in, 16)
                sp.dma_start(rows[:, :, :], d.key_rows).then_inc(k_in, 16)
                sp.dma_start(now[:, :], d.now).then_inc(o_in, 16)
                sp.dma_start(then[:, :], d.then).then_inc(o_in, 16)
                sp.dma_start(ends[:, :, :], d.ends.partition_broadcast(P)).then_inc(o_in, 16)
                sp.dma_start(m.bases[:, :], d.ends[0:1, :]).then_inc(w_in, 16)
                sp.dma_start(m.cols[:, :], d.cols).then_inc(w_in, 16)
                sp.dma_start(m.w2t[:, :], d.w2t).then_inc(w_in, 16)
                sp.wait_ge(w_in, 48)

            @block.gpsimd
            def _(g):
                g.iota(m.iota_row[:, :], [[1, P]], base=0, channel_multiplier=0,
                       allow_small_or_imprecise_dtypes=True)
                g.iota(m.iota_p[:, :], [[0, 1]], base=0, channel_multiplier=1,
                       allow_small_or_imprecise_dtypes=True).then_inc(made, 1)
                g.memset(m.ones[:, :], 1.0)
                for t in (m.ident, m.before, m.after):
                    g.memset(t[:, :], 0.0).then_inc(zeroed, 1)
                g.memset(m.real[:, :], 1.0).then_inc(zeroed, 1)
                g.wait_ge(zeroed, 4)
                g.affine_select(out=m.ident[:, :], in_=m.ident[:, :], compare_op=ALU.not_equal, fill=1.0,
                                base=0, pattern=[[-1, P]], channel_multiplier=1)
                g.affine_select(out=m.before[:, :], in_=m.before[:, :], compare_op=ALU.is_ge, fill=1.0,
                                base=0, pattern=[[1, P]], channel_multiplier=-1)
                g.affine_select(out=m.after[:, :], in_=m.after[:, :], compare_op=ALU.is_ge, fill=1.0,
                                base=0, pattern=[[-1, P]], channel_multiplier=1)
                g.affine_select(out=m.real[:, :], in_=m.real[:, :], compare_op=ALU.is_ge, fill=0.0,
                                base=N - 1, pattern=[[-P, NB]], channel_multiplier=-1)
                g.wait_ge(bad_ok, 1)
                g.partition_all_reduce(bad_all[:, :], bad[:, :], P, bass.bass_isa.ReduceOp.add
                                       ).then_inc(bad_all_ok, 1)

            @block.vector
            def _(v):
                v.wait_ge(k_in, 32)
                nc.vector.tensor_scalar(lows[:, :, :], keys[:, :, :], P - 1, None, ALU.bitwise_and).then_inc(split, 1)
                nc.vector.tensor_scalar(highs[:, :, :], keys[:, :, :], P.bit_length() - 1, None,
                                        ALU.arith_shift_right).then_inc(split, 1)
                nc.vector.tensor_scalar(row_lows[:, :, :], rows[:, :, :], P - 1, None,
                                        ALU.bitwise_and).then_inc(split, 1)
                nc.vector.tensor_copy(m.key[:, :, :], keys[:, :, :])
                nc.vector.tensor_copy(rowf[:, :, 0, :], rows[:, :, :]).then_inc(rowf_ok, 1)
                v.wait_ge(split, 3)
                nc.vector.tensor_copy(m.lo[:, :, :], lows[:, :, :])
                nc.vector.tensor_copy(m.hi[:, :, :], highs[:, :, :])
                nc.vector.tensor_copy(rowf[:, :, 1, :], row_lows[:, :, :]).then_inc(rowf_ok, 1)
                nc.vector.memset(m.visits[:, :], SLOTS)
                v.wait_ge(o_in, 48)
                step(v, nc.vector.tensor_tensor(falls[:, :], now[:, :], then[:, :], ALU.is_gt), chain, 1)
                step(v, nc.vector.tensor_reduce(bad[:, :], falls[:, :], X, ALU.add), chain, 2)
                step(v, nc.vector.tensor_tensor(span[:, :], ends[:, 1, :], ends[:, 0, :], ALU.subtract), chain, 3)
                step(v, nc.vector.tensor_scalar(wide[:, :], span[:, :], float(P), None, ALU.is_ge), chain, 4)
                step(v, nc.vector.tensor_reduce(bad2[:, :], wide[:, :], X, ALU.add), chain, 5)
                nc.vector.tensor_tensor(bad[:, :], bad[:, :], bad2[:, :], ALU.add).then_inc(bad_ok, 1)
                v.wait_ge(made, 1)
                step(v, nc.vector.tensor_copy(m.window[:, :], ends[:, 0, :]), chain, 6)
                nc.vector.tensor_tensor(m.inside[:, :].rearrange("p (g c) -> p g c", c=CG),
                                        m.key[:, 1, :].rearrange("p (g c) -> p g c", c=CG),
                                        m.window[:, :].unsqueeze(2).to_broadcast([P, GROUPS, CG]),
                                        ALU.subtract).then_inc(chain, 1)
                v.wait_ge(chain, 7)
                nc.vector.tensor_scalar(m.window[:, :], m.window[:, :], m.iota_p[:, 0:1], None, ALU.add)
                v.wait_ge(bad_all_ok, 1)
                nc.vector.tensor_scalar(m.ordered[:, :], bad_all[:, :], 0.0, None, ALU.is_equal)

            @block.scalar
            def _(act):
                act.wait_ge(rowf_ok, 2)
                act.dma_start(d.rowf.rearrange("w t (p j) -> p w t j", p=P), rowf[:, :, :, :]).then_inc(rowf_out, 16)
                act.wait_ge(rowf_out, 16)


def l0_tables(nc, d, m, placed, tag):
    ctx, sb, pb, sem = scope(nc, tag)
    W = TB_W if placed else D
    S = 3 if placed else 2
    R = 5
    with ctx:
        w = sb("w", [P, 2 * D])
        b1 = sb("b1", [P, D])
        xt = [sb(f"xt{k}", [P, P]) for k in range(R)]
        tab = [sb(f"tab{k}", [P, D + TB_W]) for k in range(R)]
        ps = [pb(f"ps{k}", [P, 2 * D]) for k in range(R)]
        w_in, mm, tab_ok = (sem(x) for x in ("w_in", "mm", "tab_ok"))
        xt_in = [sem(f"xt_in{k}") for k in range(R)]
        tab_out = [sem(f"tab_out{k}") for k in range(R)]
        with nc.Block() as block:
            @block.sync
            def _(sp):
                sp.dma_start(w[:, :], d.w1).then_inc(w_in, 16)
                sp.dma_start(b1[:, :], d.b1.partition_broadcast(P)).then_inc(w_in, 16)

                def body(i):
                    for k in range(R):
                        if not first(i):
                            sp.wait_ge(mm, i * R - R + k + 1)
                        sp.dma_start(xt[k][:, :], d.xT[:, ds(i * (R * P) + k * P, P)]).then_inc(xt_in[k], 16)
                turns(sp, NB // R, body)

            @block.tensor
            def _(pe):
                pe.wait_ge(w_in, 32)

                def body(i):
                    for k in range(R):
                        pe.wait_ge(xt_in[k], i * 16 + 16)
                        if not first(i):
                            pe.wait_ge(tab_ok, i * (S * R) - S * R + S * k + S)
                        nc.tensor.matmul(ps[k][:, :], xt[k][:, :], w[:, :], start=True, stop=True).then_inc(mm, 1)
                turns(pe, NB // R, body)

            @block.vector
            def _(v):
                v.wait_ge(w_in, 32)

                def body(i):
                    for k in range(R):
                        v.wait_ge(mm, i * R + k + 1)
                        if not first(i):
                            v.wait_ge(tab_out[k], i * 32)
                        nc.vector.tensor_tensor(tab[k][:, 0:D], ps[k][:, 0:D], b1[:, :], ALU.add).then_inc(tab_ok, 1)
                        nc.vector.tensor_scalar(tab[k][:, D:2 * D], ps[k][:, D:2 * D], 0.0, None,
                                                ALU.add).then_inc(tab_ok, 1)
                        if placed:
                            nc.vector.tensor_scalar(tab[k][:, 2 * D:2 * D + 1], m.place[:, ds(i * R + k, 1), 1], 0.0,
                                                    None, ALU.add).then_inc(tab_ok, 1)
                turns(v, NB // R, body)

            @block.gpsimd
            def _(g):
                g.nop()

            @block.scalar
            def _(act):
                def body(i):
                    for k in range(R):
                        act.wait_ge(tab_ok, i * (S * R) + S * k + S)
                        row = ds(i * (R * P) + k * P, P)
                        act.dma_start(d.ta[row, :], tab[k][:, 0:D]).then_inc(tab_out[k], 16)
                        act.dma_start(d.tb[row, 0:W], tab[k][:, D:D + W]).then_inc(tab_out[k], 16)
                turns(act, NB // R, body)
                for k in range(R):
                    act.wait_ge(tab_out[k], 32 * (NB // R))


class Ranks:
    pass


def ranks(nc, d, m, which, sb, pb, sem):
    keyrow = [sb(f"keyrow{p}", [P, 2, GE], u16) for p in range(2)]
    ohl = [sb(f"ohl{p}", [P, CG, P], bf16) for p in range(2)]
    ohh = [sb(f"ohh{p}", [P, CG, NB], bf16) for p in range(2)]
    ohT = [sb(f"ohT{p}", [P, GE]) for p in range(2)]
    apart = [sb(f"apart{p}", [P, GE]) for p in range(2)]
    same = [sb(f"same{c}", [P, P], bf16) for c in range(CG)]
    inside = [sb(f"inside{p}", [P, CG]) for p in range(2)]
    table = [sb(f"table{p}", [P, CG, NB]) for p in range(2)]
    hit = [sb(f"hit{p}", [P, CG, NB]) for p in range(2)]
    found = [sb(f"found{p}", [P, CG]) for p in range(2)]
    ps_n = [pb(f"ps_n{p}", [P, CG, NB]) for p in range(2)]
    ps_t = [pb(f"ps_t{p}", [P, CG, NB]) for p in range(2)]
    row_in = [sem(f"row_in{p}") for p in range(2)]
    (onehot, compared, counted, stepped, looked, hit_ok, found_ok, ranked, zeroed, passed_sp, apart_ok, rows_ok) = (
        sem(x) for x in ("onehot", "compared", "counted", "stepped", "looked", "hit_ok", "found_ok",
                         "ranked", "zeroed", "ranks_passed_sp", "apart_ok", "rows_ok"))

    def load(sp, i, p):
        if not first(i):
            hold(sp, compared, (i * 2 + p - 1) * CG, passed_sp)
            hold(sp, rows_ok, i * 2 + p - 1, passed_sp)
        sp.dma_start(keyrow[p][:, :, :],
                     d.rowf[which, :, ds(i * (2 * GE) + p * GE, GE)].partition_broadcast(P)).then_inc(row_in[p], 16)

    def start(v):
        step(v, nc.vector.memset(table[0][:, 0, :], 0.0), zeroed, 1)

    def finish(v, n, p, col):
        v.wait_ge(looked, n)
        step(v, nc.vector.tensor_tensor(hit[p][:, :, :], ps_t[p][:, :, :], ohh[p][:, :, :], ALU.mult), hit_ok, n)
        step(v, nc.vector.tensor_reduce(found[p][:, :], hit[p][:, :, :], X, ALU.add), found_ok, n)
        v.wait_ge(compared, n * CG)
        nc.vector.tensor_tensor(m.rank[:, which, col], found[p][:, :], inside[p][:, :], ALU.add).then_inc(ranked, 1)

    def compare(v, i, p):
        g = i * 2 + p
        at = i * (2 * CG) + p * CG
        v.wait_ge(row_in[p], i * 16 + 16)
        lo = m.lo[:, which, ds(at, CG)].unsqueeze(2).to_broadcast([P, CG, P])
        hi = m.hi[:, which, ds(at, CG)].unsqueeze(2).to_broadcast([P, CG, NB])
        nc.vector.tensor_tensor(ohl[p][:, :, :], m.iota_row[:, :].unsqueeze(1).to_broadcast([P, CG, P]),
                                lo, ALU.is_equal)
        nc.vector.tensor_tensor(ohh[p][:, :, :], m.iota_row[:, 0:NB].unsqueeze(1).to_broadcast([P, CG, NB]),
                                hi, ALU.is_equal).then_inc(onehot, 1)
        for c in range(CG):
            nc.vector.scalar_tensor_tensor(same[c][:, :], keyrow[p][:, 0, c * P:(c + 1) * P],
                                           m.key[:, which, ds(at + c, 1)], m.before[:, :], ALU.is_equal, ALU.mult,
                                           accum_out=inside[p][:, c:c + 1]).then_inc(compared, 1)
        if not (first(i) and p == 0):
            finish(v, g, 1 - p, ds(at - CG, CG))
        v.wait_ge(counted, g + 1)
        nc.vector.tensor_tensor(table[1 - p][:, 0, :], table[p][:, 0, :], ps_n[p][:, CG - 1, :], ALU.add
                                ).then_inc(stepped, 1)
        nc.vector.tensor_tensor(table[p][:, 1:CG, :], ps_n[p][:, 0:CG - 1, :],
                                table[p][:, 0:1, :].to_broadcast([P, CG - 1, NB]), ALU.add).then_inc(stepped, 1)
        v.wait_ge(stepped, g * 2 + 2)

    def end(v):
        finish(v, GROUPS, 1, ds((GROUPS - 1) * CG, CG))
        nc.vector.tensor_tensor(m.deg[:, which, 0:NB], table[0][:, 0, :], m.real[:, :], ALU.mult)
        nc.vector.tensor_copy(m.count[:, which, :], table[0][:, 0, :])

    def tally(pe, i, p):
        g = i * 2 + p
        pe.wait_ge(onehot, g + 1)
        for c in range(CG):
            last = nc.tensor.matmul(ps_n[p][:, c:CG, :], ohl[p][:, c, :],
                                    ohh[p][:, c:c + 1, :].to_broadcast([P, CG - c, NB]), start=c == 0,
                                    stop=c == CG - 1, skip_group_check=True)
        last.then_inc(counted, 1)

    def look(pe, i, p):
        g = i * 2 + p
        pe.wait_ge(rows_ok, g + 1)
        pe.wait_ge(stepped, g * 2 + 2)
        for c in range(CG):
            last = nc.tensor.matmul(ps_t[p][:, c, :], ohT[p][:, c * P:(c + 1) * P], table[p][:, c, :],
                                    start=True, stop=True)
        last.then_inc(looked, 1)

    def rows(act, i, p):
        g = i * 2 + p
        act.wait_ge(row_in[p], i * 16 + 16)
        if not first(i):
            act.wait_ge(looked, g - 1)
        nc.scalar.activation(apart[p][:, :], keyrow[p][:, 1, :], ACT.Square, bias=m.iota_p[:, 0:1], scale=-1.0
                             ).then_inc(apart_ok, 1)
        act.wait_ge(apart_ok, g + 1)
        nc.scalar.activation(ohT[p][:, :], apart[p][:, :], ACT.Relu, bias=m.ones[:, 0:1], scale=-1.0
                             ).then_inc(rows_ok, 1)

    r = Ranks()
    r.load, r.start, r.compare, r.end, r.tally, r.look, r.rows = load, start, compare, end, tally, look, rows
    return r


def rank_targets(nc, d, m):
    ctx, sb, pb, sem = scope(nc, "rank_t")
    with ctx:
        r = ranks(nc, d, m, 1, sb, pb, sem)
        with nc.Block() as block:
            @block.sync
            def _(sp):
                def body(i):
                    for p in range(2):
                        r.load(sp, i, p)
                turns(sp, GROUPS // 2, body)

            @block.gpsimd
            def _(g):
                g.nop()

            @block.scalar
            def _(act):
                def body(i):
                    for p in range(2):
                        r.rows(act, i, p)
                turns(act, GROUPS // 2, body)

            @block.vector
            def _(v):
                r.start(v)

                def body(i):
                    for p in range(2):
                        r.compare(v, i, p)
                turns(v, GROUPS // 2, body)
                r.end(v)

            @block.tensor
            def _(pe):
                def body(i):
                    for p in range(2):
                        r.tally(pe, i, p)
                        r.look(pe, i, p)
                turns(pe, GROUPS // 2, body)


def places(nc, d, m, w, tag):
    ctx, sb, pb, sem = scope(nc, tag)
    with ctx:
        total = sb("total", [NB, P])
        most, most_all, room = (sb(x, [P, 1]) for x in ("most", "most_all", "room"))
        ps_t, ps_o = pb("ps_t", [NB, P]), pb("ps_o", [P, NB])
        summed, total_ok, placed, most_ok, most_all_ok, chain = (
            sem(x) for x in ("summed", "total_ok", "placed", "most_ok", "most_all_ok", "chain"))
        with nc.Block() as block:
            @block.sync
            def _(sp):
                sp.nop()

            @block.scalar
            def _(act):
                act.nop()

            @block.tensor
            def _(pe):
                nc.tensor.matmul(ps_t[:, :], m.count[:, w, :], m.ones[:, :], start=True, stop=True).then_inc(summed, 1)
                pe.wait_ge(total_ok, 1)
                nc.tensor.matmul(ps_o[:, :], m.after[:, :], m.count[:, w, :], start=True, stop=False)
                nc.tensor.matmul(ps_o[:, :], total[:, :], m.after[0:NB, 0:NB], start=False,
                                 stop=True).then_inc(placed, 1)

            @block.vector
            def _(v):
                v.wait_ge(summed, 1)
                nc.vector.tensor_copy(total[:, :], ps_t[:, :]).then_inc(total_ok, 1)
                nc.vector.tensor_reduce(most[:, :], m.deg[:, w, 0:NB], X, ALU.max).then_inc(most_ok, 1)
                v.wait_ge(placed, 1)
                step(v, nc.vector.tensor_copy(m.place[:, 0:NB, w], ps_o[:, :]), chain, 1)
                step(v, nc.vector.tensor_scalar(m.place[:, NB:NB + AHEAD, w], m.place[:, 0:AHEAD, w], float(SLOTS),
                                                None, ALU.add), chain, 2)
                v.wait_ge(most_all_ok, 1)
                step(v, nc.vector.tensor_scalar(room[:, :], most_all[:, :], float(SLOTS - 1), float(SLOTS),
                                                ALU.add, ALU.max), chain, 3)
                step(v, nc.vector.tensor_copy(m.visits[:, w:w + 1], room[:, :]), chain, 4)
                step(v, nc.vector.tensor_tensor(m.visits[:, 2:3], m.visits[:, 0:1], m.visits[:, 1:2],
                                                ALU.max), chain, 5)
                nc.vector.tensor_scalar(m.trips[:, :], m.visits[:, :], SLOTS.bit_length() - 1, None,
                                        ALU.arith_shift_right)

            @block.gpsimd
            def _(g):
                g.wait_ge(most_ok, 1)
                g.partition_all_reduce(most_all[:, :], most[:, :], P, bass.bass_isa.ReduceOp.max
                                       ).then_inc(most_all_ok, 1)


def l0_first(nc, d, m):
    ctx, sb, pb, sem = scope(nc, "first")
    with ctx:
        r = ranks(nc, d, m, 0, sb, pb, sem)
        idx = [sb(f"idx{p}", [P, 2 * CG], i32) for p in range(2)]
        gs = [sb(f"gs{p}", [P, CG, D]) for p in range(2)]
        gt = [sb(f"gt{p}", [P, CG, TB_W]) for p in range(2)]
        hsum = [sb(f"hsum{p}", [P, CG, D]) for p in range(2)]
        h1 = [sb(f"h1{p}", [P, GE]) for p in range(2)]
        stats = sb("stats", [P, GROUPS, 6])
        ps = [pb(f"ps{p}", [P, GE]) for p in range(2)]
        idx_in = [sem(f"idx_in{p}") for p in range(2)]
        got = [sem(f"got{p}") for p in range(2)]
        stored = [sem(f"stored{p}") for p in range(2)]
        added, turned, copied, measured, passed, passed_act, stats_ok = (
            sem(x) for x in ("added", "turned", "copied", "measured", "passed", "passed_act", "stats_ok"))
        with nc.Block() as block:
            @block.sync
            def _(sp):
                def body(i):
                    for p in range(2):
                        if not first(i):
                            sp.wait_ge(got[p], i * (2 * CG * 16))
                        sp.dma_start(idx[p][:, :], d.idx[ds(i * 2 + p, 1), :, :].rearrange("a p c -> (a p) c")
                                     ).then_inc(idx_in[p], 16)
                        r.load(sp, i, p)
                turns(sp, GROUPS // 2, body)

            @block.gpsimd
            def _(g):
                def body(i):
                    for p in range(2):
                        hold(g, idx_in[p], i * 16 + 16, passed)
                        if not first(i):
                            hold(g, added, i * 2 + p - 1, passed)
                        for c in range(CG):
                            g.indirect_dma_start(gs[p][:, c, :], None, d.ta,
                                                 bass.IndirectOffsetOnAxis(ap=idx[p][:, c:c + 1], axis=0)
                                                 ).then_inc(got[p], 16)
                            g.indirect_dma_start(gt[p][:, c, :], None, d.tb,
                                                 bass.IndirectOffsetOnAxis(ap=idx[p][:, CG + c:CG + c + 1], axis=0)
                                                 ).then_inc(got[p], 16)
                turns(g, GROUPS // 2, body)

            @block.vector
            def _(v):
                r.start(v)

                def body(i):
                    for p in range(2):
                        v.wait_ge(got[p], (i + 1) * (2 * CG * 16))
                        if not first(i):
                            v.wait_ge(turned, i * 2 + p - 1)
                        at = ds(i * (2 * CG) + p * CG, CG)
                        nc.vector.tensor_tensor(m.where_t[:, at], m.rank[:, 1, at], gt[p][:, :, D], ALU.add)
                        nc.vector.tensor_tensor(hsum[p][:, :, :], gs[p][:, :, :], gt[p][:, :, 0:D],
                                                ALU.add).then_inc(added, 1)
                        r.compare(v, i, p)
                        hold(v, copied, i * 2 + p + 1, passed)
                        nc.vector.bn_stats(stats[:, ds(i * 2 + p, 1), :].rearrange("p a s -> p (a s)"),
                                           h1[p][:, :]).then_inc(measured, 1)
                turns(v, GROUPS // 2, body)
                v.wait_ge(measured, GROUPS)
                nc.vector.bn_stats(stats[:, GROUPS - 1, :], real_part(h1[1][:, :])).then_inc(stats_ok, 1)
                v.wait_ge(stats_ok, 1)
                nc.vector.bn_aggr(m.mv1[:, :], stats[:, :, :].rearrange("p g s -> p (g s)"))
                r.end(v)

            @block.tensor
            def _(pe):
                def body(i):
                    for p in range(2):
                        r.tally(pe, i, p)
                        pe.wait_ge(added, i * 2 + p + 1)
                        if not first(i):
                            pe.wait_ge(copied, i * 2 + p - 1)
                        for c in range(CG):
                            last = nc.tensor.transpose(ps[p][:, c * P:(c + 1) * P], hsum[p][:, c, :], m.ident[:, :])
                        last.then_inc(turned, 1)
                        r.look(pe, i, p)
                turns(pe, GROUPS // 2, body)

            @block.scalar
            def _(act):
                def body(i):
                    for p in range(2):
                        r.rows(act, i, p)
                        hold(act, turned, i * 2 + p + 1, passed_act)
                        if not first(i):
                            act.wait_ge(stored[p], i * 16)
                            hold(act, measured, i * 2 + p - 1, passed_act)
                        nc.scalar.activation(h1[p][:, :], ps[p][:, :], ACT.Copy).then_inc(copied, 1)
                        act.wait_ge(copied, i * 2 + p + 1)
                        act.dma_start(d.h1[:, ds(i * (2 * GE) + p * GE, GE)], h1[p][:, :]).then_inc(stored[p], 16)
                turns(act, GROUPS // 2, body)
                for p in range(2):
                    act.wait_ge(stored[p], 16 * (GROUPS // 2))


def l0_first_ordered(nc, d, m):
    ctx, sb, pb, sem = scope(nc, "firsto")
    R = 4
    with ctx:
        r = ranks(nc, d, m, 0, sb, pb, sem)
        idx = [sb(f"idx{k}", [P, CG], i32) for k in range(R)]
        gs = [sb(f"gs{k}", [P, CG, D]) for k in range(R)]
        win = [sb(f"win{k}", [P, D]) for k in range(R)]
        target = [sb(f"target{k}", [P, GE], u16) for k in range(R)]
        off = [sb(f"off{p}", [P, GE]) for p in range(2)]
        pick = [sb(f"pick{p}", [P, GE]) for p in range(2)]
        h1 = [sb(f"h1{p}", [P, GE]) for p in range(2)]
        stats = sb("stats", [P, GROUPS, 6])
        ps = [pb(f"ps{p}", [P, GE]) for p in range(2)]
        idx_in, got, win_in, target_in = (
            [sem(f"{x}{k}") for k in range(R)] for x in ("idx_in", "got", "win_in", "target_in"))
        stored = [sem(f"stored{p}") for p in range(2)]
        picked, summed, copied, measured, passed, passed_act, passed_sp, stats_ok, off_ok = (
            sem(x) for x in ("picked", "summed", "copied", "measured", "passed", "passed_act", "passed_sp",
                             "stats_ok", "off_ok"))

        def groups(eng, body):
            def turn(i):
                for k in range(R):
                    body(i, k, i * 2 + k // 2, k % 2, i * R + k + 1, first(i) and k < 2)
            turns(eng, GROUPS // R, turn)

        with nc.Block() as block:
            @block.sync
            def _(sp):
                def body(i, k, pair, p, n, fresh):
                    if not first(i):
                        sp.wait_ge(got[k], i * (CG * 16))
                    sp.dma_start(idx[k][:, :], d.idx[ds(i * R + k, 1), :, 0:CG].rearrange("a p c -> (a p) c")
                                 ).then_inc(idx_in[k], 16)
                    if not first(i):
                        hold(sp, picked, n - R, passed_sp)
                    sp.dma_start(target[k][:, :],
                                 d.rowf[1, 0, ds(i * (R * GE) + k * GE, GE)].partition_broadcast(P)
                                 ).then_inc(target_in[k], 16)
                    r.load(sp, pair, p)
                    if not first(i):
                        hold(sp, summed, n - R, passed_sp)
                    base = sp.value_load(m.bases[0:1, ds(i * R + k, 1)], min_val=0, max_val=N)
                    sp.dma_start(win[k][:, :], d.tb[ds(base, P), 0:D]).then_inc(win_in[k], 16)
                groups(sp, body)

            @block.gpsimd
            def _(g):
                def body(i, k, pair, p, n, fresh):
                    hold(g, idx_in[k], i * 16 + 16, passed)
                    if not first(i):
                        hold(g, summed, n - R, passed)
                    for c in range(CG):
                        g.indirect_dma_start(gs[k][:, c, :], None, d.ta,
                                             bass.IndirectOffsetOnAxis(ap=idx[k][:, c:c + 1], axis=0)
                                             ).then_inc(got[k], 16)
                groups(g, body)

            @block.vector
            def _(v):
                r.start(v)

                def measure(p, n):
                    hold(v, copied, n, passed)
                    nc.vector.bn_stats(stats[:, ds(n - 1, 1), :].rearrange("p a s -> p (a s)"),
                                       h1[p][:, :]).then_inc(measured, 1)

                def body(i, k, pair, p, n, fresh):
                    r.compare(v, pair, p)
                    if not (first(i) and k == 0):
                        measure(1 - p, n - 1)
                groups(v, body)
                measure(1, GROUPS)
                v.wait_ge(measured, GROUPS)
                nc.vector.bn_stats(stats[:, GROUPS - 1, :], real_part(h1[1][:, :])).then_inc(stats_ok, 1)
                v.wait_ge(stats_ok, 1)
                nc.vector.bn_aggr(m.mv1[:, :], stats[:, :, :].rearrange("p g s -> p (g s)"))
                r.end(v)

            @block.tensor
            def _(pe):
                def body(i, k, pair, p, n, fresh):
                    r.tally(pe, pair, p)
                    pe.wait_ge(picked, n)
                    pe.wait_ge(win_in[k], i * 16 + 16)
                    if not fresh:
                        pe.wait_ge(copied, n - 2)
                    nc.tensor.matmul(ps[p][:, :], win[k][:, :], pick[p][:, :], start=True, stop=False,
                                     skip_group_check=True)
                    pe.wait_ge(got[k], i * (CG * 16) + CG * 16)
                    for c in range(CG):
                        last = nc.tensor.matmul(ps[p][:, c * P:(c + 1) * P], gs[k][:, c, :], m.ident[:, :],
                                                start=False, stop=True, skip_group_check=True)
                    last.then_inc(summed, 1)
                    r.look(pe, pair, p)
                groups(pe, body)

            @block.scalar
            def _(act):
                def choose(i, k, p, n, fresh):
                    hold(act, target_in[k], i * 16 + 16, passed_act)
                    if not fresh:
                        hold(act, summed, n - 2, passed_act)
                    nc.scalar.activation(off[p][:, :], target[k][:, :], ACT.Square, bias=m.window[:, ds(n - 1, 1)],
                                         scale=-1.0).then_inc(off_ok, 1)
                    act.wait_ge(off_ok, n)
                    nc.scalar.activation(pick[p][:, :], off[p][:, :], ACT.Relu, bias=m.ones[:, 0:1], scale=-1.0
                                         ).then_inc(picked, 1)

                def store(pair, p, n, fresh):
                    act.wait_ge(summed, n)
                    if not fresh:
                        act.wait_ge(stored[p], pair * 16)
                        act.wait_ge(measured, n - 2)
                    nc.scalar.activation(h1[p][:, :], ps[p][:, :], ACT.Copy).then_inc(copied, 1)
                    act.wait_ge(copied, n)
                    act.dma_start(d.h1[:, ds((n - 1) * GE, GE)], h1[p][:, :]).then_inc(stored[p], 16)

                def body(i, k, pair, p, n, fresh):
                    choose(i, k, p, n, fresh)
                    r.rows(act, pair, p)
                    if not (first(i) and k == 0):
                        store(pair - 1 + p, 1 - p, n - 1, first(i) and k < 3)
                groups(act, body)
                store(GROUPS // 2 - 1, 1, GROUPS, False)
                for p in range(2):
                    act.wait_ge(stored[p], 16 * (GROUPS // 2))


def norm_terms(nc, m, mv, gamma, beta, scale, shift, tag, mean_extra=None):
    ctx, sb, pb, sem = scope(nc, tag)
    with ctx:
        vpe, root, inv, t = (sb(x, [P, 1]) for x in ("vpe", "root", "inv", "t"))
        eps_ok, root_ok, chain = (sem(x) for x in ("eps_ok", "root_ok", "chain"))
        with nc.Block() as block:
            @block.vector
            def _(v):
                nc.vector.tensor_scalar(vpe[:, :], mv[:, 1:2], EPS, None, ALU.add).then_inc(eps_ok, 1)
                v.wait_ge(root_ok, 1)
                step(v, nc.vector.reciprocal(inv[:, :], root[:, :]), chain, 1)
                step(v, nc.vector.tensor_tensor(scale[:, :], inv[:, :], gamma, ALU.mult), chain, 2)
                step(v, nc.vector.tensor_tensor(t[:, :], mv[:, 0:1], scale[:, :], ALU.mult), chain, 3)
                step(v, nc.vector.tensor_tensor(shift[:, :], beta, t[:, :], ALU.subtract), chain, 4)

            @block.scalar
            def _(act):
                act.wait_ge(eps_ok, 1)
                nc.scalar.activation(root[:, :], vpe[:, :], ACT.Sqrt).then_inc(root_ok, 1)


def l0_second(nc, d, m):
    ctx, sb, pb, sem = scope(nc, "second")
    R = 4
    with ctx:
        h1 = [sb(f"h1{k}", [P, GE]) for k in range(R)]
        hr = [sb(f"hr{k}", [P, GE]) for k in range(R)]
        stats = sb("stats", [P, GROUPS, 6])
        raw = sb("raw", [P, 2])
        ps = [pb(f"ps{k}", [P, GE]) for k in range(R)]
        h1_in = [sem(f"h1_in{k}") for k in range(R)]
        relued, mm, measured, passed, stats_ok, raw_ok = (
            sem(x) for x in ("relued", "mm", "measured", "passed", "stats_ok", "raw_ok"))
        with nc.Block() as block:
            @block.sync
            def _(sp):
                def body(i):
                    for k in range(R):
                        if not first(i):
                            sp.wait_ge(relued, i * R - R + k + 1)
                        sp.dma_start(h1[k][:, :], d.h1[:, ds(i * (R * GE) + k * GE, GE)]).then_inc(h1_in[k], 16)
                turns(sp, GROUPS // R, body)

            @block.scalar
            def _(act):
                def body(i):
                    for k in range(R):
                        act.wait_ge(h1_in[k], i * 16 + 16)
                        if not first(i):
                            act.wait_ge(mm, i * R - R + k + 1)
                        nc.scalar.activation(hr[k][:, :], h1[k][:, :], ACT.Relu, bias=m.shift1[:, 0:1],
                                             scale=m.scale1[:, 0:1]).then_inc(relued, 1)
                turns(act, GROUPS // R, body)

            @block.tensor
            def _(pe):
                def body(i):
                    for k in range(R):
                        pe.wait_ge(relued, i * R + k + 1)
                        if not first(i):
                            pe.wait_ge(measured, i * R - R + k + 1)
                        nc.tensor.matmul(ps[k][:, :], m.w2t[:, :], hr[k][:, :], start=True, stop=True).then_inc(mm, 1)
                turns(pe, GROUPS // R, body)

            @block.vector
            def _(v):
                def body(i):
                    for k in range(R):
                        hold(v, mm, i * R + k + 1, passed)
                        nc.vector.bn_stats(stats[:, ds(i * R + k, 1), :].rearrange("p a s -> p (a s)"),
                                           ps[k][:, :]).then_inc(measured, 1)
                turns(v, GROUPS // R, body)
                v.wait_ge(measured, GROUPS)
                nc.vector.bn_stats(stats[:, GROUPS - 1, :], real_part(ps[R - 1])).then_inc(stats_ok, 1)
                v.wait_ge(stats_ok, 1)
                step(v, nc.vector.bn_aggr(raw[:, :], stats[:, :, :].rearrange("p g s -> p (g s)")), raw_ok, 1)
                nc.vector.tensor_tensor(m.mv2[:, 0:1], raw[:, 0:1], m.cols[:, 4:5], ALU.add)
                nc.vector.tensor_copy(m.mv2[:, 1:2], raw[:, 1:2])


def fold_second(nc, d, m):
    ctx, sb, pb, sem = scope(nc, "fold")
    with ctx:
        w2 = sb("w2", [P, D])
        w2s = sb("w2s", [P, D])
        t, col, cols = sb("t", [P, 1]), sb("col", [P, 1]), sb("cols", [P, P])
        ps_w, ps_r = pb("ps_w", [P, D]), pb("ps_r", [P, D])
        w_in, scaled, t_ok, col_ok, turned = (sem(x) for x in ("w_in", "scaled", "t_ok", "col_ok", "turned"))
        with nc.Block() as block:
            @block.sync
            def _(sp):
                sp.dma_start(w2[:, :], d.w2).then_inc(w_in, 16)

            @block.vector
            def _(v):
                v.wait_ge(w_in, 16)
                nc.vector.tensor_scalar(w2s[:, :], w2[:, :], m.scale2[:, 0:1], None, ALU.mult).then_inc(scaled, 1)
                step(v, nc.vector.tensor_tensor(t[:, :], m.cols[:, 4:5], m.scale2[:, :], ALU.mult), t_ok, 1)
                step(v, nc.vector.tensor_tensor(col[:, :], t[:, :], m.shift2[:, :], ALU.add), col_ok, 1)
                nc.vector.tensor_scalar(cols[:, :], m.ones[:, :], col[:, 0:1], None, ALU.mult).then_inc(col_ok, 1)
                v.wait_ge(turned, 2)
                nc.vector.tensor_copy(m.w2ts[:, :], ps_w[:, :])
                nc.vector.tensor_copy(m.row2[:, :], ps_r[:, :])

            @block.tensor
            def _(pe):
                pe.wait_ge(scaled, 1)
                nc.tensor.transpose(ps_w[:, :], w2s[:, :], m.ident[:, :]).then_inc(turned, 1)
                pe.wait_ge(col_ok, 2)
                nc.tensor.matmul(ps_r[:, :], cols[:, :], m.ident[:, :], start=True, stop=True).then_inc(turned, 1)


def l0_third(nc, d, m):
    ctx, sb, pb, sem = scope(nc, "third")
    R = 4
    with ctx:
        h1 = [sb(f"h1{p}", [P, GE]) for p in range(R)]
        hr = [sb(f"hr{p}", [P, GE]) for p in range(R)]
        up = [sb(f"up{p}", [P, CG, D]) for p in range(R)]
        to = [sb(f"to{p}", [P, CG], i32) for p in range(R)]
        zero = sb("zero", [SLOTS, D])
        ps = [pb(f"ps{p}", [P, CG, D]) for p in range(R)]
        h1_in = [sem(f"h1_in{p}") for p in range(R)]
        put = [sem(f"put{p}") for p in range(R)]
        relued, mm, up_ok, to_ok, passed, zero_ok, zero_out = (
            sem(x) for x in ("relued", "mm", "up_ok", "to_ok", "passed", "zero_ok", "zero_out"))
        with nc.Block() as block:
            @block.sync
            def _(sp):
                sp.wait_ge(zero_ok, 1)
                sp.dma_start(d.up[EP:EP + SLOTS, :], zero[:, :]).then_inc(zero_out, 16)

                def body(i):
                    for p in range(R):
                        if not first(i):
                            sp.wait_ge(relued, i * R - R + p + 1)
                        sp.dma_start(h1[p][:, :], d.h1[:, ds(i * (R * GE) + p * GE, GE)]).then_inc(h1_in[p], 16)
                turns(sp, GROUPS // R, body)
                sp.wait_ge(zero_out, 16)

            @block.vector
            def _(v):
                nc.vector.memset(zero[:, :], 0.0).then_inc(zero_ok, 1)

                def body(i):
                    for p in range(R):
                        if not first(i):
                            v.wait_ge(put[p], i * (16 * CG))
                        nc.vector.tensor_scalar(to[p][:, :], m.where_t[:, ds(i * (R * CG) + p * CG, CG)], 0.0, None,
                                                ALU.add).then_inc(to_ok, 1)
                turns(v, GROUPS // R, body)

            @block.scalar
            def _(act):
                def body(i):
                    for p in range(R):
                        act.wait_ge(h1_in[p], i * 16 + 16)
                        if not first(i):
                            act.wait_ge(mm, i * R - R + p + 1)
                        nc.scalar.activation(hr[p][:, :], h1[p][:, :], ACT.Relu, bias=m.shift1[:, 0:1],
                                             scale=m.scale1[:, 0:1]).then_inc(relued, 1)
                    for p in range(R):
                        act.wait_ge(mm, i * R + p + 1)
                        if not first(i):
                            act.wait_ge(put[p], i * (16 * CG))
                        nc.scalar.activation(up[p][:, :, :], ps[p][:, :, :], ACT.Relu).then_inc(up_ok, 1)
                turns(act, GROUPS // R, body)

            @block.tensor
            def _(pe):
                def body(i):
                    for p in range(R):
                        pe.wait_ge(relued, i * R + p + 1)
                        if not first(i):
                            pe.wait_ge(up_ok, i * R - R + p + 1)
                        for c in range(CG):
                            nc.tensor.matmul(ps[p][:, c, :], hr[p][:, c * P:(c + 1) * P], m.w2ts[:, :],
                                             start=True, stop=False)
                            last = nc.tensor.matmul(ps[p][:, c, :], m.ones[0:1, :], m.row2[0:1, :],
                                                    start=False, stop=True)
                        last.then_inc(mm, 1)
                turns(pe, GROUPS // R, body)

            @block.gpsimd
            def _(g):
                def body(i):
                    for p in range(R):
                        hold(g, to_ok, i * R + p + 1, passed)
                        hold(g, up_ok, i * R + p + 1, passed)
                        for c in range(CG):
                            g.indirect_dma_start(d.up, bass.IndirectOffsetOnAxis(ap=to[p][:, c:c + 1], axis=0),
                                                 up[p][:, c, :], None).then_inc(put[p], 16)
                turns(g, GROUPS // R, body)
                for p in range(R):
                    g.wait_ge(put[p], 16 * CG * (GROUPS // R))


def l0_third_ordered(nc, d, m):
    ctx, sb, pb, sem = scope(nc, "thirdo")
    R = 4
    with ctx:
        h1 = [sb(f"h1{p}", [P, GE]) for p in range(R)]
        hr = [sb(f"hr{p}", [P, GE]) for p in range(R)]
        pre = [sb(f"pre{p}", [P, CG, D]) for p in range(R)]
        up = [sb(f"up{p}", [P, CG, D]) for p in range(R)]
        ohl = [sb(f"ohl{p}", [P, CG, P], bf16) for p in range(R)]
        ohh = [sb(f"ohh{p}", [P, CG, NB], bf16) for p in range(R)]
        ohw = [sb(f"ohw{p}", [P, CG, P]) for p in range(R)]
        part = [sb(f"part{q}", [P, P]) for q in range(2)]
        sums = sb("sums", [P, NP_])
        block_sums = [sb(f"block_sums{q}", [P, P]) for q in range(2)]
        ps = [pb(f"ps{p}", [P, CG, D]) for p in range(R)]
        ps_n = pb("ps_n", [P, NB])
        ps_s = [pb(f"ps_s{q}", [P, P]) for q in range(2)]
        h1_in = [sem(f"h1_in{p}") for p in range(R)]
        (relued, mm, pre_ok, up_ok, onehot, counted, summed, part_ok, taken, zeroed, cut, turned, kept, passed,
         passed_act) = (
            sem(x) for x in ("relued", "mm", "pre_ok", "up_ok", "onehot", "counted", "summed", "part_ok", "taken",
                             "zeroed", "cut", "turned", "kept", "passed", "passed_act"))
        with nc.Block() as block:
            @block.sync
            def _(sp):
                def body(i):
                    for p in range(R):
                        if not first(i):
                            sp.wait_ge(relued, i * R - R + p + 1)
                        sp.dma_start(h1[p][:, :], d.h1[:, ds(i * (R * GE) + p * GE, GE)]).then_inc(h1_in[p], 16)
                turns(sp, GROUPS // R, body)

            @block.gpsimd
            def _(g):
                g.memset(sums[:, :], 0.0).then_inc(zeroed, 1)
                g.wait_ge(zeroed, 1)

                def body(i):
                    for p in range(R):
                        n = i * R + p + 1
                        hold(g, part_ok, n, passed)
                        if not (first(i) and p == 0):
                            hold(g, taken, n - 1, passed)
                        base = g.value_load(m.bases[0:1, ds(n - 1, 1)], min_val=0, max_val=N)
                        g.tensor_tensor(sums[:, ds(base, P)], sums[:, ds(base, P)], part[p % 2][:, :], ALU.add
                                        ).then_inc(taken, 1)
                turns(g, GROUPS // R, body)

            @block.vector
            def _(v):
                def bring(i, p, n):
                    v.wait_ge(summed, n)
                    if not (first(i) and p < 2):
                        v.wait_ge(taken, n - 2)
                    nc.vector.tensor_copy(part[p % 2][:, :], ps_s[p % 2]).then_inc(part_ok, 1)

                def body(i):
                    for p in range(R):
                        n = i * R + p + 1
                        if not first(i):
                            v.wait_ge(counted, n - R)
                            v.wait_ge(summed, n - R)
                        at = ds(i * (R * CG) + p * CG, CG)
                        wide = m.iota_row[:, :].unsqueeze(1).to_broadcast([P, CG, P])
                        nc.vector.tensor_tensor(ohl[p][:, :, :], wide,
                                                m.lo[:, 1, at].unsqueeze(2).to_broadcast([P, CG, P]), ALU.is_equal)
                        nc.vector.tensor_tensor(ohw[p][:, :, :], wide,
                                                m.inside[:, at].unsqueeze(2).to_broadcast([P, CG, P]), ALU.is_equal)
                        nc.vector.tensor_tensor(ohh[p][:, :, :],
                                                m.iota_row[:, 0:NB].unsqueeze(1).to_broadcast([P, CG, NB]),
                                                m.hi[:, 1, at].unsqueeze(2).to_broadcast([P, CG, NB]),
                                                ALU.is_equal).then_inc(onehot, 1)
                        v.wait_ge(mm, n)
                        if not first(i):
                            v.wait_ge(up_ok, n - R)
                        nc.vector.tensor_tensor(pre[p][:, :, :], ps[p],
                                                m.row2[:, :].unsqueeze(1).to_broadcast([P, CG, D]), ALU.add
                                                ).then_inc(pre_ok, 1)
                        if not (first(i) and p < 2):
                            bring(i if p > 1 else 1, (p - 2) % R, n - 2)
                turns(v, GROUPS // R, body)
                bring(1, R - 2, GROUPS - 1)
                bring(1, R - 1, GROUPS)
                nc.vector.tensor_tensor(m.deg[:, 1, 0:NB], ps_n[:, :], m.real[:, :], ALU.mult)
                nc.vector.tensor_copy(m.count[:, 1, :], ps_n[:, :])

                def keep(i):
                    for q in range(2):
                        v.wait_ge(turned, i * 2 + q + 1)
                        nc.vector.tensor_scalar(m.agg[:, ds(i * 2 + q, 1), :].rearrange("p a f -> p (a f)"), ps_s[q],
                                                0.0, None, ALU.add).then_inc(kept, 1)
                turns(v, NB // 2, keep)

            @block.scalar
            def _(act):
                def body(i):
                    for p in range(R):
                        act.wait_ge(h1_in[p], i * 16 + 16)
                        if not first(i):
                            act.wait_ge(mm, i * R - R + p + 1)
                        nc.scalar.activation(hr[p][:, :], h1[p][:, :], ACT.Relu, bias=m.shift1[:, 0:1],
                                             scale=m.scale1[:, 0:1]).then_inc(relued, 1)
                    for p in range(R):
                        act.wait_ge(pre_ok, i * R + p + 1)
                        if not first(i):
                            act.wait_ge(summed, i * R - R + p + 1)
                        nc.scalar.activation(up[p][:, :, :], pre[p][:, :, :], ACT.Relu).then_inc(up_ok, 1)
                turns(act, GROUPS // R, body)
                act.wait_ge(taken, GROUPS)

                def separate(i):
                    for q in range(2):
                        if not first(i):
                            hold(act, turned, i * 2 + q - 1, passed_act)
                        nc.scalar.activation(block_sums[q][:, :], sums[:, ds(i * (2 * P) + q * P, P)], ACT.Copy
                                             ).then_inc(cut, 1)
                turns(act, NB // 2, separate)

            @block.tensor
            def _(pe):
                def add_up(i, p, n):
                    pe.wait_ge(up_ok, n)
                    if not (first(i) and p < 2):
                        pe.wait_ge(part_ok, n - 2)
                    for c in range(CG):
                        last = nc.tensor.matmul(ps_s[p % 2], up[p][:, c, :], ohw[p][:, c, :], start=c == 0,
                                                stop=c == CG - 1)
                    last.then_inc(summed, 1)

                def body(i):
                    for p in range(R):
                        n = i * R + p + 1
                        pe.wait_ge(relued, n)
                        if not first(i):
                            pe.wait_ge(pre_ok, n - R)
                        for c in range(CG):
                            last = nc.tensor.matmul(ps[p][:, c, :], hr[p][:, c * P:(c + 1) * P], m.w2ts[:, :],
                                                    start=True, stop=True)
                        last.then_inc(mm, 1)
                        pe.wait_ge(onehot, n)
                        for c in range(CG):
                            last = nc.tensor.matmul(ps_n[:, :], ohl[p][:, c, :], ohh[p][:, c, :],
                                                    start=first(i) and p == 0 and c == 0, stop=False,
                                                    skip_group_check=True)
                        last.then_inc(counted, 1)
                        if not (first(i) and p == 0):
                            add_up(i if p else 1, (p - 1) % R, n - 1)
                turns(pe, GROUPS // R, body)
                add_up(1, R - 1, GROUPS)
                pe.wait_ge(part_ok, GROUPS)

                def turn(i):
                    for q in range(2):
                        pe.wait_ge(cut, i * 2 + q + 1)
                        if not first(i):
                            pe.wait_ge(kept, i * 2 + q - 1)
                        nc.tensor.transpose(ps_s[q], block_sums[q][:, :], m.ident[:, :]).then_inc(turned, 1)
                turns(pe, NB // 2, turn)


def l0_gather(nc, d, m):
    ctx, sb, pb, sem = scope(nc, "sum")
    with ctx:
        run = [sb(f"run{p}", [P, SLOTS, D]) for p in range(2)]
        at_f = [sb(f"at_f{p}", [P, 1]) for p in range(2)]
        at_c = [sb(f"at_c{p}", [P, 1]) for p in range(2)]
        at = [sb(f"at{p}", [P, 1], i32) for p in range(2)]
        left = [sb(f"left{p}", [P, 1]) for p in range(2)]
        live = [sb(f"live{p}", [P, SLOTS]) for p in range(2)]
        masked = [sb(f"masked{p}", [P, SLOTS, D]) for p in range(2)]
        part = [sb(f"part{p}", [P, D]) for p in range(2)]
        passed_slots = sb("passed_slots", [P, 1])
        got = [sem(f"got{p}") for p in range(2)]
        at_f_ok, at_c_ok, at_ok, left_ok, live_ok, masked_ok, part_ok, passed, summed, slots_ok, zeroed = (
            sem(x) for x in ("at_f_ok", "at_c_ok", "at_ok", "left_ok", "live_ok", "masked_ok", "part_ok",
                             "passed", "summed", "slots_ok", "zeroed"))
        with nc.Block() as block:
            @block.vector
            def _(v):
                rounds = v.value_load(m.trips[0:1, 1:2], min_val=1, max_val=EP // SLOTS + 1)
                nc.vector.memset(m.agg[:, :, :], 0.0).then_inc(zeroed, 1)
                step(v, nc.vector.memset(passed_slots[:, :], 0.0), zeroed, 2)

                def aim(n, b, p):
                    step(v, nc.vector.tensor_tensor(at_f[p][:, :], m.place[:, ds(b, 1), 1], passed_slots[:, :],
                                                    ALU.add), at_f_ok, n)
                    step(v, nc.vector.tensor_scalar(at_c[p][:, :], at_f[p][:, :], float(EP), float(D), ALU.min,
                                                    ALU.mult), at_c_ok, n)
                    nc.vector.tensor_copy(at[p][:, :], at_c[p][:, :]).then_inc(at_ok, 1)

                aim(1, 0, 0)
                with v.Fori(0, rounds) as r:
                    with v.Fori(0, NB // 2) as j:
                        for p in range(2):
                            n = r * NB + j * 2 + p + 1
                            b = j * 2 + p
                            aim(n + 1, b + 1, 1 - p)
                            step(v, nc.vector.tensor_tensor(left[p][:, :], m.deg[:, 1, ds(b, 1)], passed_slots[:, :],
                                                            ALU.subtract), left_ok, n)
                            step(v, nc.vector.tensor_scalar(live[p][:, :], m.iota_row[:, 0:SLOTS], left[p][:, 0:1],
                                                            None, ALU.is_lt), live_ok, n)
                            v.wait_ge(got[p], r * (NB // 2 * 16) + j * 16 + 16)
                            step(v, nc.vector.tensor_tensor(
                                masked[p][:, :, :], run[p][:, :, :],
                                live[p][:, :].unsqueeze(2).to_broadcast([P, SLOTS, D]), ALU.mult), masked_ok, n)
                            step(v, nc.vector.tensor_reduce(part[p][:, :],
                                                            masked[p][:, :, :].rearrange("p s f -> p f s"), X,
                                                            ALU.add), part_ok, n)
                            step(v, nc.vector.tensor_tensor(m.agg[:, ds(b, 1), :].rearrange("p a f -> p (a f)"),
                                                            m.agg[:, ds(b, 1), :].rearrange("p a f -> p (a f)"),
                                                            part[p][:, :], ALU.add), summed, n)
                    step(v, nc.vector.tensor_scalar(passed_slots[:, :], passed_slots[:, :], float(SLOTS), None,
                                                    ALU.add), slots_ok, r + 1)

            @block.sync
            def _(sp):
                sp.nop()

            @block.scalar
            def _(act):
                act.nop()

            @block.tensor
            def _(pe):
                pe.nop()

            @block.gpsimd
            def _(g):
                rounds = g.value_load(m.trips[0:1, 1:2], min_val=1, max_val=EP // SLOTS + 1)
                flat = d.up.rearrange("n f -> (n f)").rearrange("(n o) -> n o", o=1)

                def fetch(n, p):
                    hold(g, at_ok, n, passed)
                    g.indirect_dma_start(run[p][:, :, :].rearrange("p s f -> p (s f)"), None, flat,
                                         bass.IndirectOffsetOnAxis(ap=at[p][:, 0:1], axis=0)).then_inc(got[p], 16)

                fetch(1, 0)
                with g.Fori(0, rounds) as r:
                    with g.Fori(0, NB // 2) as j:
                        for p in range(2):
                            n = r * NB + j * 2 + p + 1
                            fetch(n + 1, 1 - p)
                g.wait_ge(got[0], rounds * (NB // 2 * 16) + 16)


def layer_norm(nc, d, m):
    ctx, sb, pb, sem = scope(nc, "norm1")
    with ctx:
        x = sb("x", [P, NB, D])
        sq = sb("sq", [P, NB, D])
        tot, mean, var, root, inv = (sb(n, [P, NB]) for n in ("tot", "mean", "var", "root", "inv"))
        x_in, chain, sq_ok, var_ok, root_ok, out_ok, stored, cent_ok = (
            sem(n) for n in ("x_in", "chain", "sq_ok", "var_ok", "root_ok", "out_ok", "stored", "cent_ok"))
        wide = [P, NB, D]
        with nc.Block() as block:
            @block.sync
            def _(sp):
                sp.dma_start(x[:, :, :], d.x.rearrange("(b p) f -> p b f", p=P)).then_inc(x_in, 16)
                sp.wait_ge(out_ok, 1)
                sp.dma_start(d.x1.rearrange("(b p) f -> p b f", p=P), m.agg[:, :, :]).then_inc(stored, 16)
                sp.wait_ge(stored, 16)

            @block.vector
            def _(v):
                v.wait_ge(x_in, 16)
                step(v, nc.vector.tensor_tensor(x[:, :, :], x[:, :, :], m.agg[:, :, :], ALU.add), chain, 1)
                step(v, nc.vector.tensor_reduce(tot[:, :], x[:, :, :], X, ALU.add), chain, 2)
                step(v, nc.vector.tensor_scalar(mean[:, :], tot[:, :], 1.0 / D, None, ALU.mult), chain, 3)
                nc.vector.tensor_tensor(x[:, :, :], x[:, :, :], mean[:, :].unsqueeze(2).to_broadcast(wide),
                                        ALU.subtract).then_inc(cent_ok, 1)
                v.wait_ge(sq_ok, 1)
                step(v, nc.vector.tensor_reduce(tot[:, :], sq[:, :, :], X, ALU.add), chain, 4)
                nc.vector.tensor_scalar(var[:, :], tot[:, :], 1.0 / D, EPS, ALU.mult, ALU.add).then_inc(var_ok, 1)
                v.wait_ge(root_ok, 1)
                step(v, nc.vector.reciprocal(inv[:, :], root[:, :]), chain, 5)
                nc.vector.tensor_tensor(m.agg[:, :, :], x[:, :, :], inv[:, :].unsqueeze(2).to_broadcast(wide),
                                        ALU.mult).then_inc(out_ok, 1)

            @block.scalar
            def _(act):
                act.wait_ge(cent_ok, 1)
                nc.scalar.activation(sq[:, :, :], x[:, :, :], ACT.Square).then_inc(sq_ok, 1)
                act.wait_ge(var_ok, 1)
                nc.scalar.activation(root[:, :], var[:, :], ACT.Sqrt).then_inc(root_ok, 1)
def l1_self_terms(nc, d, m):
    ctx, sb, pb, sem = scope(nc, "selft")
    with ctx:
        col, cols, wt, we = sb("col", [DE, 1]), sb("cols", [DE, P]), sb("wt", [DE, D]), sb("we", [DE, 2 * D])
        ps = pb("ps", [P, 3 * D])
        w_in, cols_ok, mm = (sem(x) for x in ("w_in", "cols_ok", "mm"))
        with nc.Block() as block:
            @block.sync
            def _(sp):
                sp.dma_start(col[:, :], d.time0).then_inc(w_in, 16)
                sp.dma_start(wt[:, :], d.wt).then_inc(w_in, 16)
                sp.dma_start(we[:, :], d.we[DE:2 * DE, :]).then_inc(w_in, 16)

            @block.vector
            def _(v):
                v.wait_ge(w_in, 48)
                nc.vector.tensor_copy(cols[:, :], col[:, 0:1].to_broadcast([DE, P])).then_inc(cols_ok, 1)
                v.wait_ge(mm, 1)
                nc.vector.tensor_copy(m.selfadd[:, :], ps[:, :])

            @block.tensor
            def _(pe):
                pe.wait_ge(cols_ok, 1)
                nc.tensor.matmul(ps[:, 0:D], cols[:, :], wt[:, :], start=True, stop=True)
                nc.tensor.matmul(ps[:, D:3 * D], cols[:, :], we[:, :], start=True, stop=True).then_inc(mm, 1)


def l1_tables(nc, d, m):
    ctx, sb, pb, sem = scope(nc, "tables")
    R = 3
    NR = NB - NB % R
    with ctx:
        wx, bx = sb("wx", [P, 3 * D]), sb("bx", [P, 3 * D])
        xb = [sb(f"xb{k}", [P, D]) for k in range(R)]
        xbT = [sb(f"xbT{k}", [P, D]) for k in range(R)]
        tn = [sb(f"tn{k}", [P, TN_W]) for k in range(R)]
        me = [sb(f"me{k}", [P, 3 * D]) for k in range(R)]
        kr = [sb(f"kr{k}", [P, D]) for k in range(R)]
        qk = [sb(f"qk{k}", [P, D]) for k in range(R)]
        score = [sb(f"score{k}", [P, HEADS]) for k in range(R)]
        ps_t = [pb(f"ps_t{k}", [P, D]) for k in range(R)]
        ps = [pb(f"ps{k}", [P, 3 * D]) for k in range(R)]
        w_in, turned, xbT_ok, mm, tn_ok, me_ok, kr_ok, qk_ok, score_ok, kept = (
            sem(x) for x in ("w_in", "turned", "xbT_ok", "mm", "tn_ok", "me_ok", "kr_ok", "qk_ok", "score_ok", "kept"))
        xb_in = [sem(f"xb_in{k}") for k in range(R)]
        stored = [sem(f"stored{k}") for k in range(R)]

        def blocks(eng, one):
            def body(i):
                for k in range(R):
                    one(i, k, i * R + k + 1)
            turns(eng, NR // R, body)
            for k in range(NB - NR):
                one(NR // R, k, NR + k + 1)

        with nc.Block() as block:
            @block.sync
            def _(sp):
                sp.dma_start(wx[:, :], d.wx).then_inc(w_in, 16)
                sp.dma_start(bx[:, :], d.bx.partition_broadcast(P)).then_inc(w_in, 16)

                def one(i, k, n):
                    if not first(i):
                        sp.wait_ge(turned, n - R)
                    sp.dma_start(xb[k][:, :], d.x1[ds((n - 1) * P, P), :]).then_inc(xb_in[k], 16)
                blocks(sp, one)

            @block.tensor
            def _(pe):
                pe.wait_ge(w_in, 32)

                def one(i, k, n):
                    pe.wait_ge(xb_in[k], i * 16 + 16)
                    if not first(i):
                        pe.wait_ge(xbT_ok, n - R)
                    nc.tensor.transpose(ps_t[k][:, :], xb[k][:, :], m.ident[:, :]).then_inc(turned, 1)
                    pe.wait_ge(xbT_ok, n)
                    if not first(i):
                        pe.wait_ge(tn_ok, (n - R) * 2)
                    nc.tensor.matmul(ps[k][:, :], xbT[k][:, :], wx[:, :], start=True, stop=True).then_inc(mm, 1)
                blocks(pe, one)

            @block.scalar
            def _(act):
                def one(i, k, n):
                    act.wait_ge(turned, n)
                    if not first(i):
                        act.wait_ge(mm, n - R)
                    nc.scalar.activation(xbT[k][:, :], ps_t[k][:, :], ACT.Copy).then_inc(xbT_ok, 1)
                    act.wait_ge(tn_ok, n * 2)
                    act.dma_start(d.tn[ds((n - 1) * P, P), :], tn[k][:, :]).then_inc(stored[k], 16)
                blocks(act, one)
                for k in range(R):
                    act.wait_ge(stored[k], 16 * (NR // R + (k < NB - NR)))

            @block.vector
            def _(v):
                def one(i, k, n):
                    if not first(i):
                        v.wait_ge(stored[k], i * 16)
                    nc.vector.tensor_scalar(tn[k][:, 3 * D:TN_W], m.place[:, ds(n - 1, 1), :].rearrange("p a w -> p (a w)"),
                                            0.0, None, ALU.add).then_inc(tn_ok, 1)
                    v.wait_ge(mm, n)
                    nc.vector.tensor_tensor(tn[k][:, 0:3 * D], ps[k][:, :], bx[:, :], ALU.add).then_inc(tn_ok, 1)
                    v.wait_ge(tn_ok, n * 2)
                    step(v, nc.vector.tensor_tensor(me[k][:, :], tn[k][:, 0:3 * D], m.selfadd[:, :], ALU.add), me_ok, n)
                    step(v, nc.vector.tensor_scalar(kr[k][:, :], me[k][:, D:2 * D], 0.0, None, ALU.max), kr_ok, n)
                    step(v, nc.vector.scalar_tensor_tensor(qk[k][:, :], me[k][:, 0:D], 0.0, kr[k][:, :], ALU.max,
                                                           ALU.mult), qk_ok, n)
                    step(v, nc.vector.tensor_reduce(score[k][:, :], qk[k][:, :].rearrange("p (h f) -> p h f", h=HEADS),
                                                    X, ALU.add), score_ok, n)
                    nc.vector.tensor_scalar(m.top[:, ds(n - 1, 1), :].rearrange("p a h -> p (a h)"), score[k][:, :],
                                            0.0, None, ALU.add)
                    nc.vector.tensor_scalar(m.agg[:, ds(n - 1, 1), :].rearrange("p a f -> p (a f)"),
                                            me[k][:, 2 * D:3 * D], 0.0, None, ALU.add)
                nc.vector.memset(m.den[:, :, :], 1.0)
                blocks(v, one)


def l1_edges(nc, d, m):
    ctx, sb, pb, sem = scope(nc, "edges")
    with ctx:
        wt, we = sb("wt", [DE, D]), sb("we", [P, 2 * D])
        idx = [sb(f"idx{p}", [P, 2 * CG], i32) for p in range(2)]
        ft = [sb(f"ft{p}", [DE, GE]) for p in range(2)]
        fe = [sb(f"fe{p}", [P, GE]) for p in range(2)]
        rows = [[sb(f"rows{w}{p}", [P, CG, TN_W]) for p in range(2)] for w in range(2)]
        qk = [[sb(f"qk{w}{p}", [P, CG, 2 * D]) for p in range(2)] for w in range(2)]
        prod = [[sb(f"prod{w}{p}", [P, CG, D]) for p in range(2)] for w in range(2)]
        msg = [[sb(f"msg{w}{p}", [P, CG, MSG_W]) for p in range(2)] for w in range(2)]
        to_f = [sb(f"to_f{p}", [P, CG]) for p in range(2)]
        to = [[sb(f"to{w}{p}", [P, CG], i32) for p in range(2)] for w in range(2)]
        zero = sb("zero", [SLOTS, MSG_W])
        ps = [pb(f"ps{p}", [P, CG, BANK]) for p in range(2)]
        w_in, mm, added, v_ok, relued, prod_ok, msg_ok, to_ok, passed, zero_ok, zero_out = (
            sem(x) for x in ("w_in", "mm", "added", "v_ok", "relued", "prod_ok", "msg_ok", "to_ok", "passed", "zero_ok",
                             "zero_out"))
        idx_in, f_in, got, put = ([sem(f"{x}{p}") for p in range(2)] for x in ("idx_in", "f_in", "got", "put"))
        GOT = 2 * CG * 16
        with nc.Block() as block:
            @block.sync
            def _(sp):
                sp.dma_start(wt[:, :], d.wt).then_inc(w_in, 16)
                sp.dma_start(we[:, :], d.we).then_inc(w_in, 16)
                sp.wait_ge(zero_ok, 1)
                for w in range(2):
                    sp.dma_start(d.msg_of[w][EP:EP + SLOTS, :], zero[:, :]).then_inc(zero_out, 16)

                def body(i):
                    for p in range(2):
                        if not first(i):
                            sp.wait_ge(got[p], i * GOT)
                        sp.dma_start(idx[p][:, :], d.idx[ds(i * 2 + p, 1), :, :].rearrange("a p c -> (a p) c")
                                     ).then_inc(idx_in[p], 16)
                        if not first(i):
                            sp.wait_ge(mm, i * 2 + p - 1)
                        sp.dma_start(ft[p][:, :], d.ft[:, ds(i * (2 * GE) + p * GE, GE)]).then_inc(f_in[p], 16)
                        sp.dma_start(fe[p][:, :], d.fe[:, ds(i * (2 * GE) + p * GE, GE)]).then_inc(f_in[p], 16)
                turns(sp, GROUPS // 2, body)
                sp.wait_ge(zero_out, 32)

            @block.gpsimd
            def _(g):
                def gather(i, p, n):
                    hold(g, idx_in[p], i * 16 + 16, passed)
                    if not first(i):
                        hold(g, to_ok, (n - 2) * 2, passed)
                    for c in range(CG):
                        for w in range(2):
                            g.indirect_dma_start(rows[w][p][:, c, :], None, d.tn, bass.IndirectOffsetOnAxis(
                                ap=idx[p][:, w * CG + c:w * CG + c + 1], axis=0)).then_inc(got[p], 16)

                def scatter(p, n):
                    hold(g, msg_ok, n * 2, passed)
                    hold(g, to_ok, n * 2, passed)
                    for c in range(CG):
                        for w in range(2):
                            g.indirect_dma_start(d.msg_of[w], bass.IndirectOffsetOnAxis(
                                ap=to[w][p][:, c:c + 1], axis=0), msg[w][p][:, c, :], None).then_inc(put[p], 16)

                def body(i):
                    gather(i, 0, i * 2 + 1)
                    if not first(i):
                        scatter(1, i * 2)
                    gather(i, 1, i * 2 + 2)
                    scatter(0, i * 2 + 1)
                turns(g, GROUPS // 2, body)
                scatter(1, GROUPS)
                for p in range(2):
                    g.wait_ge(put[p], GOT * (GROUPS // 2))

            @block.tensor
            def _(pe):
                pe.wait_ge(w_in, 32)

                def body(i):
                    for p in range(2):
                        n = i * 2 + p + 1
                        pe.wait_ge(f_in[p], i * 32 + 32)
                        if not first(i):
                            pe.wait_ge(v_ok, (n - 2) * 2)
                        for c in range(CG):
                            nc.tensor.matmul(ps[p][:, c, D:3 * D], fe[p][:, c * P:(c + 1) * P], we[:, :],
                                             start=True, stop=True)
                            last = nc.tensor.matmul(ps[p][:, c, 0:D], ft[p][:, c * P:(c + 1) * P], wt[:, :],
                                                    start=True, stop=True)
                        last.then_inc(mm, 1)
                turns(pe, GROUPS // 2, body)

            @block.vector
            def _(v):
                nc.vector.memset(zero[:, :], 0.0).then_inc(zero_ok, 1)

                def finish(p, n):
                    for w in range(2):
                        v.wait_ge(relued, (n - 1) * 2 + w + 1)
                        step(v, nc.vector.tensor_tensor(prod[w][p][:, :, :], qk[w][p][:, :, 0:D],
                                                        qk[w][p][:, :, D:2 * D], ALU.mult), prod_ok, (n - 1) * 2 + w + 1)
                        nc.vector.tensor_reduce(msg[w][p][:, :, D:MSG_W],
                                                prod[w][p][:, :, :].rearrange("p c (h f) -> p c h f", h=HEADS),
                                                X, ALU.add).then_inc(msg_ok, 1)

                def body(i):
                    for p in range(2):
                        n = i * 2 + p + 1
                        v.wait_ge(mm, n)
                        v.wait_ge(got[p], (i + 1) * GOT)
                        if not first(i):
                            v.wait_ge(put[p], i * GOT)
                            v.wait_ge(msg_ok, (n - 2) * 2)
                        for w in range(2):
                            nc.vector.tensor_tensor(qk[w][p][:, :, 0:D], ps[p][:, :, 0:D], rows[w][p][:, :, 0:D],
                                                    ALU.add).then_inc(added, 1)
                            nc.vector.tensor_tensor(qk[w][p][:, :, D:2 * D], ps[p][:, :, D:2 * D],
                                                    rows[1 - w][p][:, :, D:2 * D], ALU.add).then_inc(added, 1)
                        for w in range(2):
                            nc.vector.tensor_tensor(msg[w][p][:, :, 0:D], ps[p][:, :, 2 * D:3 * D],
                                                    rows[1 - w][p][:, :, 2 * D:3 * D], ALU.add).then_inc(v_ok, 1)
                        for w in range(2):
                            at = ds(i * (2 * CG) + p * CG, CG)
                            nc.vector.tensor_tensor(to[w][p][:, :], m.rank[:, w, at], rows[w][p][:, :, 3 * D + w],
                                                    ALU.add).then_inc(to_ok, 1)
                        finish(p, n)
                turns(v, GROUPS // 2, body)

            @block.scalar
            def _(act):
                def body(i):
                    for p in range(2):
                        n = i * 2 + p + 1
                        for w in range(2):
                            act.wait_ge(added, (n - 1) * 4 + 2 * w + 2)
                            nc.scalar.activation(qk[w][p][:, :, :], qk[w][p][:, :, :], ACT.Relu).then_inc(relued, 1)
                turns(act, GROUPS // 2, body)


def l1_edges_ordered(nc, d, m):
    ctx, sb, pb, sem = scope(nc, "edgeso")
    R, AH = 4, 3
    with ctx:
        wt, we = sb("wt", [DE, D]), sb("we", [P, 2 * D])
        idx = [sb(f"idx{p}", [P, CG], i32) for p in range(R)]
        ft = [sb(f"ft{p}", [DE, GE]) for p in range(R)]
        fe = [sb(f"fe{p}", [P, GE]) for p in range(R)]
        target = [sb(f"target{p}", [P, GE], u16) for p in range(R)]
        win = [sb(f"win{p}", [P, 3 * D]) for p in range(R)]
        pick = [sb(f"pick{p}", [P, GE]) for p in range(R)]
        rows = [sb(f"rows{p}", [P, CG, TN_W]) for p in range(R)]
        fs = [sb(f"fs{p}", [P, CG, 2 * D]) for p in range(2)]
        ftr = [sb(f"ftr{p}", [P, CG, 2 * D]) for p in range(2)]
        prod = sb("prod", [P, CG, 2 * D])
        msg = [[sb(f"msg{w}{p}", [P, CG, MSG_W]) for p in range(R)] for w in range(2)]
        to = [sb(f"to{p}", [P, CG], i32) for p in range(R)]
        zero = sb("zero", [SLOTS, MSG_W])
        ps = [pb(f"ps{p}", [P, CG, BANK]) for p in range(2)]
        (w_in, picked, mm, added, sv_ok, joined, tv_ok, prod_ok, msg_ok, passed, passed_sp, zero_ok,
         zero_out) = (
            sem(x) for x in ("w_in", "picked", "mm", "added", "sv_ok", "joined", "tv_ok", "prod_ok",
                             "msg_ok", "passed", "passed_sp", "zero_ok", "zero_out"))
        idx_in, f_in, t_in, got, put, stored = (
            [sem(f"{x}{p}") for p in range(R)] for x in ("idx_in", "f_in", "t_in", "got", "put", "stored"))
        GOT = CG * 16
        T = GROUPS // R
        with nc.Block() as block:
            @block.sync
            def _(sp):
                sp.dma_start(wt[:, :], d.wt).then_inc(w_in, 16)
                sp.dma_start(we[:, :], d.we).then_inc(w_in, 16)
                sp.wait_ge(zero_ok, 1)
                for w in range(2):
                    sp.dma_start(d.msg_of[w][EP:EP + SLOTS, :], zero[:, :]).then_inc(zero_out, 16)

                def body(i):
                    for p in range(R):
                        n = i * R + p + 1
                        if not first(i):
                            sp.wait_ge(got[p], i * GOT)
                        sp.dma_start(idx[p][:, :], d.idx[ds(n - 1, 1), :, 0:CG].rearrange("a p c -> (a p) c")
                                     ).then_inc(idx_in[p], 16)
                        if not first(i):
                            sp.wait_ge(picked, n - R)
                        sp.dma_start(target[p][:, :],
                                     d.rowf[1, 0, ds(i * (R * GE) + p * GE, GE)].partition_broadcast(P)
                                     ).then_inc(t_in[p], 16)
                        if not first(i):
                            hold(sp, mm, n - R, passed_sp)
                        sp.dma_start(ft[p][:, :], d.ft[:, ds(i * (R * GE) + p * GE, GE)]).then_inc(f_in[p], 16)
                        sp.dma_start(fe[p][:, :], d.fe[:, ds(i * (R * GE) + p * GE, GE)]).then_inc(f_in[p], 16)
                        if not first(i):
                            hold(sp, joined, n - R, passed_sp)
                        base = sp.value_load(m.bases[0:1, ds(n - 1, 1)], min_val=0, max_val=N)
                        sp.dma_start(win[p][:, :], d.tn[ds(base, P), 0:3 * D]).then_inc(f_in[p], 16)
                turns(sp, T, body)
                sp.wait_ge(zero_out, 32)

            @block.gpsimd
            def _(g):
                def gather(i, p, n):
                    hold(g, idx_in[p], i * 16 + 16, passed)
                    for c in range(CG):
                        g.indirect_dma_start(rows[p][:, c, :], None, d.tn, bass.IndirectOffsetOnAxis(
                            ap=idx[p][:, c:c + 1], axis=0)).then_inc(got[p], 16)

                def scatter(p, n):
                    hold(g, msg_ok, n * 2, passed)
                    for c in range(CG):
                        g.indirect_dma_start(d.msg_of[0], bass.IndirectOffsetOnAxis(
                            ap=to[p][:, c:c + 1], axis=0), msg[0][p][:, c, :], None).then_inc(put[p], 16)

                def body(i):
                    for p in range(R):
                        n = i * R + p + 1
                        gather(i, p, n)
                        if not (first(i) and p < AH):
                            scatter((p - AH) % R, n - AH)
                turns(g, T, body)
                for n in range(GROUPS - AH, GROUPS):
                    scatter(n % R, n + 1)
                for p in range(R):
                    g.wait_ge(put[p], GOT * T)

            @block.tensor
            def _(pe):
                pe.wait_ge(w_in, 32)

                def join(p, n):
                    pe.wait_ge(picked, n)
                    pe.wait_ge(sv_ok, n)
                    for c in range(CG):
                        last = nc.tensor.matmul(ps[p % 2][:, c, 0:3 * D], pick[p][:, c * P:(c + 1) * P], win[p][:, :],
                                                start=False, stop=True, skip_group_check=True)
                    last.then_inc(joined, 1)

                def body(i):
                    for p in range(R):
                        n = i * R + p + 1
                        pe.wait_ge(f_in[p], i * 48 + 48)
                        if not (first(i) and p < 2):
                            pe.wait_ge(tv_ok, n - 2)
                        for c in range(CG):
                            nc.tensor.matmul(ps[p % 2][:, c, 0:D], ft[p][:, c * P:(c + 1) * P], wt[:, :],
                                             start=True, stop=False, skip_group_check=True)
                            last = nc.tensor.matmul(ps[p % 2][:, c, D:3 * D], fe[p][:, c * P:(c + 1) * P], we[:, :],
                                                    start=False, stop=False, skip_group_check=True)
                        last.then_inc(mm, 1)
                        if not (first(i) and p == 0):
                            join((p - 1) % R, n - 1)
                turns(pe, T, body)
                join(R - 1, GROUPS)

            @block.vector
            def _(v):
                nc.vector.memset(zero[:, :], 0.0).then_inc(zero_ok, 1)

                def finish(p, n):
                    v.wait_ge(added, n)
                    v.wait_ge(tv_ok, n)
                    step(v, nc.vector.scalar_tensor_tensor(prod[:, :, :], fs[p % 2][:, :, :], 0.0, ftr[p % 2][:, :, :],
                                                           ALU.max, ALU.mult), prod_ok, n)
                    for w in range(2):
                        nc.vector.tensor_reduce(msg[w][p][:, :, D:MSG_W],
                                                prod[:, :, w * D:(w + 1) * D].rearrange("p c (h f) -> p c h f", h=HEADS),
                                                X, ALU.add).then_inc(msg_ok, 1)
                    v.wait_ge(msg_ok, n * 2)

                def body(i):
                    for p in range(R):
                        n = i * R + p + 1
                        v.wait_ge(t_in[p], i * 16 + 16)
                        if not first(i):
                            v.wait_ge(joined, n - R)
                        nc.vector.tensor_scalar(pick[p][:, :], target[p][:, :], m.window[:, ds(n - 1, 1)], None,
                                                ALU.is_equal).then_inc(picked, 1)
                        v.wait_ge(mm, n)
                        v.wait_ge(got[p], i * GOT + GOT)
                        if not first(i):
                            v.wait_ge(put[p], i * GOT)
                            v.wait_ge(stored[p], i * 16)
                        nc.vector.tensor_tensor(fs[p % 2][:, :, :], ps[p % 2][:, :, 0:2 * D], rows[p][:, :, 0:2 * D],
                                                ALU.add).then_inc(added, 1)
                        nc.vector.tensor_tensor(msg[1][p][:, :, 0:D], ps[p % 2][:, :, 2 * D:3 * D],
                                                rows[p][:, :, 2 * D:3 * D], ALU.add).then_inc(sv_ok, 1)
                        nc.vector.tensor_tensor(to[p][:, :], m.rank[:, 0, ds(i * (R * CG) + p * CG, CG)],
                                                rows[p][:, :, 3 * D], ALU.add)
                        if not (first(i) and p == 0):
                            finish((p - 1) % R, n - 1)
                turns(v, T, body)
                finish(R - 1, GROUPS)

            @block.scalar
            def _(act):
                def store(i, p, n):
                    act.wait_ge(msg_ok, n * 2)
                    act.dma_start(d.msg_of[1][ds((n - 1) * GE, GE), :].rearrange("(p c) f -> p c f", c=CG),
                                  msg[1][p][:, :, :]).then_inc(stored[p], 16)

                def body(i):
                    for p in range(R):
                        n = i * R + p + 1
                        act.wait_ge(joined, n)
                        if not (first(i) and p < 2):
                            act.wait_ge(prod_ok, n - 2)
                        for half in range(2):
                            nc.scalar.activation(ftr[p % 2][:, :, half * D:(half + 1) * D],
                                                 ps[p % 2][:, :, (1 - half) * D:(2 - half) * D],
                                                 ACT.Relu)
                        if not first(i):
                            act.wait_ge(put[p], i * GOT)
                        nc.scalar.activation(msg[0][p][:, :, 0:D], ps[p % 2][:, :, 2 * D:3 * D], ACT.Copy
                                             ).then_inc(tv_ok, 1)
                        if not (first(i) and p == 0):
                            store(i, (p - 1) % R, n - 1)
                turns(act, T, body)
                store(T, R - 1, GROUPS)
                for p in range(R):
                    act.wait_ge(stored[p], 16 * T)


def l1_softmax(nc, d, m):
    ctx, sb, pb, sem = scope(nc, "soft")
    with ctx:
        R = SOFT_RING
        U = 2 * R
        TOP_UP = BANK // D
        run = [sb(f"run{p}", [P, 2, SLOTS, MSG_W]) for p in range(R)]
        at_f, at_c, left = ([sb(f"{x}{p}", [P, 2]) for p in range(R)] for x in ("at_f", "at_c", "left"))
        at = [sb(f"at{p}", [P, 2], i32) for p in range(R)]
        off = [sb(f"off{p}", [P, 2, SLOTS]) for p in range(R)]
        score = [sb(f"score{p}", [P, 2 * SLOTS, HEADS]) for p in range(R)]
        under = [sb(f"under{p}", [P, 2 * SLOTS, HEADS]) for p in range(R)]
        w = [sb(f"w{p}", [P, 2 * SLOTS, HEADS]) for p in range(R)]
        most, top, fall, corr, wsum, den = ([sb(f"{x}{p}", [P, HEADS]) for p in range(R)]
                                            for x in ("most", "top", "fall", "corr", "wsum", "den"))
        prod = [sb(f"prod{q}", [P, 2 * SLOTS, D]) for q in range(2)]
        part = [sb(f"part{p}", [P, D]) for p in range(R)]
        old = [sb(f"old{p}", [P, D]) for p in range(R)]
        passed_slots = sb("passed_slots", [P, 2])
        ps = [pb(f"ps{p}", [P, TOP_UP, D]) for p in range(R)]
        got = [sem(f"got{p}") for p in range(R)]
        (at_f_ok, at_c_ok, at_ok, left_ok, off_ok, score_ok, most_ok, top_ok, under_ok, w_ok, wsum_ok, den_ok,
         prod_ok, added, part_ok, old_ok, summed, passed, slots_ok) = (
            sem(x) for x in ("at_f_ok", "at_c_ok", "at_ok", "left_ok", "off_ok", "score_ok", "most_ok", "top_ok",
                             "under_ok", "w_ok", "wsum_ok", "den_ok", "prod_ok", "added", "part_ok", "old_ok", "summed",
                             "passed", "slots_ok"))
        with nc.Block() as block:
            @block.vector
            def _(v):
                rounds = v.value_load(m.trips[0:1, 2:3], min_val=1, max_val=EP // SLOTS + 1)
                step(v, nc.vector.memset(passed_slots[:, :], 0.0), slots_ok, 1)

                def place_f(n, b, p):
                    nc.vector.tensor_tensor(at_f[p][:, :], m.place[:, ds(b, 1), :].rearrange("p a w -> p (a w)"),
                                            passed_slots[:, :], ALU.add).then_inc(at_f_ok, 1)

                def place_c(n, p):
                    v.wait_ge(at_f_ok, n)
                    nc.vector.tensor_scalar(at_c[p][:, :], at_f[p][:, :], float(EP), float(MSG_W), ALU.min,
                                            ALU.mult).then_inc(at_c_ok, 1)

                def place_i(n, p):
                    v.wait_ge(at_c_ok, n)
                    nc.vector.tensor_copy(at[p][:, :], at_c[p][:, :]).then_inc(at_ok, 1)

                def denominators(n, b, p):
                    state_den = m.den[:, ds(b, 1), :].rearrange("p a h -> p (a h)")
                    nc.vector.tensor_reduce(wsum[p][:, :], w[p][:, :, :].rearrange("p s h -> p h s"),
                                            X, ALU.add).then_inc(wsum_ok, 1)
                    nc.vector.tensor_tensor(den[p][:, :], state_den, corr[p][:, :], ALU.mult).then_inc(den_ok, 1)
                    nc.vector.tensor_tensor(
                        old[p][:, :].rearrange("p (h f) -> p h f", h=HEADS),
                        m.agg[:, ds(b, 1), :].rearrange("p a (h f) -> p (a h) f", h=HEADS),
                        corr[p][:, :].unsqueeze(2).to_broadcast([P, HEADS, DK]), ALU.mult).then_inc(old_ok, 1)
                    v.wait_ge(wsum_ok, n)
                    v.wait_ge(den_ok, n * 2 - 1)
                    nc.vector.tensor_tensor(state_den, den[p][:, :], wsum[p][:, :], ALU.add).then_inc(den_ok, 1)

                def last_slots(n, p):
                    v.wait_ge(added, n)
                    nc.vector.tensor_reduce(part[p][:, :], ps[p].rearrange("p s f -> p f s"), X, ALU.add
                                            ).then_inc(part_ok, 1)

                def sums(n, b, p):
                    v.wait_ge(part_ok, n)
                    v.wait_ge(old_ok, n)
                    nc.vector.tensor_tensor(m.agg[:, ds(b, 1), :].rearrange("p a f -> p (a f)"), old[p][:, :],
                                            part[p][:, :], ALU.add).then_inc(summed, 1)

                for b in range(AHEAD):
                    place_f(b + 1, b, b)
                    place_c(b + 1, b)
                    place_i(b + 1, b)
                with v.Fori(0, rounds) as r:
                    def body(i):
                        for k in range(U):
                            n, b, p = r * NB + i * U + k + 1, i * U + k, k % R
                            q = (p + AHEAD) % R
                            one_before = not (first(i) and k == 0)
                            two_before = not (first(i) and k < 2)
                            state_top = m.top[:, ds(b, 1), :].rearrange("p a h -> p (a h)")
                            slots = run[p][:, :, :, :].rearrange("p x s f -> p (x s) f")
                            place_f(n + AHEAD, b + AHEAD, q)
                            nc.vector.tensor_tensor(left[p][:, :], m.deg[:, :, ds(b, 1)].rearrange("p w a -> p (w a)"),
                                                    passed_slots[:, :], ALU.subtract).then_inc(left_ok, 1)
                            place_c(n + AHEAD, q)
                            v.wait_ge(left_ok, n)
                            for x in range(2):
                                nc.vector.tensor_scalar(off[p][:, x, :], m.iota_row[:, 0:SLOTS], left[p][:, x:x + 1],
                                                        NEG, ALU.is_ge, ALU.mult).then_inc(off_ok, 1)
                            place_i(n + AHEAD, q)
                            v.wait_ge(off_ok, n * 2)
                            v.wait_ge(got[p], r * (NB // R * 32) + i * (U // R * 32) + (k // R) * 32 + 32)
                            nc.vector.tensor_tensor(
                                score[p][:, :, :], slots[:, :, D:MSG_W],
                                off[p][:, :, :].rearrange("p x s -> p (x s)").unsqueeze(2)
                                .to_broadcast([P, 2 * SLOTS, HEADS]), ALU.add).then_inc(score_ok, 1)
                            if two_before:
                                last_slots(n - 2, (p - 2) % R)
                            v.wait_ge(score_ok, n)
                            nc.vector.tensor_reduce(most[p][:, :], score[p][:, :, :].rearrange("p s h -> p h s"),
                                                    X, ALU.max).then_inc(most_ok, 1)
                            if two_before:
                                sums(n - 2, b - 2, (p - 2) % R)
                            v.wait_ge(most_ok, n)
                            step(v, nc.vector.tensor_tensor(top[p][:, :], most[p][:, :], state_top, ALU.max), top_ok, n)
                            nc.vector.tensor_tensor(fall[p][:, :], state_top, top[p][:, :], ALU.subtract
                                                    ).then_inc(under_ok, 1)
                            nc.vector.tensor_tensor(under[p][:, :, :], score[p][:, :, :],
                                                    top[p][:, :].unsqueeze(1).to_broadcast([P, 2 * SLOTS, HEADS]),
                                                    ALU.subtract).then_inc(under_ok, 1)
                            if one_before:
                                denominators(n - 1, b - 1, (p - 1) % R)
                            v.wait_ge(w_ok, n * 2)
                            for x in range(2):
                                half = slice(x * SLOTS, (x + 1) * SLOTS)
                                nc.vector.tensor_tensor(
                                    prod[k % 2][:, half, :].rearrange("p s (h f) -> p s h f", h=HEADS),
                                    slots[:, half, 0:D].rearrange("p s (h f) -> p s h f", h=HEADS),
                                    w[p][:, half, :].unsqueeze(3).to_broadcast([P, SLOTS, HEADS, DK]),
                                    ALU.mult).then_inc(prod_ok, 1)
                            nc.vector.tensor_scalar(state_top, top[p][:, :], 0.0, None, ALU.add)
                    turns(v, NB // U, body)
                    n = r * NB + NB
                    denominators(n, NB - 1, R - 1)
                    for back in (1, 0):
                        last_slots(n - back, R - 1 - back)
                        sums(n - back, NB - 1 - back, R - 1 - back)
                    step(v, nc.vector.tensor_scalar(passed_slots[:, :], passed_slots[:, :], float(SLOTS), None,
                                                    ALU.add), slots_ok, r + 2)

            @block.tensor
            def _(pe):
                rounds = pe.value_load(m.trips[0:1, 2:3], min_val=1, max_val=EP // SLOTS + 1)
                steps = 2 * SLOTS // TOP_UP
                with pe.Fori(0, rounds) as r:
                    with pe.Fori(0, NB // U) as j:
                        for k in range(U):
                            n, p = r * NB + j * U + k + 1, k % R
                            for x in range(2):
                                pe.wait_ge(prod_ok, n * 2 - 1 + x)
                                for c in range(x * steps // 2, (x + 1) * steps // 2):
                                    last = nc.tensor.matmul(ps[p], m.ident[:, :],
                                                            prod[k % 2][:, c * TOP_UP:(c + 1) * TOP_UP, :],
                                                            start=c == 0, stop=c == steps - 1)
                            last.then_inc(added, 1)

            @block.scalar
            def _(act):
                rounds = act.value_load(m.trips[0:1, 2:3], min_val=1, max_val=EP // SLOTS + 1)
                with act.Fori(0, rounds) as r:
                    with act.Fori(0, NB // R) as j:
                        for p in range(R):
                            n = r * NB + j * R + p + 1
                            act.wait_ge(under_ok, n * 2)
                            nc.scalar.activation(corr[p][:, :], fall[p][:, :], ACT.Exp, scale=SCALE).then_inc(w_ok, 1)
                            nc.scalar.activation(w[p][:, :, :], under[p][:, :, :], ACT.Exp, scale=SCALE
                                                 ).then_inc(w_ok, 1)

            @block.gpsimd
            def _(g):
                rounds = g.value_load(m.trips[0:1, 2:3], min_val=1, max_val=EP // SLOTS + 1)

                def fetch(n, p):
                    hold(g, at_ok, n, passed)
                    for x in range(2):
                        flat = d.msg_of[x].rearrange("n f -> (n f)").rearrange("(n o) -> n o", o=1)
                        g.indirect_dma_start(run[p][:, x, :, :].rearrange("p s f -> p (s f)"), None, flat,
                                             bass.IndirectOffsetOnAxis(ap=at[p][:, x:x + 1], axis=0)
                                             ).then_inc(got[p], 16)

                for b in range(AHEAD):
                    fetch(b + 1, b)
                with g.Fori(0, rounds) as r:
                    with g.Fori(0, NB // R) as j:
                        for p in range(R):
                            fetch(r * NB + j * R + p + 1 + AHEAD, (p + AHEAD) % R)
                for p in range(AHEAD):
                    g.wait_ge(got[p], rounds * (NB // R * 32) + 32)


def l1_out(nc, d, m):
    ctx, sb, pb, sem = scope(nc, "out")
    G = 5
    W = G * P
    BATCHES = NB // G
    with ctx:
        wa, wb, w2, b2 = sb("wa", [P, D]), sb("wb", [P, D]), sb("w2", [P, D]), sb("b2", [P, D])
        inv = sb("inv", [P, NB, HEADS])
        z = sb("z", [P, NB, D])
        x1, emb = ([sb(f"{x}{p}", [P, G, D]) for p in range(2)] for x in ("x1", "emb"))
        embT, x1T, hid = ([sb(f"{x}{p}", [P, W]) for p in range(2)] for x in ("embT", "x1T", "hid"))
        tot, mean, sqtot, var, root, rinv = (sb(x, [P, NB]) for x in ("tot", "mean", "sqtot", "var", "root", "rinv"))
        ps_e, ps_x, ps_h = (pb(x, [P, W]) for x in ("ps_e", "ps_x", "ps_h"))
        ps_y = pb("ps_y", [P, G, D])
        (w_in, inv_ok, emb_ok, x1b_ok, turned_x, turned_e, copied_x, copied_e, mm_h, hid_ok, mm_y, z_ok, chain,
         cent_ok, sq_ok, var_ok, root_ok, out_ok, stored) = (
            sem(x) for x in ("w_in", "inv_ok", "emb_ok", "x1b_ok", "turned_x", "turned_e", "copied_x", "copied_e",
                             "mm_h", "hid_ok", "mm_y", "z_ok", "chain", "cent_ok", "sq_ok", "var_ok", "root_ok",
                             "out_ok", "stored"))
        x1_in = [sem(f"x1_in{p}") for p in range(2)]
        halves = [slice(0, NB // 2), slice(NB // 2, NB)]
        with nc.Block() as block:
            @block.sync
            def _(sp):
                sp.dma_start(wa[:, :], d.l1_w1[0:D, :]).then_inc(w_in, 16)
                sp.dma_start(wb[:, :], d.l1_w1[D:2 * D, :]).then_inc(w_in, 16)
                sp.dma_start(w2[:, :], d.l1_w2).then_inc(w_in, 16)
                sp.dma_start(b2[:, :], d.l1_b2.partition_broadcast(P)).then_inc(w_in, 16)

                def body(i):
                    for p in range(2):
                        if not first(i):
                            sp.wait_ge(x1b_ok, i * 2 + p - 1)
                            sp.wait_ge(turned_x, i * 2 + p - 1)
                        sp.dma_start(x1[p][:, :, :],
                                     d.x1[ds(i * (2 * W) + p * W, W), :].rearrange("(b p) f -> p b f", p=P)
                                     ).then_inc(x1_in[p], 16)
                turns(sp, BATCHES // 2, body)
                out_rows = d.out.rearrange("(b p) f -> p b f", p=P)
                for h, part in enumerate(halves):
                    sp.wait_ge(out_ok, h + 1)
                    sp.dma_start(out_rows[:, part, :], z[:, part, :]).then_inc(stored, 16)
                sp.wait_ge(stored, 32)

            @block.tensor
            def _(pe):
                pe.wait_ge(w_in, 64)

                def second(i, p, n):
                    pe.wait_ge(hid_ok, n)
                    if not (first(i) and p == 0):
                        pe.wait_ge(z_ok, n - 1)
                    for b in range(G):
                        last = nc.tensor.matmul(ps_y[:, b, :], hid[p][:, b * P:(b + 1) * P], w2[:, :],
                                                start=True, stop=True)
                    last.then_inc(mm_y, 1)

                def body(i):
                    for p in range(2):
                        n = i * 2 + p + 1
                        pe.wait_ge(x1_in[p], i * 16 + 16)
                        if not (first(i) and p == 0):
                            pe.wait_ge(copied_x, n - 1)
                        for b in range(G):
                            last = nc.tensor.transpose(ps_x[:, b * P:(b + 1) * P], x1[p][:, b, :], m.ident[:, :])
                        last.then_inc(turned_x, 1)
                        pe.wait_ge(emb_ok, n)
                        if not (first(i) and p == 0):
                            pe.wait_ge(copied_e, n - 1)
                        for b in range(G):
                            last = nc.tensor.transpose(ps_e[:, b * P:(b + 1) * P], emb[p][:, b, :], m.ident[:, :])
                        last.then_inc(turned_e, 1)
                        if not (first(i) and p == 0):
                            second(i if p else 1, 1 - p, n - 1)
                        pe.wait_ge(copied_x, n)
                        pe.wait_ge(copied_e, n)
                        for at in range(0, W, BANK):
                            part = slice(at, min(at + BANK, W))
                            nc.tensor.matmul(ps_h[:, part], wa[:, :], embT[p][:, part], start=True, stop=False)
                            last = nc.tensor.matmul(ps_h[:, part], wb[:, :], x1T[p][:, part], start=False, stop=True)
                        last.then_inc(mm_h, 1)
                turns(pe, BATCHES // 2, body)
                second(1, 1, BATCHES)

            @block.scalar
            def _(act):
                def body(i):
                    for p in range(2):
                        n = i * 2 + p + 1
                        act.wait_ge(turned_e, n)
                        nc.scalar.activation(embT[p][:, :], ps_e, ACT.Copy).then_inc(copied_e, 1)
                        act.wait_ge(mm_h, n)
                        nc.scalar.activation(hid[p][:, :], ps_h, ACT.Relu, bias=m.cols[:, 5:6]).then_inc(hid_ok, 1)
                turns(act, BATCHES // 2, body)
                for h, part in enumerate(halves):
                    act.wait_ge(cent_ok, h + 1)
                    nc.scalar.activation(m.agg[:, part, :], z[:, part, :], ACT.Square).then_inc(sq_ok, 1)
                for h, part in enumerate(halves):
                    act.wait_ge(var_ok, h + 1)
                    nc.scalar.activation(root[:, part], var[:, part], ACT.Sqrt).then_inc(root_ok, 1)

            @block.vector
            def _(v):
                v.wait_ge(w_in, 64)
                step(v, nc.vector.reciprocal(inv[:, :, :], m.den[:, :, :]), inv_ok, 1)

                def blocks(i, p):
                    return ds(i * (2 * G) + p * G, G)

                def finish(i, p, n):
                    v.wait_ge(mm_y, n)
                    v.wait_ge(x1b_ok, n)
                    nc.vector.tensor_tensor(z[:, blocks(i, p), :], z[:, blocks(i, p), :], ps_y, ALU.add
                                            ).then_inc(z_ok, 1)

                def body(i):
                    for p in range(2):
                        n = i * 2 + p + 1
                        nc.vector.tensor_tensor(
                            emb[p][:, :, :].rearrange("p b (h f) -> p (b h) f", h=HEADS),
                            m.agg[:, blocks(i, p), :].rearrange("p b (h f) -> p (b h) f", h=HEADS),
                            inv[:, blocks(i, p), :].rearrange("p b h -> p (b h)").unsqueeze(2)
                            .to_broadcast([P, G * HEADS, DK]), ALU.mult).then_inc(emb_ok, 1)
                        v.wait_ge(x1_in[p], i * 16 + 16)
                        nc.vector.tensor_tensor(z[:, blocks(i, p), :], x1[p][:, :, :],
                                                b2[:, :].unsqueeze(1).to_broadcast([P, G, D]), ALU.add
                                                ).then_inc(x1b_ok, 1)
                        v.wait_ge(turned_x, n)
                        nc.vector.tensor_copy(x1T[p][:, :], ps_x).then_inc(copied_x, 1)
                        if not (first(i) and p == 0):
                            finish(i - 1 + p, 1 - p, n - 1)
                turns(v, BATCHES // 2, body)
                finish(BATCHES // 2 - 1, 1, BATCHES)
                v.wait_ge(z_ok, BATCHES)

                def center(h, part):
                    wide = [P, NB // 2, D]
                    step(v, nc.vector.tensor_reduce(tot[:, part], z[:, part, :], X, ALU.add), chain, h * 2 + 1)
                    step(v, nc.vector.tensor_scalar(mean[:, part], tot[:, part], 1.0 / D, None, ALU.mult),
                         chain, h * 2 + 2)
                    nc.vector.tensor_tensor(z[:, part, :], z[:, part, :],
                                            mean[:, part].unsqueeze(2).to_broadcast(wide),
                                            ALU.subtract).then_inc(cent_ok, 1)

                def spread(h, part):
                    v.wait_ge(sq_ok, h + 1)
                    step(v, nc.vector.tensor_reduce(sqtot[:, part], m.agg[:, part, :], X, ALU.add), chain, h + 5)
                    nc.vector.tensor_scalar(var[:, part], sqtot[:, part], 1.0 / D, EPS, ALU.mult, ALU.add
                                            ).then_inc(var_ok, 1)

                def scale(h, part):
                    wide = [P, NB // 2, D]
                    v.wait_ge(root_ok, h + 1)
                    step(v, nc.vector.reciprocal(rinv[:, part], root[:, part]), chain, h + 7)
                    nc.vector.tensor_tensor(z[:, part, :], z[:, part, :],
                                            rinv[:, part].unsqueeze(2).to_broadcast(wide),
                                            ALU.mult).then_inc(out_ok, 1)

                for what in (center, spread, scale):
                    for h, part in enumerate(halves):
                        what(h, part)


def build(nc, d):
    ctx = ExitStack()
    with ctx:
        def keep(name, shape, dt=f32):
            return ctx.enter_context(nc.sbuf_tensor(name, shape, dt))
        m = Names()
        m.iota_row, m.iota_p, m.ones = keep("iota_row", [P, P]), keep("iota_p", [P, 1]), keep("ones", [P, P])
        m.ident, m.before, m.after = keep("ident", [P, P]), keep("before", [P, P]), keep("after", [P, P])
        m.real, m.cols = keep("real", [P, NB]), keep("cols", [P, 6])
        m.w2t, m.w2ts, m.row2 = keep("w2t", [P, D]), keep("w2ts", [P, D]), keep("row2", [P, D])
        m.selfadd = keep("selfadd", [P, 3 * D])
        m.key, m.lo, m.hi = (keep(x, [P, 2, EP // P]) for x in ("key", "lo", "hi"))
        m.rank, m.where_t = keep("rank", [P, 2, EP // P]), keep("where_t", [P, EP // P])
        m.count, m.deg, m.place = keep("count", [P, 2, NB]), keep("deg", [P, 2, NB]), keep("place", [P, NB + AHEAD, 2])
        m.visits, m.trips = keep("visits", [P, 3], i32), keep("trips", [P, 3], i32)
        m.mv1, m.mv2 = keep("mv1", [P, 2]), keep("mv2", [P, 2])
        m.scale1, m.shift1 = keep("scale1", [P, 1]), keep("shift1", [P, 1])
        m.scale2, m.shift2 = keep("scale2", [P, 1]), keep("shift2", [P, 1])
        m.agg, m.top, m.den = keep("agg", [P, NB, D]), keep("top", [P, NB, HEADS]), keep("den", [P, NB, HEADS])
        m.bases, m.ordered = keep("bases", [1, GROUPS], i32), keep("ordered", [P, 1], i32)
        m.window = keep("window", [P, GROUPS])
        m.inside = keep("inside", [P, EP // P])
        setup(nc, d, m)

        def ordered():
            return nc.values_load(m.ordered[0:1, 0:1], min_val=0, max_val=1) > 0

        with nc.If(ordered()):
            l0_tables(nc, d, m, False, "tab0o")
            l0_first_ordered(nc, d, m)
        with nc.Else():
            rank_targets(nc, d, m)
            places(nc, d, m, 1, "places_t")
            l0_tables(nc, d, m, True, "tab0")
            l0_first(nc, d, m)
        places(nc, d, m, 0, "places_s")
        norm_terms(nc, m, m.mv1, m.cols[:, 0:1], m.cols[:, 1:2], m.scale1, m.shift1, "norm_a")
        l0_second(nc, d, m)
        norm_terms(nc, m, m.mv2, m.cols[:, 2:3], m.cols[:, 3:4], m.scale2, m.shift2, "norm_b")
        fold_second(nc, d, m)
        with nc.If(ordered()):
            l0_third_ordered(nc, d, m)
            places(nc, d, m, 1, "places_o")
        with nc.Else():
            l0_third(nc, d, m)
            l0_gather(nc, d, m)
        layer_norm(nc, d, m)
        l1_self_terms(nc, d, m)
        l1_tables(nc, d, m)
        with nc.If(ordered()):
            l1_edges_ordered(nc, d, m)
        with nc.Else():
            l1_edges(nc, d, m)
        l1_softmax(nc, d, m)
        l1_out(nc, d, m)


def kernel(**inputs):
    import numpy as np
    import concourse.bacc as bacc
    from concourse.bass_utils import run_bass_kernel_spmd

    a = {k: np.asarray(v) for k, v in inputs.items()}

    def rows_to(x, n, fill=0):
        return np.concatenate([x, np.full((n - x.shape[0],) + x.shape[1:], fill, x.dtype)])

    x = rows_to(a["x"], NP_)
    src, dst = rows_to(a["src"], EP, PAD), rows_to(a["dst"], EP, PAD)
    by_chunk = [k.reshape(GROUPS, P, CG).transpose(1, 0, 2).reshape(P, -1) for k in (src, dst)]

    def chunked(x):
        return x.reshape(-1, GROUPS, P, CG).transpose(0, 1, 3, 2).reshape(x.shape)

    ef, tf, et = (chunked(rows_to(a[k], EP).T) for k in ("edge_attr_64", "edge_attr_64_n2", "edge_attr_64_n3"))
    w1 = a["L0_gnn_W1"]
    wq, wk, wv = a["L1_gnn_Wq"], a["L1_gnn_Wk"], a["L1_gnn_Wv"]
    nc = bacc.Bacc("TRN2", target_bir_lowering=False, num_devices=1)
    arrays = {}

    def given(name, v):
        arrays[name] = np.ascontiguousarray(v)
        return nc.dram_tensor(name, v.shape, mybir.dt.from_np(v.dtype), kind="ExternalInput").ap()

    def scratch(name, *shape):
        return nc.dram_tensor(name, shape, f32, kind="Internal").ap()

    d = Names()
    d.x, d.xT = given("in_x", x), given("in_xT", x.T)
    d.idx = given("in_idx", np.concatenate([k.reshape(GROUPS, P, CG) for k in (src, dst)], axis=2))
    d.keys = given("in_keys", np.stack(by_chunk, axis=1))
    d.key_rows = given("in_key_rows", np.stack([chunked(k).reshape(P, -1) for k in (src, dst)], axis=1))
    d.now = given("in_now", dst.reshape(P, -1))
    d.then = given("in_then", rows_to(dst[1:], EP, PAD).reshape(P, -1))
    d.ends = given("in_ends", np.stack([dst[::GE], dst[GE - 1::GE]]))
    d.ft, d.fe = given("in_ft", tf), given("in_fe", np.concatenate([ef, et]))
    d.time0 = given("in_time0", a["edge_attr_64_n2"][0:1].T)
    d.w1 = given("in_w1", np.concatenate([w1[:, :D].T, w1[:, D:].T], axis=1))
    d.b1 = given("in_b1", a["L0_gnn_b1"])
    d.w2, d.w2t = given("in_w2", a["L0_gnn_W2"]), given("in_w2t", a["L0_gnn_W2"].T)
    d.cols = given("in_cols", np.stack([a[k] for k in ("L0_gnn_g1", "L0_gnn_be1", "L0_gnn_g2", "L0_gnn_be2",
                                                       "L0_gnn_b2", "L1_gnn_b1")], axis=1))
    d.wx = given("in_wx", np.concatenate([w[:D] for w in (wq, wk, wv)], axis=1))
    d.bx = given("in_bx", np.concatenate([a[k] for k in ("L1_gnn_bq", "L1_gnn_bk", "L1_gnn_bv")]))
    d.wt, d.we = given("in_wt", wq[D:]), given("in_we", np.concatenate([wk[D:], wv[D:]], axis=1))
    d.l1_w1, d.l1_w2 = given("in_l1_w1", a["L1_gnn_W1"]), given("in_l1_w2", a["L1_gnn_W2"])
    d.l1_b2 = given("in_l1_b2", a["L1_gnn_b2"])
    d.ta, d.tb, d.tn = scratch("ta", NP_, D), scratch("tb", NP_, TB_W), scratch("tn", NP_, TN_W)
    d.rowf = nc.dram_tensor("rowf", (2, 2, EP), u16, kind="Internal").ap()
    d.h1, d.up, d.x1 = scratch("h1", D, EP), scratch("up", EP + SLOTS, D), scratch("x1", NP_, D)
    d.msg_of = [scratch("msg_s", EP + SLOTS, MSG_W), scratch("msg_t", EP + SLOTS, MSG_W)]
    d.out = nc.dram_tensor("out", (NP_, D), f32, kind="ExternalOutput").ap()
    build(nc, d)
    r = run_bass_kernel_spmd(nc, [arrays], core_ids=[0])
    return r.results[0]["out"][:N]
```
